# Optimizing a Trainium2 kernel written in Bass

```python
import numpy as np
import jax
import jax.numpy as jnp

def _softmax(x, axis=-1):
    return jax.nn.softmax(x, axis=axis)

def _gelu(x):
    return jax.nn.gelu(x, approximate=True)

def _silu(x):
    return jax.nn.silu(x)

def _sigmoid(x):
    return jax.nn.sigmoid(x)

def _layernorm(x, axis=-1, eps=1e-05):
    m = jnp.mean(x, axis=axis, keepdims=True)
    v = jnp.var(x, axis=axis, keepdims=True)
    return (x - m) / jnp.sqrt(v + eps)

def _scatter_add(tgt, idx, src, axis=0):
    return tgt.at[idx].add(src)

def _segment_sum(src, seg, n):
    return jax.ops.segment_sum(src, seg, n)
kernel_name = 'mk_gnn_resnorm_d2_gnn_r32_6c0a6a'

def setup_inputs(seed: int=0):
    np.random.seed(seed)
    _w = jnp.asarray

    def _rec_inputs():
        import jax
        import jax.numpy as jnp
        _gk = jax.random.key(seed)
        x = -0.0003713 + 1 * jax.random.normal(jax.random.fold_in(_gk, 1), (3125, 128), jnp.float32)
        src = jax.random.randint(jax.random.fold_in(_gk, 2), (50000,), 0, 3125, jnp.int32)
        dst = jnp.minimum((3125 * jax.random.uniform(jax.random.fold_in(_gk, 3), (50000,)) ** 2.0).astype(jnp.int32), 99999)
        _o = jnp.argsort(dst, stable=True)
        src = src[_o]
        dst = dst[_o]
        edge_weight = jax.random.uniform(jax.random.fold_in(_gk, 12), (50000,), jnp.float32, 0.0, 0.999998)
        return (x, src, dst, edge_weight)
    x, src, dst, edge_weight = _rec_inputs()

    def _L0_gnn_setup():
        import jax, jax.numpy as jnp
        import numpy as np
        N_NODES = 3125
        N_EDGES = 18750
        H = 128
        NUM_STEPS = 5
        key = jax.random.key(seed)
        ks = jax.random.split(key, 8)
        s = 0.05
        return {'x': jax.random.normal(ks[0], (N_NODES, H), dtype=jnp.float32), 'edge_index': jax.random.randint(ks[1], (2, N_EDGES), 0, N_NODES, dtype=jnp.int64), 'W_msg': jax.random.normal(ks[2], (H, H), dtype=jnp.float32) * s, 'b_msg': jax.random.normal(ks[3], (H,), dtype=jnp.float32) * s, 'W_ih': jax.random.normal(ks[4], (3 * H, H), dtype=jnp.float32) * s, 'W_hh': jax.random.normal(ks[5], (3 * H, H), dtype=jnp.float32) * s, 'b_ih': jax.random.normal(ks[6], (3 * H,), dtype=jnp.float32) * s, 'b_hh': jax.random.normal(ks[7], (3 * H,), dtype=jnp.float32) * s}
    _L0_gnn_all = _L0_gnn_setup()
    _L0_gnn_in = {k: v for k, v in _L0_gnn_all.items() if k in ('W_msg', 'b_msg', 'W_ih', 'W_hh', 'b_ih', 'b_hh')}
    del _L0_gnn_all

    def _L1_gnn_setup():
        import jax, jax.numpy as jnp
        import numpy as np
        N = 50000
        E = 25000
        D = 128

        def _glorot(key, shape):
            fan_in = shape[0]
            return jax.random.normal(key, shape, dtype=jnp.float32) * (1.0 / np.sqrt(fan_in))

        def _gnn_layer(edge_index, x, edge_attr, norm, We, be, Wn, bn):
            src, dst = (edge_index[0], edge_index[1])
            parts = [x[src], x[dst]]
            if edge_attr is not None:
                parts.append(edge_attr)
            e = jax.nn.relu(jnp.concatenate(parts, axis=-1) @ We + be)
            msg = e * norm[:, None] if norm is not None else e
            agg = jax.ops.segment_sum(msg, dst, num_segments=x.shape[0])
            x_new = jax.nn.relu(jnp.concatenate([x, agg], axis=-1) @ Wn + bn)
            return (x_new, e)
        key = jax.random.key(seed)
        ks = jax.random.split(key, 16)
        inp = {'edge_index': jax.random.randint(ks[0], (2, E), 0, N, dtype=jnp.int64), 'z': jax.random.normal(ks[1], (N, D), dtype=jnp.float32), 'norm': jax.random.uniform(ks[2], (E,), dtype=jnp.float32), 'We0': _glorot(ks[3], (2 * D, D)), 'be0': jnp.zeros((D,), jnp.float32), 'Wn0': _glorot(ks[4], (2 * D, D)), 'bn0': jnp.zeros((D,), jnp.float32), 'We1': _glorot(ks[5], (3 * D, D)), 'be1': jnp.zeros((D,), jnp.float32), 'Wn1': _glorot(ks[6], (2 * D, D)), 'bn1': jnp.zeros((D,), jnp.float32), 'We2': _glorot(ks[7], (3 * D, D)), 'be2': jnp.zeros((D,), jnp.float32), 'Wn2': _glorot(ks[8], (2 * D, D)), 'bn2': jnp.zeros((D,), jnp.float32)}
        return inp
    _L1_gnn_all = _L1_gnn_setup()
    _L1_gnn_in = {k: v for k, v in _L1_gnn_all.items() if k in ('We0', 'be0', 'Wn0', 'bn0', 'We1', 'be1', 'Wn1', 'bn1', 'We2', 'be2', 'Wn2', 'bn2')}
    del _L1_gnn_all
    return {'x': x, 'src': src, 'dst': dst, 'edge_weight': edge_weight, 'L0_gnn_W_msg': _L0_gnn_in['W_msg'], 'L0_gnn_b_msg': _L0_gnn_in['b_msg'], 'L0_gnn_W_ih': _L0_gnn_in['W_ih'], 'L0_gnn_W_hh': _L0_gnn_in['W_hh'], 'L0_gnn_b_ih': _L0_gnn_in['b_ih'], 'L0_gnn_b_hh': _L0_gnn_in['b_hh'], 'L1_gnn_We0': _L1_gnn_in['We0'], 'L1_gnn_be0': _L1_gnn_in['be0'], 'L1_gnn_Wn0': _L1_gnn_in['Wn0'], 'L1_gnn_bn0': _L1_gnn_in['bn0'], 'L1_gnn_We1': _L1_gnn_in['We1'], 'L1_gnn_be1': _L1_gnn_in['be1'], 'L1_gnn_Wn1': _L1_gnn_in['Wn1'], 'L1_gnn_bn1': _L1_gnn_in['bn1'], 'L1_gnn_We2': _L1_gnn_in['We2'], 'L1_gnn_be2': _L1_gnn_in['be2'], 'L1_gnn_Wn2': _L1_gnn_in['Wn2'], 'L1_gnn_bn2': _L1_gnn_in['bn2']}

def reference(x, src, dst, edge_weight, L0_gnn_W_msg, L0_gnn_b_msg, L0_gnn_W_ih, L0_gnn_W_hh, L0_gnn_b_ih, L0_gnn_b_hh, L1_gnn_We0, L1_gnn_be0, L1_gnn_Wn0, L1_gnn_bn0, L1_gnn_We1, L1_gnn_be1, L1_gnn_Wn1, L1_gnn_bn1, L1_gnn_We2, L1_gnn_be2, L1_gnn_Wn2, L1_gnn_bn2):
    import jax
    import jax.numpy as jnp

    def _L0_gnn_ref(x, edge_index, W_msg, b_msg, W_ih, W_hh, b_ih, b_hh):
        import jax, jax.numpy as jnp
        import numpy as np
        N_NODES = 3125
        N_EDGES = 18750
        H = 128
        NUM_STEPS = 5
        num_nodes = x.shape[0]
        row, col = (edge_index[0], edge_index[1])

        def step(h, _):
            messages = h[col] @ W_msg.T + b_msg
            agg = jax.ops.segment_sum(messages, row, num_segments=num_nodes)
            gi = agg @ W_ih.T + b_ih
            gh = h @ W_hh.T + b_hh
            i_r, i_z, i_n = jnp.split(gi, 3, axis=-1)
            h_r, h_z, h_n = jnp.split(gh, 3, axis=-1)
            r = jax.nn.sigmoid(i_r + h_r)
            z = jax.nn.sigmoid(i_z + h_z)
            n = jnp.tanh(i_n + r * h_n)
            h_new = (1.0 - z) * n + z * h
            return (h_new, None)
        h, _ = jax.lax.scan(step, x, None, length=NUM_STEPS)
        return h

    def _L1_gnn_ref(edge_index, z, norm, We0, be0, Wn0, bn0, We1, be1, Wn1, bn1, We2, be2, Wn2, bn2):
        import jax, jax.numpy as jnp
        import numpy as np
        N = 50000
        E = 25000
        D = 128

        def _glorot(key, shape):
            fan_in = shape[0]
            return jax.random.normal(key, shape, dtype=jnp.float32) * (1.0 / np.sqrt(fan_in))

        def _gnn_layer(edge_index, x, edge_attr, norm, We, be, Wn, bn):
            src, dst = (edge_index[0], edge_index[1])
            parts = [x[src], x[dst]]
            if edge_attr is not None:
                parts.append(edge_attr)
            e = jax.nn.relu(jnp.concatenate(parts, axis=-1) @ We + be)
            msg = e * norm[:, None] if norm is not None else e
            agg = jax.ops.segment_sum(msg, dst, num_segments=x.shape[0])
            x_new = jax.nn.relu(jnp.concatenate([x, agg], axis=-1) @ Wn + bn)
            return (x_new, e)
        x, edge_attr = _gnn_layer(edge_index, z, None, norm, We0, be0, Wn0, bn0)
        x, edge_attr = _gnn_layer(edge_index, x, edge_attr, norm, We1, be1, Wn1, bn1)
        x, edge_attr = _gnn_layer(edge_index, x, edge_attr, norm, We2, be2, Wn2, bn2)
        return x
    edge_index = jnp.stack([src, dst])
    x = _layernorm(x + _L0_gnn_ref(x, edge_index, L0_gnn_W_msg, L0_gnn_b_msg, L0_gnn_W_ih, L0_gnn_W_hh, L0_gnn_b_ih, L0_gnn_b_hh), axis=-1)
    x = _layernorm(x + _L1_gnn_ref(edge_index, x, edge_weight, L1_gnn_We0, L1_gnn_be0, L1_gnn_Wn0, L1_gnn_bn0, L1_gnn_We1, L1_gnn_be1, L1_gnn_Wn1, L1_gnn_bn1, L1_gnn_We2, L1_gnn_be2, L1_gnn_Wn2, L1_gnn_bn2), axis=-1)
    return x

_drawn_inputs = setup_inputs


def setup_inputs(seed=0):
    import zlib

    import numpy as np

    out = dict(_drawn_inputs(seed))
    spreads = {'L1_gnn_be0': (0.0, 0.1),
     'L1_gnn_bn0': (0.0, 0.337),
     'L1_gnn_be1': (0.0, 0.1),
     'L1_gnn_bn1': (0.0, 0.419),
     'L1_gnn_be2': (0.0, 0.287),
     'L1_gnn_bn2': (0.0, 0.478)}
    factors = {}
    for name, (base, spread) in spreads.items():
        noise = np.random.default_rng([zlib.crc32(name.encode()), seed]).standard_normal(out[name].shape)
        drawn = base * np.exp(spread * noise) if base else spread * noise
        out[name] = jnp.asarray(drawn.astype(out[name].dtype))
    for name, factor in factors.items():
        out[name] = (out[name] * factor).astype(out[name].dtype)
    return out
```

```python
from contextlib import ExitStack

import concourse.bass as bass
from concourse import mybir

F32 = mybir.dt.float32
BF16 = mybir.dt.bfloat16
F16 = mybir.dt.float16
I32 = mybir.dt.int32
U32 = mybir.dt.uint32
ALU = mybir.AluOpType
ACT = mybir.ActivationFunctionType
AX_X = mybir.AxisListType.X

P = 128
NODES = 3125
EDGES = 50000
D = 128
GRU_STEPS = 5
EPS = 1e-5
WINDOWS = -(-NODES // P)
PADDED = WINDOWS * P
LAST = NODES - (WINDOWS - 1) * P
TILES = -(-EDGES // P)
EVAC_DVE = (1, 3, 5)
TCH = 4
GROUP = 4
SLOTS = 4
MAX_ROUNDS = -(-((TILES + WINDOWS - 1 + (GROUP - 1) * WINDOWS) // GROUP) // SLOTS)
GROUPS = MAX_ROUNDS * SLOTS
STEPS = GROUPS * GROUP
MIN_ROUNDS = TILES // (GROUP * SLOTS)
CHUNK = 512
CHUNKS = -(-NODES // CHUNK)
NO_NODE = 100000.0


class Marks:

    def __init__(self, sem, base=0):
        self.sem, self.base, self.n = sem, base, 0

    def on(self, ins):
        self.n += 1
        ins.then_inc(self.sem, 1)
        return self.base + self.n


def build(nc, x, xT, src, dst, edge_weight, W_msgT, b_msg, W_ihT, W_hhT, b_ih, b_hh,
          We0, be0, Wn0, bn0, We1, be1, Wn1, bn1, We2, be2, Wn2, bn2, out, debug=None):
    ctx = ExitStack()
    with ctx:
        psum = ctx.enter_context(nc.psum_tensor("psum", [P, 8, CHUNK], F32))

        def sb(name, shape, dt):
            return ctx.enter_context(nc.sbuf_tensor(name, shape, dt))

        keep = {
            "ident": sb("ident", [P, P], F32),
            "ones": sb("ones", [P, P], F32),
            "lane_f": sb("lane_f", [P, 1], F32),
            "col_f": sb("col_f", [P, P], F32),
            "pairs_i": sb("pairs_i", [1, WINDOWS, 4], I32),
            "win_i": sb("win_i", [1, GROUPS], I32),
            "rounds_i": sb("rounds_i", [1, 2], I32),
        }
        hT = sb("hT", [P, PADDED], F32)
        dst_rows = nc.dram_tensor("dst_rows", ((STEPS + GROUP) * P,), BF16, kind="Internal").ap()
        tables = nc.dram_tensor("tables", (3, P, STEPS), F32, kind="Internal").ap()
        deg_row = nc.dram_tensor("deg_row", (PADDED,), F32, kind="Internal").ap()
        x1_dram = nc.dram_tensor("x1_dram", (PADDED, D), F32, kind="Internal").ap()

        with ExitStack() as l0:
            adj = l0.enter_context(nc.sbuf_tensor("adj", [P, WINDOWS, NODES], BF16))
            with ExitStack() as tab:
                for name, dt in (("src_f", F32), ("dst_loc", F32), ("weight", F32)):
                    keep[name] = tab.enter_context(nc.sbuf_tensor(name, [P, STEPS], dt))
                step_tables(nc, src, dst, edge_weight, psum, keep, dst_rows, tables)
                if debug:
                    debug("tables", nc, keep)
                build_adjacency(nc, psum, keep, adj, deg_row)
                if debug:
                    debug("adj", nc, {"adj": adj})
            gated_steps(nc, xT, W_msgT, b_msg, W_ihT, W_hhT, b_ih, b_hh, psum, keep, hT, adj, deg_row)
            if debug:
                debug("h5", nc, {"hT": hT})
        add_and_norm(nc, "_0", x, x1_dram, psum, keep, hT, turn_back=True)
        if debug:
            debug("x1", nc, {"hT": hT})
        edge_layers(nc, ((We0, be0, Wn0, bn0), (We1, be1, Wn1, bn1), (We2, be2, Wn2, bn2)),
                    psum, keep, hT, dst_rows, tables, debug)
        add_and_norm(nc, "_1", x1_dram[0:NODES, :], out, psum, keep, hT, turn_back=False)


def clear_semaphores(nc):
    used = sorted(int(n) for n in nc.released_uncleared_semaphores)
    with nc.Block() as block:
        @block.sync
        def _(sp):
            start = 0
            for i in range(1, len(used) + 1):
                if i == len(used) or used[i] != used[i - 1] + 1:
                    sp.sem_clear(range(used[start], used[i - 1] + 1))
                    start = i


def step_tables(nc, src, dst, edge_weight, psum, keep, dst_rows, tables):
    with ExitStack() as ctx:
        def sb(name, shape, dt):
            return ctx.enter_context(nc.sbuf_tensor(name, shape, dt))

        def sem(name):
            return ctx.enter_context(nc.semaphore(name))

        W = WINDOWS
        whole = EDGES // P
        rest = EDGES - whole * P
        q_full = whole // P
        q_rows = whole - q_full * P
        raw = {n: sb(f"raw_{n}", [P, TCH, P], dt) for n, dt in
               (("dst", I32), ("src", I32), ("weight", F32))}
        rows = {"dst": sb("rows_dst", [P, TCH, P], F32), "src": sb("rows_src", [P, TCH, P], F32),
                "weight": raw["weight"]}
        below = sb("below", [P, TCH * P], F32)
        counts = sb("counts", [P, W + 1], F32)
        step_i = sb("step_i", [P, STEPS], I32)
        step_f = sb("step_f", [P, STEPS], F32)
        lane_i = sb("lane_i", [P, 1], I32)
        col_i = sb("col_i", [P, P], I32)
        tri = sb("tri", [P, P], F32)
        edge_i = sb("edge_i", [W, 2], I32)
        edge_f = sb("edge_f", [W, 2], F32)
        size_f = sb("size_f", [W, 1], F32)
        size_i = sb("size_i", [W, 2], I32)
        size_g = sb("size_g", [W, 2], F32)
        bounds = sb("bounds", [W, 6], F32)
        flags = sb("flags", [W, 2, STEPS], F32)
        names = sb("names", [W, 2, P], F32)
        totals_i = sb("totals_i", [1, 2], I32)
        tile_of = sb("tile_of", [P, STEPS], F32)
        lane_q = sb("lane_q", [P, TCH], F32)
        pick = sb("pick", [P, TCH, STEPS], F32)
        dst_t = sb("dst_t", [P, TCH, P], BF16)

        edges_in = {n: sem(f"{n}_in") for n in raw}
        padded = sem("padded")
        iotas = sem("iotas")
        vec = sem("vec")
        small = sem("small")
        picked = sem("picked")
        turned = sem("turned")
        dst_out = sem("dst_out")
        done = {}

        block = ctx.enter_context(nc.Block())

        @block.gpsimd
        def _(pool):
            nc.gpsimd.memset(raw["dst"][:, TCH - 1, :], int(NO_NODE)).then_inc(padded, 1)
            nc.gpsimd.memset(raw["src"][:, TCH - 1, :], 0).then_inc(padded, 1)
            nc.gpsimd.memset(raw["weight"][:, TCH - 1, :], 0.0).then_inc(padded, 1)
            nc.gpsimd.iota(step_i[:], [[1, STEPS]], 0, 0).then_inc(iotas, 1)
            nc.gpsimd.iota(lane_i[:], [[0, 1]], 0, 1).then_inc(iotas, 1)
            nc.gpsimd.iota(col_i[:], [[1, P]], 0, 0).then_inc(iotas, 1)
            nc.gpsimd.memset(keep["ones"][:], 1.0).then_inc(iotas, 1)

        @block.vector
        def _(dve):
            v = Marks(vec)

            def after(ins):
                dve.wait_ge(vec, v.on(ins))

            dve.wait_ge(iotas, 4)
            v.on(nc.vector.memset(dst_t[:, TCH - 1, :], 0.0))
            v.on(nc.vector.tensor_copy(step_f[:], step_i[:]))
            v.on(nc.vector.tensor_copy(keep["lane_f"][:], lane_i[:]))
            v.on(nc.vector.memset(counts[:, 0:1], 0.0))
            after(nc.vector.tensor_copy(keep["col_f"][:], col_i[:]))
            v.on(nc.vector.tensor_scalar(keep["ident"][:], keep["col_f"][:], keep["lane_f"][:, 0:1],
                                         None, ALU.is_equal))
            v.on(nc.vector.tensor_scalar(tri[:], keep["col_f"][:], keep["lane_f"][:, 0:1],
                                         None, ALU.is_gt))
            v.on(nc.vector.tensor_scalar(names[:, 0, :], keep["ones"][0:W, :], keep["lane_f"][0:W, 0:1],
                                         None, ALU.mult))
            for q in range(TCH):
                v.on(nc.vector.tensor_scalar(lane_q[:, q:q + 1], keep["lane_f"][:], float(q * P), None,
                                             ALU.add))
            dve.wait_ge(edges_in["dst"], 48)
            after(nc.vector.tensor_copy(rows["dst"][:], raw["dst"][:]))
            flat = rows["dst"][:].rearrange("p q c -> p (q c)")
            for w in range(1, W + 1):
                after(nc.vector.tensor_scalar(below[:], flat, float(w * P), 0.0, ALU.is_lt,
                                              ALU.add, accum_out=counts[:, w:w + 1]))
            done["counts"] = v.n
            dve.wait_ge(edges_in["src"], 48)
            v.on(nc.vector.tensor_copy(rows["src"][:], raw["src"][:]))
            dve.wait_ge(small, 1)
            after(nc.vector.tensor_copy(edge_i[:], psum[0:W, 0, 0:2]))
            after(nc.vector.tensor_scalar(edge_i[:], edge_i[:], P.bit_length() - 1, None,
                                          ALU.logical_shift_right))
            after(nc.vector.tensor_copy(edge_f[:], edge_i[:]))
            after(nc.vector.tensor_tensor(size_f[:], edge_f[:, 1:2], edge_f[:, 0:1], ALU.subtract))
            v.on(nc.vector.tensor_scalar(size_i[:, 0:1], size_f[:], float(GROUP), None, ALU.add))
            after(nc.vector.tensor_scalar(size_i[:, 1:2], size_f[:], 2.0, 4.0, ALU.add, ALU.max))
            v.on(nc.vector.tensor_scalar(size_i[:, 0:1], size_i[:, 0:1], GROUP.bit_length() - 1, None,
                                         ALU.logical_shift_right))
            after(nc.vector.tensor_scalar(size_i[:, 1:2], size_i[:, 1:2], 1, None,
                                          ALU.logical_shift_right))
            after(nc.vector.tensor_copy(size_g[:], size_i[:]))
            done["sizes"] = v.n
            dve.wait_ge(small, 2)
            after(nc.vector.tensor_scalar(bounds[:, 0:1], psum[0:W, 1, 0:1], float(GROUP), None, ALU.mult))
            v.on(nc.vector.scalar_tensor_tensor(out=bounds[:, 1:2], in0=size_g[:, 0:1],
                                                scalar=float(GROUP), in1=bounds[:, 0:1],
                                                op0=ALU.mult, op1=ALU.add))
            v.on(nc.vector.tensor_copy(bounds[:, 3:4], psum[0:W, 1, 1:2]))
            v.on(nc.vector.tensor_tensor(bounds[:, 4:5], psum[0:W, 1, 1:2], size_g[:, 1:2], ALU.add))
            after(nc.vector.tensor_scalar(bounds[:, 5:6], psum[0:W, 1, 0:1], 2.0, None, ALU.mult))
            v.on(nc.vector.tensor_tensor(bounds[:, 5:6], bounds[:, 5:6], bounds[:, 3:4], ALU.subtract))
            after(nc.vector.tensor_tensor(bounds[:, 2:3], bounds[:, 0:1], edge_f[:, 0:1], ALU.subtract))
            v.on(nc.vector.tensor_scalar(names[:, 1, :], keep["ones"][0:W, :], bounds[:, 2:3],
                                         None, ALU.mult))
            v.on(nc.vector.tensor_scalar(flags[:, 0, :], step_f[0:W, :], bounds[:, 0:1], None, ALU.is_ge))
            after(nc.vector.tensor_scalar(flags[:, 1, :], step_f[0:W, :], bounds[:, 1:2], None,
                                          ALU.is_lt))
            after(nc.vector.tensor_tensor(flags[:, 1, :], flags[:, 1, :], flags[:, 0, :], ALU.mult))
            done["flags"] = v.n
            dve.wait_ge(small, 3)
            v.on(nc.vector.memset(keep["pairs_i"][:, :, 3], 0))
            for i in range(3):
                v.on(nc.vector.tensor_copy(keep["pairs_i"][:, :, i], psum[0:1, 2, i * W:(i + 1) * W]))
            after(nc.vector.tensor_scalar(totals_i[:, 0:1], psum[0:1, 2, 3 * W:3 * W + 1],
                                          float(SLOTS - 1), None, ALU.add))
            v.on(nc.vector.tensor_scalar(totals_i[:, 1:2], psum[0:1, 2, 3 * W:3 * W + 1], -1.0, None,
                                         ALU.add))
            v.on(nc.vector.tensor_scalar(keep["rounds_i"][:, 0:1], totals_i[:, 0:1],
                                         SLOTS.bit_length() - 1, None, ALU.logical_shift_right))
            dve.wait_ge(vec, v.n)
            v.on(nc.vector.tensor_scalar(keep["rounds_i"][:, 1:2], totals_i[:, 1:2],
                                         SLOTS.bit_length() - 1, None, ALU.logical_shift_right))
            dve.wait_ge(small, 4)
            v.on(nc.vector.tensor_copy(keep["win_i"][:], psum[0:1, 3, 0:STEPS:GROUP]))
            after(nc.vector.scalar_tensor_tensor(out=tile_of[:], in0=psum[:, 4, 0:STEPS], scalar=-1.0,
                                                 in1=step_f[:], op0=ALU.mult, op1=ALU.add))
            for q in range(TCH):
                v.on(nc.vector.tensor_scalar(pick[:, q, :], tile_of[:], lane_q[:, q:q + 1], None,
                                             ALU.is_equal))
            done["pick"] = v.n
            dve.wait_ge(vec, v.n)
            after(nc.vector.tensor_copy(tile_of[:], psum[:, 3, 0:STEPS]))
            dve.wait_ge(picked, 1)
            v.on(nc.vector.tensor_copy(keep["src_f"][:], psum[:, 5, 0:STEPS]))
            dve.wait_ge(picked, 2)
            after(nc.vector.scalar_tensor_tensor(
                out=keep["dst_loc"][:], in0=tile_of[:], scalar=-float(P), in1=psum[:, 6, 0:STEPS],
                op0=ALU.mult, op1=ALU.add))
            done["dst_loc"] = v.n
            dve.wait_ge(picked, 3)
            v.on(nc.vector.tensor_copy(keep["weight"][:], psum[:, 7, 0:STEPS]))
            for q in range(TCH):
                n_q = min(P, STEPS - q * P)
                dve.wait_ge(turned, q + 1)
                v.on(nc.vector.tensor_copy(dst_t[0:n_q, q, :], psum[0:n_q, q, 0:P]))
            done["dst_t"] = v.n

        @block.tensor
        def _(pe):
            ones = keep["ones"]
            pe.wait_ge(vec, done["counts"])
            pe.wait_ge(iotas, 4)
            nc.tensor.matmul(psum[0:W, 0, 0:1], counts[:, 0:W], ones[:, 0:1], start=True, stop=True)
            nc.tensor.matmul(psum[0:W, 0, 1:2], counts[:, 1:W + 1], ones[:, 0:1],
                             start=True, stop=True).then_inc(small, 1)
            pe.wait_ge(vec, done["sizes"])
            nc.tensor.matmul(psum[0:W, 1, 0:2], tri[0:W, 0:W], size_g[:],
                             start=True, stop=True).then_inc(small, 1)
            pe.wait_ge(vec, done["flags"])
            for i in range(3):
                nc.tensor.matmul(psum[0:1, 2, i * W:(i + 1) * W], bounds[:, 3 + i:4 + i],
                                 keep["ident"][0:W, 0:W], start=True, stop=True)
            nc.tensor.matmul(psum[0:1, 2, 3 * W:3 * W + 1], size_g[:, 0:1], ones[0:W, 0:1],
                             start=True, stop=True).then_inc(small, 1)
            for b in range(2):
                mm = nc.tensor.matmul(psum[:, 3 + b, 0:STEPS], names[:, b, :], flags[:, 1, :],
                                      start=True, stop=True)
            mm.then_inc(small, 1)
            pe.wait_ge(vec, done["pick"])
            pe.wait_ge(edges_in["weight"], 48)
            for b, name in ((5, "src"), (6, "dst"), (7, "weight")):
                for q in range(TCH):
                    mm = nc.tensor.matmul(psum[:, b, 0:STEPS], rows[name][:, q, :], pick[:, q, :],
                                          start=(q == 0), stop=(q == TCH - 1))
                mm.then_inc(picked, 1)
            pe.wait_ge(vec, done["dst_loc"])
            for q in range(TCH):
                n = min(P, STEPS - q * P)
                nc.tensor.transpose(psum[0:n, q, 0:P], keep["dst_loc"][:, q * P:q * P + n],
                                    keep["ident"][:]).then_inc(turned, 1)

        @block.sync
        def _(sp):
            sp.wait_ge(padded, 3)
            for n, dram in (("dst", dst), ("src", src), ("weight", edge_weight)):
                full = dram[0:q_full * P * P].rearrange("(q r p) -> r q p", p=P, r=P)
                sp.dma_start(raw[n][:, 0:q_full, :], full).then_inc(edges_in[n], 16)
                part = dram[q_full * P * P:whole * P].rearrange("(r p) -> r p", p=P)
                sp.dma_start(raw[n][0:q_rows, q_full, :], part).then_inc(edges_in[n], 16)
                tail = dram[whole * P:EDGES].rearrange("(r p) -> r p", r=1)
                sp.dma_start(raw[n][q_rows:q_rows + 1, q_full, 0:rest], tail).then_inc(edges_in[n], 16)
            sp.wait_ge(vec, done["dst_t"])
            for q in range(TCH):
                n = min(P, STEPS + GROUP - q * P)
                sp.dma_start(dst_rows[q * P * P:(q * P + n) * P].rearrange("(r p) -> r p", p=P),
                             dst_t[0:n, q, :]).then_inc(dst_out, 16)
            for i, name in enumerate(("src_f", "dst_loc", "weight")):
                sp.dma_start(tables[i], keep[name][:]).then_inc(dst_out, 16)
            sp.wait_ge(dst_out, 16 * (TCH + 3))


def build_adjacency(nc, psum, keep, adj, deg_row):
    with ExitStack() as ctx:
        def sb(name, shape, dt):
            return ctx.enter_context(nc.sbuf_tensor(name, shape, dt))

        def sem(name):
            return ctx.enter_context(nc.semaphore(name))

        node_h = sb("node_h", [P, NODES], F16)
        col_h = sb("col_h", [P, P], F16)
        src_c = sb("src_c", [P, STEPS], F32)
        src_hot = sb("src_hot", [P, 2, NODES], BF16)
        dst_hot = sb("dst_hot", [P, 2, P], BF16)
        one_col = sb("one_col", [P, 1], BF16)
        deg_sb = sb("deg_sb", [1, NODES], F32)
        CENTER = NODES // 2
        HALF = CHUNKS // 2 * CHUNK

        iotas = sem("iotas_a")
        consts = sem("consts_a")
        hot = sem("hot")
        half_used = sem("half_used")
        used = sem("used")
        act_out = sem("act_out")
        dve_out = sem("dve_out")
        degs = sem("degs")
        deg_done = sem("deg_done")
        deg_out = sem("deg_out")

        def width(c):
            return min(CHUNK, NODES - c * CHUNK)

        act_banks = [c for c in range(CHUNKS) if c not in EVAC_DVE]
        block = ctx.enter_context(nc.Block())

        @block.gpsimd
        def _(pool):
            nc.gpsimd.iota(node_h[:], [[1, NODES]], -CENTER, 0,
                           allow_small_or_imprecise_dtypes=True).then_inc(iotas, 1)
            nc.gpsimd.iota(col_h[:], [[1, P]], 0, 0,
                           allow_small_or_imprecise_dtypes=True).then_inc(iotas, 1)
            nc.gpsimd.memset(one_col[:], 1.0).then_inc(iotas, 1)

        def window_pairs(w, engine):
            _, (first, end, shift, _) = nc.values_load_multi_w_load_instructions(
                keep["pairs_i"][0:1, w if isinstance(w, int) else bass.ds(w, 1), :],
                engines=(engine,), min_val=0, max_val=STEPS)
            return first, end, shift

        @block.vector
        def _(dve):
            nc.vector.tensor_scalar(src_c[:], keep["src_f"][:], -float(CENTER), None,
                                    ALU.add).then_inc(consts, 1)
            dve.sem_inc(half_used, 2)
            dve.sem_inc(used, 2)
            dve.wait_ge(iotas, 3)
            dve.wait_ge(consts, 1)

            def one_hots(pair, shift):
                step = nc.s_assert_within(
                    (pair + shift) * 2, 0, STEPS - 2,
                    skip_runtime_bounds_check_because="the tables have room for all windows' pairs")
                for j in range(2):
                    k = bass.ds(step + j, 1)
                    dve.wait_ge(half_used, pair * 2 + j + 1)
                    nc.vector.tensor_scalar(src_hot[:, j, 0:HALF], node_h[:, 0:HALF], src_c[:, k],
                                            None, ALU.is_equal).then_inc(hot, 1)
                    dve.wait_ge(used, pair * 2 + j + 1)
                    nc.vector.tensor_scalar(dst_hot[:, j, :], col_h[:], keep["dst_loc"][:, k], None,
                                            ALU.is_equal).then_inc(hot, 1)
                    nc.vector.tensor_scalar(src_hot[:, j, HALF:NODES], node_h[:, HALF:NODES],
                                            src_c[:, k], None, ALU.is_equal).then_inc(hot, 1)

            def rest_of(first, end, shift):
                with dve.Fori(first + 1, end) as pair:
                    one_hots(pair, shift)

            def take(w, end):
                dve.wait_ge(used, end * 2 + 2)
                for c in EVAC_DVE:
                    nc.vector.tensor_copy(adj[:, w, c * CHUNK:c * CHUNK + width(c)],
                                          psum[:, c, 0:width(c)]).then_inc(dve_out, 1)

            first, _, shift = window_pairs(0, mybir.EngineType.DVE)
            one_hots(first, shift)
            with dve.Fori(0, WINDOWS - 1) as w:
                first, end, shift = window_pairs(w, mybir.EngineType.DVE)
                rest_of(first, end, shift)
                first, _, shift = window_pairs(w + 1, mybir.EngineType.DVE)
                one_hots(first, shift)
                take(bass.ds(w, 1), end)
            first, end, shift = window_pairs(WINDOWS - 1, mybir.EngineType.DVE)
            rest_of(first, end, shift)
            take(WINDOWS - 1, end)

        @block.scalar
        def _(act):
            nc.scalar.preload_act_table(ACT.Copy)
            with act.Fori(0, WINDOWS) as w:
                _, end, _ = window_pairs(w, mybir.EngineType.Activation)
                act.wait_ge(used, end * 2 + 2)
                for c in act_banks:
                    nc.scalar.copy(adj[:, bass.ds(w, 1), c * CHUNK:c * CHUNK + width(c)],
                                   psum[:, c, 0:width(c)]).then_inc(act_out, 1)
            act.wait_ge(degs, 1)
            for c in range(CHUNKS):
                nc.scalar.copy(deg_sb[0:1, c * CHUNK:c * CHUNK + width(c)],
                               psum[0:1, c, 0:width(c)]).then_inc(deg_done, 1)

        @block.sync
        def _(sp):
            sp.wait_ge(deg_done, CHUNKS)
            sp.dma_start(deg_row[0:NODES].rearrange("(a n) -> a n", a=1), deg_sb[:]).then_inc(deg_out, 16)
            sp.wait_ge(deg_out, 16)

        @block.tensor
        def _(pe):
            pe.sem_inc(act_out, len(act_banks))
            pe.sem_inc(dve_out, len(EVAC_DVE))
            pe.wait_ge(iotas, 3)

            def multiply(pair, w=None):
                for j in range(2):
                    pe.wait_ge(hot, pair * 6 + 3 * j + 2)
                    for c in range(CHUNKS):
                        if c * CHUNK == HALF:
                            pe.wait_ge(hot, pair * 6 + 3 * j + 3)
                        start = w is not None and j == 0
                        if start and c in EVAC_DVE:
                            pe.wait_ge(dve_out, w * len(EVAC_DVE) + EVAC_DVE.index(c) + 1)
                        elif start:
                            pe.wait_ge(act_out, w * len(act_banks) + act_banks.index(c) + 1)
                        mm = nc.tensor.matmul(psum[:, c, 0:width(c)], dst_hot[:, j, :],
                                              src_hot[:, j, c * CHUNK:c * CHUNK + width(c)],
                                              start=start, stop=False, skip_group_check=True)
                        if (c + 1) * CHUNK == HALF:
                            mm.then_inc(half_used, 1)
                    mm.then_inc(used, 1)

            with pe.Fori(0, WINDOWS) as w:
                first, end, _ = window_pairs(w, mybir.EngineType.PE)
                multiply(first, w)
                with pe.Fori(first + 1, end) as pair:
                    multiply(pair)
            pe.wait_ge(act_out, (WINDOWS + 1) * len(act_banks))
            pe.wait_ge(dve_out, (WINDOWS + 1) * len(EVAC_DVE))
            for c in range(CHUNKS):
                nc.tensor.matmul(psum[0:1, c, 0:width(c)], one_col[:],
                                 adj[:, 0, c * CHUNK:c * CHUNK + width(c)],
                                 start=True, stop=False, skip_group_check=True)
            with pe.Fori(1, WINDOWS) as w:
                for c in range(CHUNKS):
                    mm = nc.tensor.matmul(psum[0:1, c, 0:width(c)], one_col[:],
                                          adj[:, bass.ds(w, 1), c * CHUNK:c * CHUNK + width(c)],
                                          start=False, stop=False, skip_group_check=True)
                mm.then_inc(used, 1)
            pe.drain().then_inc(degs, 1)


def chunk_width(c):
    return min(CHUNK, NODES - c * CHUNK)


def group_tiles(g):
    return range(4 * g, min(4 * g + 4, WINDOWS))


def gated_steps(nc, xT, W_msgT, b_msg, W_ihT, W_hhT, b_ih, b_hh, psum, keep, hT, adj, deg_row):
    with ExitStack() as ctx:
        def sb(name, shape, dt):
            return ctx.enter_context(nc.sbuf_tensor(name, shape, dt))

        def sem(name):
            return ctx.enter_context(nc.semaphore(name))

        parts = sb("parts", [P, WINDOWS, 3, P], BF16)
        residue = sb("residue", [P, CHUNK], F32)
        agg = sb("agg", [P, CHUNK], F32)
        msg = sb("msg", [P, CHUNK], F32)
        r = sb("r", [P, CHUNK], F32)
        z = sb("z", [P, CHUNK], F32)
        n = sb("n", [P, CHUNK], F32)
        deg = sb("deg", [1, CHUNK], F32)
        w_msg = sb("w_msg", [P, D], F32)
        w_ih = sb("w_ih", [P, 3 * D], F32)
        w_hh = sb("w_hh", [P, 3 * D], F32)
        b_row = sb("b_row", [1, D], F32)
        b_i = sb("b_i", [P, 3], F32)
        b_h = sb("b_h", [P, 3], F32)
        b_rz = sb("b_rz", [P, 2], F32)
        ident = keep["ident"]

        loads = sem("l0_loads")
        deg_in = sem("deg_in")
        setup = sem("l0_setup")
        turned = sem("h_turned")
        high = sem("high")
        resid = sem("resid")
        mid = sem("mid")
        low = sem("low")
        summed = sem("summed")
        agg_out = sem("agg_out")
        mixed = sem("mixed")
        msg_out = sem("msg_out")
        gates = sem("gates")
        r_on = sem("r_on")
        z_on = sem("z_on")
        n_pre = sem("n_pre")
        n_on = sem("n_on")
        h_new = sem("h_new")
        inner = sem("l0_inner")

        T_BANKS, MSG_BANK, AGG_BANK = (0, 1), 2, 3
        R_BANK, Z_BANK, IN_BANK, HN_BANK = 4, 5, 6, 7
        N_LOADS = 8

        block = ctx.enter_context(nc.Block())

        @block.sync
        def _(sp):
            sp.dma_start(hT[:, 0:NODES], xT).then_inc(loads, 16)
            sp.dma_start(w_msg[:], W_msgT).then_inc(loads, 16)
            sp.dma_start(w_ih[:], W_ihT).then_inc(loads, 16)
            sp.dma_start(w_hh[:], W_hhT).then_inc(loads, 16)
            sp.dma_start(b_row[:], b_msg.rearrange("(a n) -> a n", a=1)).then_inc(loads, 16)
            for b_sb, b_dram in ((b_i, b_ih), (b_h, b_hh)):
                with nc.allow_non_contiguous_dma(reason="384 biases, one a partition"):
                    sp.dma_start(b_sb[:], b_dram.rearrange("(g p) -> p g", p=P)).then_inc(loads, 16)
            sp.dma_start(deg[0:1, 0:1], deg_row[0:1].rearrange("(a n) -> a n", a=1)).then_inc(loads, 16)
            sp.wait_ge(loads, 16 * N_LOADS)
            with sp.Fori(0, GRU_STEPS) as s:
                for c in range(CHUNKS):
                    if c:
                        sp.wait_ge(mixed, s * CHUNKS + c)
                    else:
                        sp.wait_ge(h_new, s * CHUNKS + CHUNKS)
                    sp.dma_start(deg[0:1, 0:chunk_width(c)],
                                 deg_row[c * CHUNK:c * CHUNK + chunk_width(c)]
                                 .rearrange("(a n) -> a n", a=1)).then_inc(deg_in, 16)

        @block.tensor
        def _(pe):
            pe.wait_ge(loads, 16 * N_LOADS)

            def turn(s, g):
                pe.wait_ge(h_new, s * CHUNKS + g + 1)
                if g >= 2:
                    pe.wait_ge(resid, s * CHUNKS + g - 1)
                for i, t in enumerate(group_tiles(g)):
                    mm = nc.tensor.transpose(psum[:, T_BANKS[g % 2], i * P:(i + 1) * P],
                                             hT[:, t * P:(t + 1) * P], ident[:])
                mm.then_inc(turned, 1)

            def sum_over(cols, n_cols, windows):
                for w in windows:
                    for part in range(3):
                        mm = nc.tensor.matmul(psum[:, AGG_BANK, 0:n_cols], parts[:, w, part, :],
                                              adj[:, w, cols], start=(w == 0 and part == 0),
                                              stop=(w == WINDOWS - 1 and part == 2))
                return mm

            def gate_products(at, cols, n_cols):
                pe.wait_ge(agg_out, at)
                pe.wait_ge(deg_in, at * 16)
                nc.tensor.matmul(psum[:, MSG_BANK, 0:n_cols], w_msg[:], agg[:, 0:n_cols],
                                 start=True, stop=False)
                nc.tensor.matmul(psum[:, MSG_BANK, 0:n_cols], b_row[:], deg[:, 0:n_cols],
                                 start=False, stop=True).then_inc(mixed, 1)
                h_c = hT[:, cols]
                pe.wait_ge(h_new, at + CHUNKS - 1)
                for bank, g, alone in ((R_BANK, 0, False), (Z_BANK, 1, False), (HN_BANK, 2, True)):
                    nc.tensor.matmul(psum[:, bank, 0:n_cols], w_hh[:, g * D:(g + 1) * D], h_c,
                                     start=True, stop=alone)
                pe.wait_ge(msg_out, at)
                for bank, g, alone in ((R_BANK, 0, False), (Z_BANK, 1, False), (IN_BANK, 2, True)):
                    mm = nc.tensor.matmul(psum[:, bank, 0:n_cols], w_ih[:, g * D:(g + 1) * D],
                                          msg[:, 0:n_cols], start=alone, stop=True)
                mm.then_inc(gates, 1)

            with pe.Fori(0, GRU_STEPS) as s:
                turn(s, 0)
                for g in range(CHUNKS):
                    if g + 1 < CHUNKS:
                        turn(s, g + 1)
                    pe.wait_ge(low, s * CHUNKS + g + 1)
                    mm = sum_over(slice(0, CHUNK), CHUNK, group_tiles(g))
                mm.then_inc(summed, 1)
                with pe.Fori(1, CHUNKS - 1) as c:
                    pe.wait_ge(agg_out, s * CHUNKS + c)
                    sum_over(bass.ds(c * CHUNK, CHUNK), CHUNK, range(WINDOWS)).then_inc(summed, 1)
                    gate_products(s * CHUNKS + c, bass.ds((c - 1) * CHUNK, CHUNK), CHUNK)
                c = CHUNKS - 1
                pe.wait_ge(agg_out, s * CHUNKS + c)
                sum_over(slice(c * CHUNK, NODES), chunk_width(c), range(WINDOWS)).then_inc(summed, 1)
                gate_products(s * CHUNKS + c, slice((c - 1) * CHUNK, c * CHUNK), CHUNK)
                gate_products(s * CHUNKS + c + 1, slice(c * CHUNK, NODES), chunk_width(c))

        @block.scalar
        def _(act):
            act.wait_ge(setup, 1)

            def split(s, g):
                k = len(group_tiles(g))
                bank = psum[:, T_BANKS[g % 2], 0:k * P].rearrange("p (t d) -> p t d", d=P)
                act.wait_ge(turned, s * CHUNKS + g + 1)
                nc.scalar.activation(parts[:, 4 * g:4 * g + k, 0, :], bank, ACT.Copy).then_inc(high, 1)
                act.wait_ge(resid, s * CHUNKS + g + 1)
                nc.scalar.activation(parts[:, 4 * g:4 * g + k, 1, :],
                                     residue[:, 0:k * P].rearrange("p (t d) -> p t d", d=P),
                                     ACT.Copy).then_inc(mid, 1)

            def take_sum(at, n_cols, first=False):
                act.wait_ge(summed, at)
                if not first:
                    act.wait_ge(mixed, at - 1)
                nc.scalar.activation(agg[:, 0:n_cols], psum[:, AGG_BANK, 0:n_cols],
                                     ACT.Copy).then_inc(agg_out, 1)

            def take_msg(at, n_cols):
                act.wait_ge(mixed, at)
                nc.scalar.activation(msg[:, 0:n_cols], psum[:, MSG_BANK, 0:n_cols],
                                     ACT.Copy).then_inc(msg_out, 1)

            def gate(at, n_cols):
                act.wait_ge(gates, at)
                act.wait_ge(h_new, at + CHUNKS - 1)
                nc.scalar.activation(r[:, 0:n_cols], psum[:, R_BANK, 0:n_cols], ACT.Sigmoid,
                                     bias=b_rz[:, 0:1]).then_inc(r_on, 1)
                nc.scalar.activation(z[:, 0:n_cols], psum[:, Z_BANK, 0:n_cols], ACT.Sigmoid,
                                     bias=b_rz[:, 1:2]).then_inc(z_on, 1)
                act.wait_ge(n_pre, at)
                nc.scalar.activation(n[:, 0:n_cols], n[:, 0:n_cols], ACT.Tanh,
                                     bias=b_i[:, 2:3]).then_inc(n_on, 1)

            with act.Fori(0, GRU_STEPS) as s:
                for g in range(CHUNKS):
                    split(s, g)
                take_sum(s * CHUNKS + 1, CHUNK, first=True)
                with act.Fori(1, CHUNKS - 1) as c:
                    take_msg(s * CHUNKS + c, CHUNK)
                    take_sum(s * CHUNKS + c + 1, CHUNK)
                    gate(s * CHUNKS + c, CHUNK)
                c = CHUNKS - 1
                take_msg(s * CHUNKS + c, CHUNK)
                take_sum(s * CHUNKS + c + 1, chunk_width(c))
                gate(s * CHUNKS + c, CHUNK)
                take_msg(s * CHUNKS + c + 1, chunk_width(c))
                gate(s * CHUNKS + c + 1, chunk_width(c))

        @block.vector
        def _(dve):
            dve.wait_ge(loads, 16 * N_LOADS)
            nc.vector.tensor_tensor(b_rz[:], b_i[:, 0:2], b_h[:, 0:2], ALU.add).then_inc(setup, 1)
            nc.vector.memset(hT[:, NODES:PADDED], 0.0).then_inc(inner, 1)
            dve.wait_ge(inner, 1)
            dve.sem_inc(h_new, CHUNKS)

            def split(s, g):
                k = len(group_tiles(g))
                bank = psum[:, T_BANKS[g % 2], 0:k * P].rearrange("p (t d) -> p t d", d=P)
                rest = residue[:, 0:k * P].rearrange("p (t d) -> p t d", d=P)
                dve.wait_ge(high, s * CHUNKS + g + 1)
                if g:
                    dve.wait_ge(low, s * CHUNKS + g)
                nc.vector.tensor_tensor(rest, bank, parts[:, 4 * g:4 * g + k, 0, :],
                                        ALU.subtract).then_inc(resid, 1)
                dve.wait_ge(mid, s * CHUNKS + g + 1)
                nc.vector.tensor_tensor(parts[:, 4 * g:4 * g + k, 2, :], rest,
                                        parts[:, 4 * g:4 * g + k, 1, :], ALU.subtract).then_inc(low, 1)

            def gate(at, cols, n_cols):
                h_c = hT[:, cols]
                first = at * 3 - 2
                dve.wait_ge(r_on, at)
                nc.vector.scalar_tensor_tensor(
                    out=n[:, 0:n_cols], in0=psum[:, HN_BANK, 0:n_cols], scalar=b_h[:, 2:3],
                    in1=r[:, 0:n_cols], op0=ALU.add, op1=ALU.mult).then_inc(inner, 1)
                dve.wait_ge(inner, first + 1)
                nc.vector.tensor_tensor(n[:, 0:n_cols], psum[:, IN_BANK, 0:n_cols], n[:, 0:n_cols],
                                        ALU.add).then_inc(n_pre, 1)
                dve.wait_ge(n_on, at)
                nc.vector.tensor_tensor(r[:, 0:n_cols], h_c, n[:, 0:n_cols],
                                        ALU.subtract).then_inc(inner, 1)
                dve.wait_ge(inner, first + 2)
                dve.wait_ge(z_on, at)
                nc.vector.tensor_tensor(r[:, 0:n_cols], r[:, 0:n_cols], z[:, 0:n_cols],
                                        ALU.mult).then_inc(inner, 1)
                dve.wait_ge(inner, first + 3)
                nc.vector.tensor_tensor(h_c, r[:, 0:n_cols], n[:, 0:n_cols],
                                        ALU.add).then_inc(h_new, 1)
                dve.wait_ge(h_new, at + CHUNKS)

            with dve.Fori(0, GRU_STEPS) as s:
                for g in range(CHUNKS):
                    split(s, g)
                with dve.Fori(1, CHUNKS - 1) as c:
                    gate(s * CHUNKS + c, bass.ds((c - 1) * CHUNK, CHUNK), CHUNK)
                c = CHUNKS - 1
                gate(s * CHUNKS + c, slice((c - 1) * CHUNK, c * CHUNK), CHUNK)
                gate(s * CHUNKS + c + 1, slice(c * CHUNK, NODES), chunk_width(c))


def add_and_norm(nc, tag, base, result, psum, keep, hT, turn_back):
    with ExitStack() as ctx:
        def sb(name, shape, dt):
            return ctx.enter_context(nc.sbuf_tensor(name + tag, shape, dt))

        def sem(name):
            return ctx.enter_context(nc.semaphore(name + tag))

        v = sb("v", [P, WINDOWS, D], F32)
        stats = sb("stats", [P, WINDOWS, 6], F32)
        moments = sb("moments", [P, WINDOWS, 2], F32)
        spread = sb("spread", [P, WINDOWS], F32)
        base_in = sem("base_in")
        cleared = sem("cleared")
        turned = sem("turned_n")
        vec = sem("vec_n")
        rooted = sem("rooted")
        scaled = sem("scaled")
        back = sem("back")
        back_out = sem("back_out")
        stored = sem("stored")
        full = WINDOWS - 1
        at = {}

        block = ctx.enter_context(nc.Block())

        @block.sync
        def _(sp):
            sp.dma_start(v[:, 0:full, :],
                         base[0:full * P, :].rearrange("(t p) d -> p t d", p=P)).then_inc(base_in, 16)
            sp.wait_ge(cleared, 1)
            sp.dma_start(v[0:LAST, full, :], base[full * P:NODES, :]).then_inc(base_in, 16)
            sp.wait_ge(scaled, WINDOWS)
            sp.dma_start(result[0:full * P, :].rearrange("(t p) d -> p t d", p=P),
                         v[:, 0:full, :]).then_inc(stored, 16)
            sp.dma_start(result[full * P:NODES, :], v[0:LAST, full, :]).then_inc(stored, 16)
            sp.wait_ge(stored, 32)

        @block.tensor
        def _(pe):
            for g in range(CHUNKS):
                for i, t in enumerate(group_tiles(g)):
                    mm = nc.tensor.transpose(psum[:, g, i * P:(i + 1) * P], hT[:, t * P:(t + 1) * P],
                                             keep["ident"][:])
                mm.then_inc(turned, 1)
            if turn_back:
                for g in range(CHUNKS):
                    pe.wait_ge(scaled, group_tiles(g)[-1] + 1)
                    for i, t in enumerate(group_tiles(g)):
                        mm = nc.tensor.transpose(psum[:, g, i * P:(i + 1) * P], v[:, t, :],
                                                 keep["ident"][:])
                    mm.then_inc(back, 1)

        @block.vector
        def _(dve):
            m = Marks(vec)
            nc.vector.memset(v[:, full, :], 0.0).then_inc(cleared, 1)
            dve.wait_ge(base_in, 32)
            for g in range(CHUNKS):
                k = len(group_tiles(g))
                v_g = v[:, 4 * g:4 * g + k, :]
                dve.wait_ge(turned, g + 1)
                dve.wait_ge(vec, m.on(nc.vector.tensor_tensor(
                    v_g, psum[:, g, 0:k * P].rearrange("p (t d) -> p t d", d=D), v_g, ALU.add)))
                for t in group_tiles(g):
                    m.on(nc.vector.bn_stats(stats[:, t, :], v[:, t, :]))
            dve.wait_ge(vec, m.n)
            for t in range(WINDOWS):
                m.on(nc.vector.bn_aggr(moments[:, t, :], stats[:, t, :]))
            dve.wait_ge(vec, m.n)
            at["spread"] = m.on(nc.vector.tensor_scalar(spread[:], moments[:, :, 1], EPS, None, ALU.add))
            dve.wait_ge(rooted, 1)
            dve.wait_ge(vec, m.on(nc.vector.reciprocal(spread[:], spread[:])))
            for t in range(WINDOWS):
                nc.vector.tensor_scalar(v[:, t, :], v[:, t, :], moments[:, t, 0:1], spread[:, t:t + 1],
                                        ALU.subtract, ALU.mult).then_inc(scaled, 1)

        @block.scalar
        def _(act):
            act.wait_ge(vec, at["spread"])
            nc.scalar.activation(spread[:], spread[:], ACT.Sqrt).then_inc(rooted, 1)
            if turn_back:
                for g in range(CHUNKS):
                    n = chunk_width(g)
                    act.wait_ge(back, g + 1)
                    nc.scalar.activation(hT[:, g * CHUNK:g * CHUNK + n], psum[:, g, 0:n],
                                         ACT.Copy).then_inc(back_out, 1)




def edge_layers(nc, weights, psum, keep, hT, dst_rows, tables, debug):
    with ExitStack() as ctx:
        def sb(name, shape, dt):
            return ctx.enter_context(nc.sbuf_tensor(name, shape, dt))

        t = {
            "q_parts": sb("q_parts", [P, WINDOWS, 3, D], BF16),
            "agg_t": sb("agg_t", [P, PADDED], F32),
            "dst_loc": sb("dst_loc_e", [P, STEPS], F32),
            "weight": sb("weight_e", [P, STEPS], F32),
            "src_i": sb("src_i", [P, STEPS + SLOTS * GROUP], I32),
        }
        p_dram = nc.dram_tensor("p_dram", (NODES, D), F32, kind="Internal").ap()
        e_dram = [nc.dram_tensor(f"e{i}_dram", (GROUPS, P, CHUNK), F32, kind="Internal").ap()
                  for i in range(2)]
        for l, (We, be, Wn, bn) in enumerate(weights):
            clear_semaphores(nc)
            node_products(nc, l, We, be, psum, keep, hT, tables, t, p_dram)
            edge_pass(nc, f"_{l}", We[2 * D:3 * D, :] if l else None, psum, keep, t, dst_rows, p_dram,
                      e_dram[l - 1] if l else None, e_dram[l] if l < 2 else None)
            node_update(nc, f"_{l}", Wn, bn, psum, hT, t)
            if debug:
                debug(f"l{l}", nc, {"hT": hT, "agg": t["agg_t"]})


def node_products(nc, l, We, be, psum, keep, hT, tables, t, p_dram):
    tag = f"_{l}"
    with ExitStack() as ctx:
        def sb(name, shape, dt):
            return ctx.enter_context(nc.sbuf_tensor(name + tag, shape, dt))

        def sem(name):
            return ctx.enter_context(nc.semaphore(name + tag))

        w_ab = sb("w_ab", [P, 2 * D], F32)
        b_rep = sb("b_rep", [P, D], F32)
        p_sb = sb("p_sb", [P, WINDOWS, D], F32)
        residue = sb("residue_q", [P, 2, 2, D], F32)
        src_f = sb("src_f_e", [P, STEPS], F32) if l == 0 else None
        loads = sem("w_loads")
        b_in = sem("b_in")
        product = sem("product")
        p_out = sem("p_out")
        high, mid, resid, low = sem("q_high"), sem("q_mid"), sem("q_resid"), sem("q_low")
        stored = sem("p_stored")
        tabs = sem("tabs_in")
        made = sem("made")
        pairs = [range(a, min(a + 2, WINDOWS)) for a in range(0, WINDOWS, 2)]
        N = len(pairs)
        q_parts = t["q_parts"]

        def bank(i, half):
            k = len(pairs[i])
            return psum[:, i % 8, 0:k * 2 * D].rearrange("p (k h d) -> p k h d", k=k, h=2)[:, :, half, :]

        block = ctx.enter_context(nc.Block())

        @block.sync
        def _(sp):
            sp.dma_start(w_ab[:, 0:D], We[0:D, :]).then_inc(loads, 16)
            sp.dma_start(w_ab[:, D:2 * D], We[D:2 * D, :]).then_inc(loads, 16)
            sp.dma_start(b_rep[:], be.rearrange("(a n) -> a n", a=1).broadcast_to([P, D])).then_inc(b_in, 16)
            if l == 0:
                for i, to in enumerate((src_f, t["dst_loc"], t["weight"])):
                    sp.dma_start(to[:], tables[i]).then_inc(tabs, 16)
            for i in (3, 6, 9, N - 2):
                a = {3: 0, 6: 4, 9: 7, N - 2: 10}[i] * 2
                b = (i + 1) * 2
                sp.wait_ge(p_out, i + 1)
                sp.dma_start(p_dram[a * P:b * P, :].rearrange("(t p) d -> p t d", p=P),
                             p_sb[:, a:b, :]).then_inc(stored, 16)
            sp.wait_ge(p_out, N)
            sp.dma_start(p_dram[(WINDOWS - 1) * P:NODES, :], p_sb[0:LAST, WINDOWS - 1, :]).then_inc(stored, 16)
            sp.wait_ge(stored, 80)

        @block.gpsimd
        def _(pool):
            nc.gpsimd.memset(t["agg_t"][:], 0.0).then_inc(made, 1)
            if l == 0:
                nc.gpsimd.memset(t["src_i"][:, STEPS:], 0).then_inc(made, 1)
                pool.wait_ge(tabs, 48)
                nc.gpsimd.tensor_copy(t["src_i"][:, 0:STEPS], src_f[:]).then_inc(made, 1)

        @block.tensor
        def _(pe):
            pe.wait_ge(loads, 32)
            for i, pair in enumerate(pairs):
                if i >= 8:
                    pe.wait_ge(p_out, i - 7)
                    pe.wait_ge(resid, i - 7)
                for k, w in enumerate(pair):
                    mm = nc.tensor.matmul(psum[:, i % 8, k * 2 * D:(k + 1) * 2 * D],
                                          hT[:, w * P:(w + 1) * P], w_ab[:], start=True, stop=True)
                mm.then_inc(product, 1)

        @block.scalar
        def _(act):
            def second_part(i):
                a, k = pairs[i][0], len(pairs[i])
                act.wait_ge(resid, i + 1)
                nc.scalar.activation(q_parts[:, a:a + k, 1, :], residue[:, i % 2, 0:k, :],
                                     ACT.Copy).then_inc(mid, 1)

            for i, pair in enumerate(pairs):
                a, k = pair[0], len(pair)
                act.wait_ge(product, i + 1)
                nc.scalar.activation(q_parts[:, a:a + k, 0, :], bank(i, 1), ACT.Copy).then_inc(high, 1)
                if i >= 1:
                    second_part(i - 1)
            second_part(N - 1)

        @block.vector
        def _(dve):
            def third_part(i):
                a, k = pairs[i][0], len(pairs[i])
                dve.wait_ge(mid, i + 1)
                nc.vector.tensor_tensor(q_parts[:, a:a + k, 2, :], residue[:, i % 2, 0:k, :],
                                        q_parts[:, a:a + k, 1, :], ALU.subtract).then_inc(low, 1)

            dve.wait_ge(b_in, 16)
            for i, pair in enumerate(pairs):
                a, k = pair[0], len(pair)
                dve.wait_ge(high, i + 1)
                if i >= 2:
                    dve.wait_ge(low, i - 1)
                nc.vector.tensor_tensor(residue[:, i % 2, 0:k, :], bank(i, 1), q_parts[:, a:a + k, 0, :],
                                        ALU.subtract).then_inc(resid, 1)
                nc.vector.tensor_tensor(p_sb[:, a:a + k, :], bank(i, 0),
                                        b_rep[:].unsqueeze(1).broadcast_to([P, k, D]),
                                        ALU.add).then_inc(p_out, 1)
                if i >= 1:
                    third_part(i - 1)
            third_part(N - 1)


def edge_pass(nc, tag, Wc, psum, keep, t, dst_rows, p_dram, e_before, e_after):
    with ExitStack() as ctx:
        def sb(name, shape, dt):
            return ctx.enter_context(nc.sbuf_tensor(name + tag, shape, dt))

        def sem(name):
            return ctx.enter_context(nc.semaphore(name + tag))

        w_c = sb("w_c", [P, D], F32)
        ids = sb("ids", [P, SLOTS, GROUP], I32)
        p_rows = sb("p_rows", [P, SLOTS, CHUNK], F32)
        before = sb("before", [P, SLOTS, CHUNK], F32)
        locals_ = sb("locals", [P, SLOTS, CHUNK], BF16)
        hot_t = sb("hot_t", [P, 2, CHUNK], BF16)
        pre = sb("pre", [P, 2, CHUNK], F32)
        e = sb("e", [P, 2, CHUNK], F32)
        after = sb("after", [P, SLOTS, CHUNK], F32)
        hot_w = sb("hot_w", [P, 2, GROUP, P], F32)

        w_in = sem("w_in")
        ids_on = sem("ids_on")
        gathering = sem("gathering")
        rows_in = [sem(f"rows{j}") for j in range(SLOTS)]
        before_in = [sem(f"before{j}") for j in range(SLOTS)]
        locals_in = [sem(f"locals{j}") for j in range(SLOTS)]
        stored = [sem(f"stored{j}") for j in range(SLOTS)]
        all_stored = sem("all_stored")
        hot_t_on = sem("hot_t_on")
        spread = sem("spread")
        added = sem("added")
        hot_on = sem("hot_on")
        e_on = sem("e_on")
        e_turned = sem("e_turned")
        after_on = sem("after_on")
        summed = sem("summed_e")
        agg_on = sem("agg_on")

        E_BANKS, T_BANKS, A_BANKS = (0, 1), (2, 3), (4, 5)

        def rounds(engine):
            return nc.values_load(keep["rounds_i"][0:1, 0:1], engines=(engine,),
                                  min_val=MIN_ROUNDS, max_val=MAX_ROUNDS)

        def windows_of(i, engine):
            _, windows = nc.values_load_multi_w_load_instructions(
                keep["win_i"][0:1, bass.ds(i * SLOTS, SLOTS)], engines=(engine,),
                min_val=0, max_val=WINDOWS - 1)
            return windows

        block = ctx.enter_context(nc.Block())

        @block.gpsimd
        def _(pool):
            with pool.Fori(0, rounds(mybir.EngineType.Pool)) as i:
                for j in range(SLOTS):
                    pool.wait_ge(ids_on, i * SLOTS + j + 1)
                    pool.sem_inc(gathering, 1)
                    for m in range(GROUP):
                        nc.gpsimd.indirect_dma_start(
                            out=p_rows[:, j, m * D:(m + 1) * D], out_offset=None, in_=p_dram,
                            in_offset=bass.IndirectOffsetOnAxis(ap=ids[:, j, m:m + 1].bitcast(U32), axis=0),
                        ).then_inc(rows_in[j], 16)

        @block.sync
        def _(sp):
            if e_before is not None:
                sp.dma_start(w_c[:], Wc).then_inc(w_in, 16)

            def load_locals(g, j):
                sp.dma_start(locals_[:, j, :], dst_rows[bass.ds(g * CHUNK, CHUNK)]
                             .rearrange("(a n) -> a n", a=1).broadcast_to([P, CHUNK])
                             ).then_inc(locals_in[j], 16)

            def load_before(g, j):
                sp.dma_start(before[:, j, :], e_before[bass.ds(g, 1), :, :]
                             .rearrange("a p n -> (a p) n")).then_inc(before_in[j], 16)

            def store(i, j):
                sp.wait_ge(after_on, i * SLOTS + j + 3)
                sp.dma_start(e_after[bass.ds(i * SLOTS + j, 1), :, :].rearrange("a p n -> (a p) n"),
                             after[:, j, :]).then_inc(stored[j], 16)

            for j in range(SLOTS):
                load_locals(j, j)
                if e_before is not None:
                    load_before(j, j)
            last = nc.values_load(keep["rounds_i"][0:1, 1:2], engines=(mybir.EngineType.SP,),
                                  min_val=MIN_ROUNDS - 1, max_val=MAX_ROUNDS - 1)
            with sp.Fori(0, last) as i:
                for j in range(SLOTS):
                    sp.wait_ge(hot_t_on, i * SLOTS + j + 1)
                    load_locals((i + 1) * SLOTS + j, j)
                    if e_before is not None:
                        sp.wait_ge(spread, i * SLOTS + j + 1)
                        load_before((i + 1) * SLOTS + j, j)
                    if e_after is not None:
                        store(i, j)
            sp.wait_ge(hot_t_on, last * SLOTS + 1)
            load_locals((last + 1) * SLOTS, 0)
            if e_after is not None:
                for j in range(SLOTS):
                    store(last, j)
                for j in range(SLOTS):
                    sp.wait_ge(stored[j], last * 16 + 32)
                    sp.sem_inc(all_stored, 1)

        @block.tensor
        def _(pe):
            pe.sem_inc(summed, 2)
            if e_before is not None:
                pe.wait_ge(w_in, 16)

            def products(i, j, windows):
                if j >= 2:
                    pe.wait_ge(added, i * SLOTS + j - 1)
                pe.wait_ge(hot_t_on, i * SLOTS + j + 1)
                if e_before is not None:
                    pe.wait_ge(before_in[j], i * 16 + 16)
                for m in range(GROUP):
                    o = psum[:, E_BANKS[j % 2], m * D:(m + 1) * D]
                    for part in range(3):
                        mm = nc.tensor.matmul(o, hot_t[:, j % 2, m * P:(m + 1) * P],
                                              t["q_parts"][:, bass.ds(windows[j], 1), part, :],
                                              start=(part == 0), stop=(part == 2 and e_before is None))
                    if e_before is not None:
                        mm = nc.tensor.matmul(o, before[:, j, m * P:(m + 1) * P], w_c[:],
                                              start=False, stop=True)
                mm.then_inc(spread, 1)

            def turn_and_sum(i, j):
                pe.wait_ge(e_on, i * SLOTS + j + 3)
                if e_after is not None:
                    pe.wait_ge(after_on, i * SLOTS + j + 1)
                    for m in range(GROUP):
                        mm = nc.tensor.transpose(psum[:, T_BANKS[j % 2], m * P:(m + 1) * P],
                                                 e[:, j % 2, m * D:(m + 1) * D], keep["ident"][:])
                    mm.then_inc(e_turned, 1)
                pe.wait_ge(hot_on, i * (SLOTS * GROUP) + (j + 1) * GROUP)
                pe.wait_ge(agg_on, i * SLOTS + j + 1)
                for m in range(GROUP):
                    mm = nc.tensor.matmul(psum[:, A_BANKS[j % 2], 0:P],
                                          e[:, j % 2, m * D:(m + 1) * D], hot_w[:, j % 2, m, :],
                                          start=(m == 0), stop=(m == GROUP - 1))
                mm.then_inc(summed, 1)

            with pe.Fori(0, rounds(mybir.EngineType.PE)) as i:
                windows = windows_of(i, mybir.EngineType.PE)
                products(i, 0, windows)
                for j in range(1, SLOTS):
                    products(i, j, windows)
                    turn_and_sum(i, j - 1)
                turn_and_sum(i, SLOTS - 1)

        @block.scalar
        def _(act):
            act.sem_inc(e_on, 2)
            act.sem_inc(after_on, 2)
            for j in range(SLOTS):
                act.sem_inc(stored[j], 16)

            def relu(i, j):
                act.wait_ge(added, i * SLOTS + j + 1)
                act.wait_ge(summed, i * SLOTS + j + 1)
                nc.scalar.activation(e[:, j % 2, :], pre[:, j % 2, :], ACT.Relu).then_inc(e_on, 1)

            def take(i, j):
                if e_after is not None:
                    act.wait_ge(e_turned, i * SLOTS + j + 1)
                    act.wait_ge(stored[j], i * 16 + 16)
                    nc.scalar.activation(after[:, j, :], psum[:, T_BANKS[j % 2], :],
                                         ACT.Copy).then_inc(after_on, 1)

            nc.scalar.preload_act_table(ACT.Relu)
            with act.Fori(0, rounds(mybir.EngineType.Activation)) as i:
                relu(i, 0)
                for j in range(1, SLOTS):
                    relu(i, j)
                    take(i, j - 1)
                take(i, SLOTS - 1)

        @block.vector
        def _(dve):
            dve.sem_inc(agg_on, 2)
            nc.vector.tensor_copy(ids[:], t["src_i"][:, 0:SLOTS * GROUP]
                                  .rearrange("p (j m) -> p j m", m=GROUP)).then_inc(ids_on, 1)
            dve.wait_ge(ids_on, 1)
            dve.sem_inc(ids_on, SLOTS - 1)

            def turned_hot(i, j):
                dve.wait_ge(locals_in[j], i * 16 + 16)
                nc.vector.tensor_scalar(hot_t[:, j % 2, :], locals_[:, j, :], keep["lane_f"][:, 0:1],
                                        None, ALU.is_equal).then_inc(hot_t_on, 1)

            def hots(i, j):
                for m in range(GROUP):
                    k = i * (SLOTS * GROUP) + (j * GROUP + m)
                    nc.vector.tensor_scalar(hot_w[:, j % 2, m, :], keep["col_f"][:],
                                            t["dst_loc"][:, bass.ds(k, 1)],
                                            t["weight"][:, bass.ds(k, 1)],
                                            ALU.is_equal, ALU.mult).then_inc(hot_on, 1)

            def add(i, j):
                dve.wait_ge(spread, i * SLOTS + j + 1)
                dve.wait_ge(rows_in[j], i * (16 * GROUP) + 16 * GROUP)
                dve.wait_ge(e_on, i * SLOTS + j + 1)
                nc.vector.tensor_tensor(pre[:, j % 2, :], psum[:, E_BANKS[j % 2], :], p_rows[:, j, :],
                                        ALU.add).then_inc(added, 1)
                dve.wait_ge(added, i * SLOTS + j + 1)
                nc.vector.tensor_copy(ids[:, j, :],
                                      t["src_i"][:, bass.ds(i * (SLOTS * GROUP) + (SLOTS + j) * GROUP, GROUP)]
                                      ).then_inc(ids_on, 1)

            def gather_up(i, j, windows):
                dve.wait_ge(summed, i * SLOTS + j + 3)
                dve.wait_ge(agg_on, i * SLOTS + j + 2)
                a = t["agg_t"][:, bass.ds(windows[j] * P, P)]
                nc.vector.tensor_tensor(a, psum[:, A_BANKS[j % 2], 0:P], a, ALU.add).then_inc(agg_on, 1)

            turned_hot(0, 0)
            with dve.Fori(0, rounds(mybir.EngineType.DVE)) as i:
                windows = windows_of(i, mybir.EngineType.DVE)
                for j in range(SLOTS):
                    hots(i, j)
                    add(i, j)
                    if j + 1 < SLOTS:
                        turned_hot(i, j + 1)
                    else:
                        turned_hot(i + 1, 0)
                    if j:
                        gather_up(i, j - 1, windows)
                gather_up(i, SLOTS - 1, windows)


def node_update(nc, tag, Wn, bn, psum, hT, t):
    with ExitStack() as ctx:
        def sb(name, shape, dt):
            return ctx.enter_context(nc.sbuf_tensor(name + tag, shape, dt))

        def sem(name):
            return ctx.enter_context(nc.semaphore(name + tag))

        w_n = sb("w_n", [P, 2, D], F32)
        b_n = sb("b_n", [P, 1], F32)
        loads = sem("wn_loads")
        product = sem("wn_product")
        x_on = sem("x_on")
        block = ctx.enter_context(nc.Block())

        @block.sync
        def _(sp):
            sp.dma_start(w_n[:], Wn.rearrange("(h p) d -> p h d", p=P)).then_inc(loads, 16)
            sp.dma_start(b_n[:], bn.rearrange("(p a) -> p a", a=1)).then_inc(loads, 16)

        @block.tensor
        def _(pe):
            pe.wait_ge(loads, 32)
            for c in range(CHUNKS):
                n = chunk_width(c)
                nc.tensor.matmul(psum[:, c, 0:n], w_n[:, 0, :], hT[:, c * CHUNK:c * CHUNK + n],
                                 start=True, stop=False)
                nc.tensor.matmul(psum[:, c, 0:n], w_n[:, 1, :], t["agg_t"][:, c * CHUNK:c * CHUNK + n],
                                 start=False, stop=True).then_inc(product, 1)

        @block.scalar
        def _(act):
            act.wait_ge(loads, 32)
            for c in range(CHUNKS):
                n = chunk_width(c)
                act.wait_ge(product, c + 1)
                nc.scalar.activation(hT[:, c * CHUNK:c * CHUNK + n], psum[:, c, 0:n], ACT.Relu,
                                     bias=b_n[:, 0:1]).then_inc(x_on, 1)


_INS = ["x", "src", "dst", "edge_weight", "L0_gnn_W_msg", "L0_gnn_b_msg", "L0_gnn_W_ih", "L0_gnn_W_hh",
        "L0_gnn_b_ih", "L0_gnn_b_hh", "L1_gnn_We0", "L1_gnn_be0", "L1_gnn_Wn0", "L1_gnn_bn0",
        "L1_gnn_We1", "L1_gnn_be1", "L1_gnn_Wn1", "L1_gnn_bn1", "L1_gnn_We2", "L1_gnn_be2",
        "L1_gnn_Wn2", "L1_gnn_bn2"]
_TRANSPOSED = ("L0_gnn_W_msg", "L0_gnn_W_ih", "L0_gnn_W_hh")


def kernel(**inputs):
    import numpy as np
    from concourse import bacc
    from concourse.bass_utils import run_bass_kernel_spmd

    nc = bacc.Bacc("TRN2", target_bir_lowering=False, num_devices=1)
    laid = []
    for name in _INS:
        a = np.asarray(inputs[name])
        laid.append((name, np.ascontiguousarray(a.T if name in _TRANSPOSED else a)))
        if name == "x":
            laid.append(("xT", np.ascontiguousarray(a.T)))
    arrays, args = {}, []
    for name, a in laid:
        arrays[f"in_{name}"] = a
        args.append(nc.dram_tensor(f"in_{name}", a.shape, mybir.dt.from_np(a.dtype),
                                   kind="ExternalInput").ap())
    out = nc.dram_tensor("out", (NODES, D), F32, kind="ExternalOutput").ap()
    build(nc, *args, out)
    results = run_bass_kernel_spmd(nc, [arrays], core_ids=[0])
    return results.results[0]["out"]
```

```python
from contextlib import ExitStack

import concourse.bass as bass
from concourse import mybir

F32 = mybir.dt.float32
BF16 = mybir.dt.bfloat16
F16 = mybir.dt.float16
I32 = mybir.dt.int32
U32 = mybir.dt.uint32
ALU = mybir.AluOpType
ACT = mybir.ActivationFunctionType
AXIS_X = mybir.AxisListType.X

P = 128
NODES = 3125
EDGES = 50000
D = 128
GRU_STEPS = 5
EPS = 1e-5
WINDOWS = -(-NODES // P)
PADDED = WINDOWS * P
LAST = NODES - (WINDOWS - 1) * P
TILES = -(-EDGES // P)
EVAC_DVE = (1, 3, 5)
TCH = 4
GROUP = 4
SLOTS = 4
MAX_ROUNDS = -(-((TILES + WINDOWS - 1 + (GROUP - 1) * WINDOWS) // GROUP) // SLOTS)
GROUPS = MAX_ROUNDS * SLOTS
STEPS = GROUPS * GROUP
MIN_ROUNDS = TILES // (GROUP * SLOTS)
CHUNK = 512
CHUNKS = -(-NODES // CHUNK)
NO_NODE = 100000.0


class Marks:

    def __init__(self, sem, base=0):
        self.sem, self.base, self.n = sem, base, 0

    def on(self, ins):
        self.n += 1
        ins.then_inc(self.sem, 1)
        return self.base + self.n


def build(nc, x, xT, src, dst, edge_weight, W_msgT, b_msg, W_ihT, W_hhT, b_ih, b_hh,
          We0, be0, Wn0, bn0, We1, be1, Wn1, bn1, We2, be2, Wn2, bn2, out, debug=None):
    ctx = ExitStack()
    with ctx:
        psum = ctx.enter_context(nc.psum_tensor("psum", [P, 8, CHUNK], F32))

        def sb(name, shape, dt):
            return ctx.enter_context(nc.sbuf_tensor(name, shape, dt))

        keep = {
            "ident": sb("ident", [P, P], F32),
            "ones": sb("ones", [P, P], F32),
            "lane_f": sb("lane_f", [P, 1], F32),
            "col_f": sb("col_f", [P, P], F32),
            "pairs_i": sb("pairs_i", [1, WINDOWS, 4], I32),
            "win_i": sb("win_i", [1, GROUPS], I32),
            "rounds_i": sb("rounds_i", [1, 2], I32),
        }
        hT = sb("hT", [P, PADDED], F32)
        dst_rows = nc.dram_tensor("dst_rows", ((STEPS + GROUP) * P,), BF16, kind="Internal").ap()
        tables = nc.dram_tensor("tables", (3, P, STEPS), F32, kind="Internal").ap()
        x1_dram = nc.dram_tensor("x1_dram", (PADDED, D), F32, kind="Internal").ap()

        with ExitStack() as l0:
            adj = l0.enter_context(nc.sbuf_tensor("adj", [P, WINDOWS, NODES], F16))
            params = {name: l0.enter_context(nc.sbuf_tensor(name, shape, F32)) for name, shape in (
                ("w_msg", [P, D]), ("w_ih", [P, 3 * D]), ("w_hh", [P, 3 * D]),
                ("b_rep", [P, D]), ("b_i", [P, 3]), ("b_h", [P, 3]))}
            with ExitStack() as tab:
                for name, dt in (("src_f", F32), ("dst_loc", F32), ("weight", F32)):
                    keep[name] = tab.enter_context(nc.sbuf_tensor(name, [P, STEPS], dt))
                step_tables(nc, src, dst, edge_weight, psum, keep, dst_rows, tables)
                if debug:
                    debug("tables", nc, keep)
                build_adjacency(nc, (xT, W_msgT, b_msg, W_ihT, W_hhT, b_ih, b_hh), psum, keep, hT,
                                params, adj)
                if debug:
                    debug("adj", nc, {"adj": adj})
            gated_steps(nc, psum, keep, hT, params, adj)
            if debug:
                debug("h5", nc, {"hT": hT})
        add_and_norm(nc, "_0", x, x1_dram, psum, keep, hT, turn_back=True)
        if debug:
            debug("x1", nc, {"hT": hT})
        edge_layers(nc, ((We0, be0, Wn0, bn0), (We1, be1, Wn1, bn1), (We2, be2, Wn2, bn2)),
                    psum, keep, hT, dst_rows, tables, debug)
        add_and_norm(nc, "_1", x1_dram[0:NODES, :], out, psum, keep, hT, turn_back=False)


def clear_semaphores(nc):
    used = sorted(int(n) for n in nc.released_uncleared_semaphores)
    with nc.Block() as block:
        @block.sync
        def _(sp):
            start = 0
            for i in range(1, len(used) + 1):
                if i == len(used) or used[i] != used[i - 1] + 1:
                    sp.sem_clear(range(used[start], used[i - 1] + 1))
                    start = i


def step_tables(nc, src, dst, edge_weight, psum, keep, dst_rows, tables):
    with ExitStack() as ctx:
        def sb(name, shape, dt):
            return ctx.enter_context(nc.sbuf_tensor(name, shape, dt))

        def sem(name):
            return ctx.enter_context(nc.semaphore(name))

        W = WINDOWS
        whole = EDGES // P
        rest = EDGES - whole * P
        q_full = whole // P
        q_rows = whole - q_full * P
        raw = {n: sb(f"raw_{n}", [P, TCH, P], dt) for n, dt in
               (("dst", I32), ("src", I32), ("weight", F32))}
        rows = {"dst": sb("rows_dst", [P, TCH, P], F32), "src": sb("rows_src", [P, TCH, P], F32),
                "weight": raw["weight"]}
        counts = sb("counts", [P, W + 1], F32)
        step_i = sb("step_i", [P, STEPS], I32)
        step_f = sb("step_f", [P, STEPS], F32)
        lane_i = sb("lane_i", [P, 1], I32)
        tri = sb("tri", [P, P], F32)
        edge_i = sb("edge_i", [W, 2], I32)
        edge_f = sb("edge_f", [W, 2], F32)
        size_f = sb("size_f", [W, 1], F32)
        size_i = sb("size_i", [W, 2], I32)
        size_g = sb("size_g", [W, 2], F32)
        bounds = sb("bounds", [W, 6], F32)
        flags = sb("flags", [W, 2, STEPS], F32)
        names = sb("names", [W, 2, P], F32)
        totals_i = sb("totals_i", [1, 2], I32)
        tile_of = sb("tile_of", [P, STEPS], F32)
        lane_q = sb("lane_q", [P, TCH], F32)
        pick = sb("pick", [P, TCH, STEPS], F32)
        below = pick[:].rearrange("p q s -> p (q s)")[:, 0:TCH * P]
        dst_t = sb("dst_t", [P, TCH, P], BF16)

        edges_in = {n: sem(f"{n}_in") for n in raw}
        padded = sem("padded")
        iotas = sem("iotas")
        vec = sem("vec")
        small = sem("small")
        picked = sem("picked")
        turned = sem("turned")
        dst_out = sem("dst_out")
        done = {}

        block = ctx.enter_context(nc.Block())

        @block.gpsimd
        def _(pool):
            nc.gpsimd.memset(raw["dst"][:, TCH - 1, :], int(NO_NODE)).then_inc(padded, 1)
            nc.gpsimd.memset(raw["src"][:, TCH - 1, :], 0).then_inc(padded, 1)
            nc.gpsimd.memset(raw["weight"][:, TCH - 1, :], 0.0).then_inc(padded, 1)
            nc.gpsimd.iota(step_i[:], [[1, STEPS]], 0, 0).then_inc(iotas, 1)
            nc.gpsimd.iota(lane_i[:], [[0, 1]], 0, 1).then_inc(iotas, 1)
            nc.gpsimd.memset(keep["ones"][:], 1.0).then_inc(iotas, 1)

        @block.vector
        def _(dve):
            v = Marks(vec)

            def after(ins):
                dve.wait_ge(vec, v.on(ins))

            dve.wait_ge(iotas, 3)
            v.on(nc.vector.memset(dst_t[:, TCH - 1, :], 0.0))
            v.on(nc.vector.tensor_copy(step_f[:], step_i[:]))
            v.on(nc.vector.tensor_copy(keep["lane_f"][:], lane_i[:]))
            v.on(nc.vector.memset(counts[:, 0:1], 0.0))
            after(nc.vector.tensor_copy(keep["col_f"][:], step_i[:, 0:P]))
            v.on(nc.vector.tensor_scalar(keep["ident"][:], keep["col_f"][:], keep["lane_f"][:, 0:1],
                                         None, ALU.is_equal))
            v.on(nc.vector.tensor_scalar(tri[:], keep["col_f"][:], keep["lane_f"][:, 0:1],
                                         None, ALU.is_gt))
            v.on(nc.vector.tensor_scalar(names[:, 0, :], keep["ones"][0:W, :], keep["lane_f"][0:W, 0:1],
                                         None, ALU.mult))
            for q in range(TCH):
                v.on(nc.vector.tensor_scalar(lane_q[:, q:q + 1], keep["lane_f"][:], float(q * P), None,
                                             ALU.add))
            dve.wait_ge(edges_in["dst"], 48)
            after(nc.vector.tensor_copy(rows["dst"][:], raw["dst"][:]))
            flat = rows["dst"][:].rearrange("p q c -> p (q c)")
            for w in range(1, W + 1):
                after(nc.vector.tensor_scalar(below, flat, float(w * P), 0.0, ALU.is_lt,
                                              ALU.add, accum_out=counts[:, w:w + 1]))
            done["counts"] = v.n
            dve.wait_ge(edges_in["src"], 48)
            v.on(nc.vector.tensor_copy(rows["src"][:], raw["src"][:]))
            dve.wait_ge(small, 1)
            after(nc.vector.tensor_copy(edge_i[:], psum[0:W, 0, 0:2]))
            after(nc.vector.tensor_scalar(edge_i[:], edge_i[:], P.bit_length() - 1, None,
                                          ALU.logical_shift_right))
            after(nc.vector.tensor_copy(edge_f[:], edge_i[:]))
            after(nc.vector.tensor_tensor(size_f[:], edge_f[:, 1:2], edge_f[:, 0:1], ALU.subtract))
            v.on(nc.vector.tensor_scalar(size_i[:, 0:1], size_f[:], float(GROUP), None, ALU.add))
            after(nc.vector.tensor_scalar(size_i[:, 1:2], size_f[:], 2.0, 4.0, ALU.add, ALU.max))
            v.on(nc.vector.tensor_scalar(size_i[:, 0:1], size_i[:, 0:1], GROUP.bit_length() - 1, None,
                                         ALU.logical_shift_right))
            after(nc.vector.tensor_scalar(size_i[:, 1:2], size_i[:, 1:2], 1, None,
                                          ALU.logical_shift_right))
            after(nc.vector.tensor_copy(size_g[:], size_i[:]))
            done["sizes"] = v.n
            dve.wait_ge(small, 2)
            after(nc.vector.tensor_scalar(bounds[:, 0:1], psum[0:W, 1, 0:1], float(GROUP), None, ALU.mult))
            v.on(nc.vector.scalar_tensor_tensor(out=bounds[:, 1:2], in0=size_g[:, 0:1],
                                                scalar=float(GROUP), in1=bounds[:, 0:1],
                                                op0=ALU.mult, op1=ALU.add))
            v.on(nc.vector.tensor_copy(bounds[:, 3:4], psum[0:W, 1, 1:2]))
            v.on(nc.vector.tensor_tensor(bounds[:, 4:5], psum[0:W, 1, 1:2], size_g[:, 1:2], ALU.add))
            after(nc.vector.tensor_scalar(bounds[:, 5:6], psum[0:W, 1, 0:1], 2.0, None, ALU.mult))
            v.on(nc.vector.tensor_tensor(bounds[:, 5:6], bounds[:, 5:6], bounds[:, 3:4], ALU.subtract))
            after(nc.vector.tensor_tensor(bounds[:, 2:3], bounds[:, 0:1], edge_f[:, 0:1], ALU.subtract))
            v.on(nc.vector.tensor_scalar(names[:, 1, :], keep["ones"][0:W, :], bounds[:, 2:3],
                                         None, ALU.mult))
            v.on(nc.vector.tensor_scalar(flags[:, 0, :], step_f[0:W, :], bounds[:, 0:1], None, ALU.is_ge))
            after(nc.vector.tensor_scalar(flags[:, 1, :], step_f[0:W, :], bounds[:, 1:2], None,
                                          ALU.is_lt))
            after(nc.vector.tensor_tensor(flags[:, 1, :], flags[:, 1, :], flags[:, 0, :], ALU.mult))
            done["flags"] = v.n
            dve.wait_ge(small, 3)
            v.on(nc.vector.memset(keep["pairs_i"][:, :, 3], 0))
            for i in range(3):
                v.on(nc.vector.tensor_copy(keep["pairs_i"][:, :, i], psum[0:1, 2, i * W:(i + 1) * W]))
            after(nc.vector.tensor_scalar(totals_i[:, 0:1], psum[0:1, 2, 3 * W:3 * W + 1],
                                          float(SLOTS - 1), None, ALU.add))
            v.on(nc.vector.tensor_scalar(totals_i[:, 1:2], psum[0:1, 2, 3 * W:3 * W + 1], -1.0, None,
                                         ALU.add))
            v.on(nc.vector.tensor_scalar(keep["rounds_i"][:, 0:1], totals_i[:, 0:1],
                                         SLOTS.bit_length() - 1, None, ALU.logical_shift_right))
            dve.wait_ge(vec, v.n)
            v.on(nc.vector.tensor_scalar(keep["rounds_i"][:, 1:2], totals_i[:, 1:2],
                                         SLOTS.bit_length() - 1, None, ALU.logical_shift_right))
            dve.wait_ge(small, 4)
            v.on(nc.vector.tensor_copy(keep["win_i"][:], psum[0:1, 3, 0:STEPS:GROUP]))
            after(nc.vector.scalar_tensor_tensor(out=tile_of[:], in0=psum[:, 4, 0:STEPS], scalar=-1.0,
                                                 in1=step_f[:], op0=ALU.mult, op1=ALU.add))
            for q in range(TCH):
                v.on(nc.vector.tensor_scalar(pick[:, q, :], tile_of[:], lane_q[:, q:q + 1], None,
                                             ALU.is_equal))
            done["pick"] = v.n
            dve.wait_ge(vec, v.n)
            after(nc.vector.tensor_copy(tile_of[:], psum[:, 3, 0:STEPS]))
            dve.wait_ge(picked, 1)
            v.on(nc.vector.tensor_copy(keep["src_f"][:], psum[:, 5, 0:STEPS]))
            dve.wait_ge(picked, 2)
            after(nc.vector.scalar_tensor_tensor(
                out=keep["dst_loc"][:], in0=tile_of[:], scalar=-float(P), in1=psum[:, 6, 0:STEPS],
                op0=ALU.mult, op1=ALU.add))
            done["dst_loc"] = v.n
            dve.wait_ge(picked, 3)
            v.on(nc.vector.tensor_copy(keep["weight"][:], psum[:, 7, 0:STEPS]))
            for q in range(TCH):
                n_q = min(P, STEPS - q * P)
                dve.wait_ge(turned, q + 1)
                v.on(nc.vector.tensor_copy(dst_t[0:n_q, q, :], psum[0:n_q, q, 0:P]))
            done["dst_t"] = v.n

        @block.tensor
        def _(pe):
            ones = keep["ones"]
            pe.wait_ge(vec, done["counts"])
            pe.wait_ge(iotas, 3)
            nc.tensor.matmul(psum[0:W, 0, 0:1], counts[:, 0:W], ones[:, 0:1], start=True, stop=True)
            nc.tensor.matmul(psum[0:W, 0, 1:2], counts[:, 1:W + 1], ones[:, 0:1],
                             start=True, stop=True).then_inc(small, 1)
            pe.wait_ge(vec, done["sizes"])
            nc.tensor.matmul(psum[0:W, 1, 0:2], tri[0:W, 0:W], size_g[:],
                             start=True, stop=True).then_inc(small, 1)
            pe.wait_ge(vec, done["flags"])
            for i in range(3):
                nc.tensor.matmul(psum[0:1, 2, i * W:(i + 1) * W], bounds[:, 3 + i:4 + i],
                                 keep["ident"][0:W, 0:W], start=True, stop=True)
            nc.tensor.matmul(psum[0:1, 2, 3 * W:3 * W + 1], size_g[:, 0:1], ones[0:W, 0:1],
                             start=True, stop=True).then_inc(small, 1)
            for b in range(2):
                mm = nc.tensor.matmul(psum[:, 3 + b, 0:STEPS], names[:, b, :], flags[:, 1, :],
                                      start=True, stop=True)
            mm.then_inc(small, 1)
            pe.wait_ge(vec, done["pick"])
            pe.wait_ge(edges_in["weight"], 48)
            for b, name in ((5, "src"), (6, "dst"), (7, "weight")):
                for q in range(TCH):
                    mm = nc.tensor.matmul(psum[:, b, 0:STEPS], rows[name][:, q, :], pick[:, q, :],
                                          start=(q == 0), stop=(q == TCH - 1))
                mm.then_inc(picked, 1)
            pe.wait_ge(vec, done["dst_loc"])
            for q in range(TCH):
                n = min(P, STEPS - q * P)
                nc.tensor.transpose(psum[0:n, q, 0:P], keep["dst_loc"][:, q * P:q * P + n],
                                    keep["ident"][:]).then_inc(turned, 1)

        @block.sync
        def _(sp):
            sp.wait_ge(padded, 3)
            for n, dram in (("dst", dst), ("src", src), ("weight", edge_weight)):
                full = dram[0:q_full * P * P].rearrange("(q r p) -> r q p", p=P, r=P)
                sp.dma_start(raw[n][:, 0:q_full, :], full).then_inc(edges_in[n], 16)
                part = dram[q_full * P * P:whole * P].rearrange("(r p) -> r p", p=P)
                sp.dma_start(raw[n][0:q_rows, q_full, :], part).then_inc(edges_in[n], 16)
                tail = dram[whole * P:EDGES].rearrange("(r p) -> r p", r=1)
                sp.dma_start(raw[n][q_rows:q_rows + 1, q_full, 0:rest], tail).then_inc(edges_in[n], 16)
            sp.wait_ge(vec, done["dst_t"])
            for q in range(TCH):
                n = min(P, STEPS + GROUP - q * P)
                sp.dma_start(dst_rows[q * P * P:(q * P + n) * P].rearrange("(r p) -> r p", p=P),
                             dst_t[0:n, q, :]).then_inc(dst_out, 16)
            for i, name in enumerate(("src_f", "dst_loc", "weight")):
                sp.dma_start(tables[i], keep[name][:]).then_inc(dst_out, 16)
            sp.wait_ge(dst_out, 16 * (TCH + 3))


def build_adjacency(nc, l0_inputs, psum, keep, hT, params, adj):
    xT, W_msgT, b_msg, W_ihT, W_hhT, b_ih, b_hh = l0_inputs
    with ExitStack() as ctx:
        def sb(name, shape, dt):
            return ctx.enter_context(nc.sbuf_tensor(name, shape, dt))

        def sem(name):
            return ctx.enter_context(nc.semaphore(name))

        node_h = sb("node_h", [P, NODES], F16)
        col_h = sb("col_h", [P, P], F16)
        src_c = sb("src_c", [P, STEPS], F32)
        src_hot = sb("src_hot", [P, 2, NODES], F16)
        dst_hot = sb("dst_hot", [P, 2, P], F16)
        CENTER = NODES // 2
        HALF = CHUNKS // 2 * CHUNK

        iotas = sem("iotas_a")
        consts = sem("consts_a")
        hot = sem("hot")
        half_used = sem("half_used")
        used = sem("used")
        act_out = sem("act_out")
        dve_out = sem("dve_out")
        loads = sem("l0_loads")

        def width(c):
            return min(CHUNK, NODES - c * CHUNK)

        act_banks = [c for c in range(CHUNKS) if c not in EVAC_DVE]
        block = ctx.enter_context(nc.Block())

        @block.gpsimd
        def _(pool):
            nc.gpsimd.iota(node_h[:], [[1, NODES]], -CENTER, 0,
                           allow_small_or_imprecise_dtypes=True).then_inc(iotas, 1)
            nc.gpsimd.iota(col_h[:], [[1, P]], 0, 0,
                           allow_small_or_imprecise_dtypes=True).then_inc(iotas, 1)

        def window_pairs(w, engine):
            _, (first, end, shift, _) = nc.values_load_multi_w_load_instructions(
                keep["pairs_i"][0:1, w if isinstance(w, int) else bass.ds(w, 1), :],
                engines=(engine,), min_val=0, max_val=STEPS)
            return first, end, shift

        @block.vector
        def _(dve):
            nc.vector.tensor_scalar(src_c[:], keep["src_f"][:], -float(CENTER), None,
                                    ALU.add).then_inc(consts, 1)
            dve.sem_inc(half_used, 2)
            dve.sem_inc(used, 2)
            dve.wait_ge(iotas, 2)
            dve.wait_ge(consts, 1)

            def one_hots(pair, shift):
                step = nc.s_assert_within(
                    (pair + shift) * 2, 0, STEPS - 2,
                    skip_runtime_bounds_check_because="the tables have room for all windows' pairs")
                for j in range(2):
                    k = bass.ds(step + j, 1)
                    dve.wait_ge(half_used, pair * 2 + j + 1)
                    nc.vector.tensor_scalar(src_hot[:, j, 0:HALF], node_h[:, 0:HALF], src_c[:, k],
                                            None, ALU.is_equal).then_inc(hot, 1)
                    dve.wait_ge(used, pair * 2 + j + 1)
                    nc.vector.tensor_scalar(dst_hot[:, j, :], col_h[:], keep["dst_loc"][:, k], None,
                                            ALU.is_equal).then_inc(hot, 1)
                    nc.vector.tensor_scalar(src_hot[:, j, HALF:NODES], node_h[:, HALF:NODES],
                                            src_c[:, k], None, ALU.is_equal).then_inc(hot, 1)

            def rest_of(first, end, shift):
                with dve.Fori(first + 1, end) as pair:
                    one_hots(pair, shift)

            def take(w, end):
                dve.wait_ge(used, end * 2 + 2)
                for c in EVAC_DVE:
                    nc.vector.tensor_copy(adj[:, w, c * CHUNK:c * CHUNK + width(c)],
                                          psum[:, c, 0:width(c)]).then_inc(dve_out, 1)

            first, _, shift = window_pairs(0, mybir.EngineType.DVE)
            one_hots(first, shift)
            with dve.Fori(0, WINDOWS - 1) as w:
                first, end, shift = window_pairs(w, mybir.EngineType.DVE)
                rest_of(first, end, shift)
                first, _, shift = window_pairs(w + 1, mybir.EngineType.DVE)
                one_hots(first, shift)
                take(bass.ds(w, 1), end)
            first, end, shift = window_pairs(WINDOWS - 1, mybir.EngineType.DVE)
            rest_of(first, end, shift)
            take(WINDOWS - 1, end)

        @block.scalar
        def _(act):
            nc.scalar.preload_act_table(ACT.Copy)
            with act.Fori(0, WINDOWS) as w:
                _, end, _ = window_pairs(w, mybir.EngineType.Activation)
                act.wait_ge(used, end * 2 + 2)
                for c in act_banks:
                    nc.scalar.copy(adj[:, bass.ds(w, 1), c * CHUNK:c * CHUNK + width(c)],
                                   psum[:, c, 0:width(c)]).then_inc(act_out, 1)

        @block.sync
        def _(sp):
            sp.dma_start(hT[:, 0:NODES], xT).then_inc(loads, 16)
            for name, dram in (("w_msg", W_msgT), ("w_ih", W_ihT), ("w_hh", W_hhT)):
                sp.dma_start(params[name][:], dram).then_inc(loads, 16)
            sp.dma_start(params["b_rep"][:], b_msg.rearrange("(a n) -> a n", a=1)
                         .broadcast_to([P, D])).then_inc(loads, 16)
            for name, dram in (("b_i", b_ih), ("b_h", b_hh)):
                with nc.allow_non_contiguous_dma(reason="384 biases, one a partition"):
                    sp.dma_start(params[name][:], dram.rearrange("(g p) -> p g", p=P)).then_inc(loads, 16)
            sp.wait_ge(loads, 7 * 16)

        @block.tensor
        def _(pe):
            pe.sem_inc(act_out, len(act_banks))
            pe.sem_inc(dve_out, len(EVAC_DVE))

            def multiply(pair, w=None):
                for j in range(2):
                    pe.wait_ge(hot, pair * 6 + 3 * j + 2)
                    for c in range(CHUNKS):
                        if c * CHUNK == HALF:
                            pe.wait_ge(hot, pair * 6 + 3 * j + 3)
                        start = w is not None and j == 0
                        if start and c in EVAC_DVE:
                            pe.wait_ge(dve_out, w * len(EVAC_DVE) + EVAC_DVE.index(c) + 1)
                        elif start:
                            pe.wait_ge(act_out, w * len(act_banks) + act_banks.index(c) + 1)
                        mm = nc.tensor.matmul(psum[:, c, 0:width(c)], dst_hot[:, j, :],
                                              src_hot[:, j, c * CHUNK:c * CHUNK + width(c)],
                                              start=start, stop=False, skip_group_check=True)
                        if (c + 1) * CHUNK == HALF:
                            mm.then_inc(half_used, 1)
                    mm.then_inc(used, 1)

            with pe.Fori(0, WINDOWS) as w:
                first, end, _ = window_pairs(w, mybir.EngineType.PE)
                multiply(first, w)
                with pe.Fori(first + 1, end) as pair:
                    multiply(pair)


def chunk_width(c):
    return min(CHUNK, NODES - c * CHUNK)


def group_tiles(g):
    return range(4 * g, min(4 * g + 4, WINDOWS))


def gated_steps(nc, psum, keep, hT, params, adj):
    with ExitStack() as ctx:
        def sb(name, shape, dt):
            return ctx.enter_context(nc.sbuf_tensor(name, shape, dt))

        def sem(name):
            return ctx.enter_context(nc.semaphore(name))

        parts = sb("parts", [P, WINDOWS, 2, P], F16)
        scaled_m = sb("scaled_m", [P, 2, CHUNK], F32)
        agg = sb("agg", [P, 2, CHUNK], F32)
        r = sb("r", [P, CHUNK], F32)
        z = sb("z", [P, CHUNK], F32)
        n = sb("n", [P, CHUNK], F32)
        b_rz = sb("b_rz", [P, 2], F32)
        largest = sb("largest", [P, 3], F32)
        of_all = sb("of_all", [3, 1], F32)
        spread3 = sb("spread3", [3, 3], F32)
        limits = sb("limits", [P, 3], F32)
        scales = sb("scales", [P, 2], F32)
        w_msg, w_ih, w_hh, b_rep, b_i, b_h = (
            params[k] for k in ("w_msg", "w_ih", "w_hh", "b_rep", "b_i", "b_h"))

        setup = sem("l0_setup")
        limit = sem("limit")
        messages = sem("messages")
        scaled = sem("scaled")
        high = sem("high")
        low = sem("low")
        summed = sem("summed")
        agg_out = sem("agg_out")
        gates = sem("gates")
        r_on = sem("r_on")
        z_on = sem("z_on")
        n_pre = sem("n_pre")
        n_on = sem("n_on")
        h_new = sem("h_new")
        inner = sem("l0_inner")

        M_BANKS, AGG_BANK = (0, 1, 2), 3
        R_BANK, Z_BANK, IN_BANK, HN_BANK = 4, 5, 6, 7
        AHEAD = len(M_BANKS)
        EARLY = 5
        EXPONENT, TOP, TWICE = 0x7F800000, float((127 + 127 + 14) << 23), float((127 + 127) << 23)
        at = {}

        block = ctx.enter_context(nc.Block())

        @block.vector
        def _(dve):
            m = Marks(setup)

            def after(ins):
                dve.wait_ge(setup, m.on(ins))

            m.on(nc.vector.memset(hT[:, NODES:PADDED], 0.0))
            m.on(nc.vector.tensor_tensor(b_rz[:], b_i[:, 0:2], b_h[:, 0:2], ALU.add))
            for i, of in enumerate((hT[:, 0:NODES], w_msg[:], b_rep[:])):
                at["largest"] = m.on(nc.vector.tensor_reduce(largest[:, i:i + 1], of, AXIS_X, ALU.max,
                                                             apply_absolute_value=True))
            dve.wait_ge(limit, 1)
            after(nc.vector.tensor_reduce(of_all[:], psum[0:3, R_BANK, 0:P], AXIS_X, ALU.max))
            at["spread3"] = m.on(nc.vector.tensor_scalar(spread3[:], keep["ident"][0:3, 0:3], of_all[:, 0:1],
                                                         None, ALU.mult))
            dve.wait_ge(limit, 2)
            after(nc.vector.tensor_copy(limits[:], psum[:, Z_BANK, 0:3]))
            after(nc.vector.tensor_scalar(limits[:, 0:1], limits[:, 0:1], 1.0, float(D), ALU.max, ALU.mult))
            after(nc.vector.scalar_tensor_tensor(out=limits[:, 0:1], in0=limits[:, 0:1],
                                                 scalar=limits[:, 1:2], in1=limits[:, 2:3],
                                                 op0=ALU.mult, op1=ALU.add))
            after(nc.vector.tensor_scalar(limits[:, 0:1], limits[:, 0:1], 1e-30, None, ALU.max))
            bits = scales[:].bitcast(I32)
            after(nc.vector.tensor_scalar(bits[:, 1:2], limits[:, 0:1].bitcast(I32), EXPONENT, None,
                                          ALU.bitwise_and))
            after(nc.vector.tensor_scalar(bits[:, 0:1], bits[:, 1:2], -1.0, TOP, ALU.mult, ALU.add))
            after(nc.vector.tensor_scalar(bits[:, 1:2], bits[:, 0:1], -1.0, TWICE, ALU.mult, ALU.add))
            after(nc.vector.tensor_scalar(b_rep[:], b_rep[:], scales[:, 0:1], None, ALU.mult))
            at["scales"] = m.n
            dve.sem_inc(h_new, CHUNKS)

            def scale(s, g):
                k = len(group_tiles(g))
                dve.wait_ge(messages, s * CHUNKS + g + 1)
                nc.vector.scalar_tensor_tensor(
                    out=scaled_m[:, g % 2, 0:k * P].rearrange("p (t d) -> p t d", d=P),
                    in0=psum[:, M_BANKS[g % AHEAD], 0:k * P].rearrange("p (t d) -> p t d", d=P),
                    scalar=scales[:, 0:1], in1=b_rep[:].unsqueeze(1).broadcast_to([P, k, D]),
                    op0=ALU.mult, op1=ALU.add).then_inc(scaled, 1)

            def split(s, g):
                k = len(group_tiles(g))
                dve.wait_ge(high, s * CHUNKS + g + 1)
                nc.vector.tensor_tensor(parts[:, 4 * g:4 * g + k, 1, :],
                                        scaled_m[:, g % 2, 0:k * P].rearrange("p (t d) -> p t d", d=P),
                                        parts[:, 4 * g:4 * g + k, 0, :], ALU.subtract).then_inc(low, 1)

            def split_groups(s, groups):
                if groups[0] or not isinstance(s, int):
                    dve.wait_ge(low, s * CHUNKS + groups[0])
                scale(s, groups[0])
                for g in groups[1:]:
                    if g >= 2:
                        dve.wait_ge(low, s * CHUNKS + g - 1)
                    scale(s, g)
                    split(s, g - 1)
                split(s, groups[-1])

            def gate(at, cols, n_cols):
                h_c = hT[:, cols]
                first = at * 3 - 3
                dve.wait_ge(r_on, at)
                nc.vector.scalar_tensor_tensor(
                    out=n[:, 0:n_cols], in0=psum[:, HN_BANK, 0:n_cols], scalar=b_h[:, 2:3],
                    in1=r[:, 0:n_cols], op0=ALU.add, op1=ALU.mult).then_inc(inner, 1)
                dve.wait_ge(inner, first + 1)
                nc.vector.tensor_tensor(n[:, 0:n_cols], psum[:, IN_BANK, 0:n_cols], n[:, 0:n_cols],
                                        ALU.add).then_inc(n_pre, 1)
                dve.wait_ge(n_on, at)
                nc.vector.tensor_tensor(r[:, 0:n_cols], h_c, n[:, 0:n_cols],
                                        ALU.subtract).then_inc(inner, 1)
                dve.wait_ge(inner, first + 2)
                dve.wait_ge(z_on, at)
                nc.vector.tensor_tensor(r[:, 0:n_cols], r[:, 0:n_cols], z[:, 0:n_cols],
                                        ALU.mult).then_inc(inner, 1)
                dve.wait_ge(inner, first + 3)
                nc.vector.tensor_tensor(h_c, r[:, 0:n_cols], n[:, 0:n_cols],
                                        ALU.add).then_inc(h_new, 1)
                dve.wait_ge(h_new, at + CHUNKS)

            def step(s, last):
                first = s * CHUNKS
                split_groups(s, range(EARLY, CHUNKS))
                with dve.Fori(0, CHUNKS - 2) as c:
                    gate(first + c + 1, bass.ds(c * CHUNK, CHUNK), CHUNK)
                if not last:
                    split_groups(s + 1, range(AHEAD))
                c = CHUNKS - 1
                gate(first + c, slice((c - 1) * CHUNK, c * CHUNK), CHUNK)
                if not last:
                    split_groups(s + 1, range(AHEAD, EARLY))
                gate(first + c + 1, slice(c * CHUNK, NODES), chunk_width(c))

            split_groups(0, range(EARLY))
            with dve.Fori(0, GRU_STEPS - 1) as s:
                step(s, last=False)
            step(GRU_STEPS - 1, last=True)

        @block.tensor
        def _(pe):
            def make_messages(s, g):
                pe.wait_ge(h_new, s * CHUNKS + g + 1)
                if g >= AHEAD:
                    pe.wait_ge(scaled, s * CHUNKS + g - AHEAD + 1)
                for i, t in enumerate(group_tiles(g)):
                    mm = nc.tensor.matmul(psum[:, M_BANKS[g % AHEAD], i * P:(i + 1) * P],
                                          hT[:, t * P:(t + 1) * P], w_msg[:], start=True, stop=True)
                mm.then_inc(messages, 1)

            def sum_over(cols, n_cols, windows):
                for w in windows:
                    for part in range(2):
                        mm = nc.tensor.matmul(psum[:, AGG_BANK, 0:n_cols], parts[:, w, part, :],
                                              adj[:, w, cols], start=(w == 0 and part == 0),
                                              stop=(w == WINDOWS - 1 and part == 1))
                return mm

            def sum_chunk(at, cols, n_cols):
                pe.wait_ge(agg_out, at - 1)
                sum_over(cols, n_cols, range(WINDOWS)).then_inc(summed, 1)

            def gate_products(at, slot, cols, n_cols):
                pe.wait_ge(h_new, at + CHUNKS - 1)
                for bank, g, alone in ((R_BANK, 0, False), (Z_BANK, 1, False), (HN_BANK, 2, True)):
                    nc.tensor.matmul(psum[:, bank, 0:n_cols], w_hh[:, g * D:(g + 1) * D], hT[:, cols],
                                     start=True, stop=alone)
                pe.wait_ge(agg_out, at)
                for bank, g, alone in ((R_BANK, 0, False), (Z_BANK, 1, False), (IN_BANK, 2, True)):
                    mm = nc.tensor.matmul(psum[:, bank, 0:n_cols], w_ih[:, g * D:(g + 1) * D],
                                          agg[:, slot, 0:n_cols], start=alone, stop=True)
                mm.then_inc(gates, 1)

            pe.wait_ge(setup, at["largest"])
            nc.tensor.transpose(psum[0:3, R_BANK, 0:P], largest[:], keep["ident"][:]).then_inc(limit, 1)
            pe.wait_ge(setup, at["spread3"])
            nc.tensor.matmul(psum[:, Z_BANK, 0:3], keep["ones"][0:3, :], spread3[:],
                             start=True, stop=True).then_inc(limit, 1)

            def sum_groups(s, groups, to_make):
                for g in groups:
                    pe.wait_ge(low, s * CHUNKS + g + 1)
                    mm = sum_over(slice(0, CHUNK), CHUNK, group_tiles(g))
                    if g + AHEAD in to_make:
                        make_messages(s, g + AHEAD)
                return mm

            def start_step(s):
                for g in range(AHEAD):
                    make_messages(s, g)

            def step(s, last):
                first = s * CHUNKS
                make_messages(s, EARLY)
                sum_groups(s, range(AHEAD, CHUNKS), range(EARLY + 1, CHUNKS)).then_inc(summed, 1)
                with pe.Fori(0, (CHUNKS - 3) // 2) as c2:
                    for k in range(2):
                        sum_chunk(first + (c2 * 2 + k + 2), bass.ds((c2 * 2 + k + 1) * CHUNK, CHUNK), CHUNK)
                        gate_products(first + (c2 * 2 + k + 1), k, bass.ds((c2 * 2 + k) * CHUNK, CHUNK), CHUNK)
                for c in range(CHUNKS - 2, CHUNKS):
                    sum_chunk(first + c + 1, slice(c * CHUNK, c * CHUNK + chunk_width(c)), chunk_width(c))
                    if c + 1 == CHUNKS and not last:
                        start_step(s + 1)
                    gate_products(first + c, (c - 1) % 2, slice((c - 1) * CHUNK, c * CHUNK), CHUNK)
                if not last:
                    pe.wait_ge(agg_out, first + CHUNKS)
                    sum_groups(s + 1, range(AHEAD), range(AHEAD, EARLY))
                gate_products(first + CHUNKS, (CHUNKS - 1) % 2, slice(c * CHUNK, NODES), chunk_width(c))

            start_step(0)
            sum_groups(0, range(AHEAD), range(AHEAD, EARLY))
            with pe.Fori(0, GRU_STEPS - 1) as s:
                step(s, last=False)
            step(GRU_STEPS - 1, last=True)

        @block.scalar
        def _(act):
            def split(s, g):
                k = len(group_tiles(g))
                act.wait_ge(scaled, s * CHUNKS + g + 1)
                nc.scalar.activation(parts[:, 4 * g:4 * g + k, 0, :],
                                     scaled_m[:, g % 2, 0:k * P].rearrange("p (t d) -> p t d", d=P),
                                     ACT.Copy).then_inc(high, 1)

            def take_sum(at, slot, n_cols):
                act.wait_ge(summed, at)
                nc.scalar.activation(agg[:, slot, 0:n_cols], psum[:, AGG_BANK, 0:n_cols],
                                     ACT.Copy, scale=scales[:, 1:2]).then_inc(agg_out, 1)

            def gate(at, n_cols):
                act.wait_ge(gates, at)
                act.wait_ge(h_new, at + CHUNKS - 1)
                nc.scalar.activation(r[:, 0:n_cols], psum[:, R_BANK, 0:n_cols], ACT.Sigmoid,
                                     bias=b_rz[:, 0:1]).then_inc(r_on, 1)
                nc.scalar.activation(z[:, 0:n_cols], psum[:, Z_BANK, 0:n_cols], ACT.Sigmoid,
                                     bias=b_rz[:, 1:2]).then_inc(z_on, 1)
                act.wait_ge(n_pre, at)
                nc.scalar.activation(n[:, 0:n_cols], n[:, 0:n_cols], ACT.Tanh,
                                     bias=b_i[:, 2:3]).then_inc(n_on, 1)

            nc.scalar.preload_act_table(ACT.Sigmoid)
            act.wait_ge(setup, at["scales"])
            def step(s, last):
                first = s * CHUNKS
                for g in range(EARLY, CHUNKS):
                    split(s, g)
                take_sum(first + 1, 0, CHUNK)
                with act.Fori(0, (CHUNKS - 3) // 2) as c2:
                    for k in range(2):
                        take_sum(first + (c2 * 2 + k + 2), (k + 1) % 2, CHUNK)
                        gate(first + (c2 * 2 + k + 1), CHUNK)
                c = CHUNKS - 2
                take_sum(first + c + 1, c % 2, CHUNK)
                gate(first + c, CHUNK)
                take_sum(first + CHUNKS, (CHUNKS - 1) % 2, chunk_width(CHUNKS - 1))
                if not last:
                    for g in range(AHEAD):
                        split(s + 1, g)
                gate(first + CHUNKS - 1, CHUNK)
                if not last:
                    for g in range(AHEAD, EARLY):
                        split(s + 1, g)
                gate(first + CHUNKS, chunk_width(CHUNKS - 1))

            for g in range(EARLY):
                split(0, g)
            with act.Fori(0, GRU_STEPS - 1) as s:
                step(s, last=False)
            step(GRU_STEPS - 1, last=True)


def add_and_norm(nc, tag, base, result, psum, keep, hT, turn_back):
    with ExitStack() as ctx:
        def sb(name, shape, dt):
            return ctx.enter_context(nc.sbuf_tensor(name + tag, shape, dt))

        def sem(name):
            return ctx.enter_context(nc.semaphore(name + tag))

        v = sb("v", [P, WINDOWS, D], F32)
        stats = sb("stats", [P, WINDOWS, 6], F32)
        moments = sb("moments", [P, WINDOWS, 2], F32)
        spread = sb("spread", [P, WINDOWS], F32)
        base_in = sem("base_in")
        cleared = sem("cleared")
        turned = sem("turned_n")
        vec = sem("vec_n")
        rooted = sem("rooted")
        scaled = sem("scaled")
        back = sem("back")
        back_out = sem("back_out")
        stored = sem("stored")
        full = WINDOWS - 1
        at = {}

        block = ctx.enter_context(nc.Block())

        @block.sync
        def _(sp):
            sp.dma_start(v[:, 0:full, :],
                         base[0:full * P, :].rearrange("(t p) d -> p t d", p=P)).then_inc(base_in, 16)
            sp.wait_ge(cleared, 1)
            sp.dma_start(v[0:LAST, full, :], base[full * P:NODES, :]).then_inc(base_in, 16)
            sp.wait_ge(scaled, WINDOWS)
            sp.dma_start(result[0:full * P, :].rearrange("(t p) d -> p t d", p=P),
                         v[:, 0:full, :]).then_inc(stored, 16)
            sp.dma_start(result[full * P:NODES, :], v[0:LAST, full, :]).then_inc(stored, 16)
            sp.wait_ge(stored, 32)

        @block.tensor
        def _(pe):
            for g in range(CHUNKS):
                for i, t in enumerate(group_tiles(g)):
                    mm = nc.tensor.transpose(psum[:, g, i * P:(i + 1) * P], hT[:, t * P:(t + 1) * P],
                                             keep["ident"][:])
                mm.then_inc(turned, 1)
            if turn_back:
                for g in range(CHUNKS):
                    pe.wait_ge(scaled, group_tiles(g)[-1] + 1)
                    for i, t in enumerate(group_tiles(g)):
                        mm = nc.tensor.transpose(psum[:, g, i * P:(i + 1) * P], v[:, t, :],
                                                 keep["ident"][:])
                    mm.then_inc(back, 1)

        @block.vector
        def _(dve):
            m = Marks(vec)
            nc.vector.memset(v[:, full, :], 0.0).then_inc(cleared, 1)
            dve.wait_ge(base_in, 32)
            for g in range(CHUNKS):
                k = len(group_tiles(g))
                v_g = v[:, 4 * g:4 * g + k, :]
                dve.wait_ge(turned, g + 1)
                dve.wait_ge(vec, m.on(nc.vector.tensor_tensor(
                    v_g, psum[:, g, 0:k * P].rearrange("p (t d) -> p t d", d=D), v_g, ALU.add)))
                for t in group_tiles(g):
                    m.on(nc.vector.bn_stats(stats[:, t, :], v[:, t, :]))
            dve.wait_ge(vec, m.n)
            for t in range(WINDOWS):
                m.on(nc.vector.bn_aggr(moments[:, t, :], stats[:, t, :]))
            dve.wait_ge(vec, m.n)
            at["spread"] = m.on(nc.vector.tensor_scalar(spread[:], moments[:, :, 1], EPS, None, ALU.add))
            dve.wait_ge(rooted, 1)
            dve.wait_ge(vec, m.on(nc.vector.reciprocal(spread[:], spread[:])))
            for t in range(WINDOWS):
                nc.vector.tensor_scalar(v[:, t, :], v[:, t, :], moments[:, t, 0:1], spread[:, t:t + 1],
                                        ALU.subtract, ALU.mult).then_inc(scaled, 1)

        @block.scalar
        def _(act):
            act.wait_ge(vec, at["spread"])
            nc.scalar.activation(spread[:], spread[:], ACT.Sqrt).then_inc(rooted, 1)
            if turn_back:
                for g in range(CHUNKS):
                    n = chunk_width(g)
                    act.wait_ge(back, g + 1)
                    nc.scalar.activation(hT[:, g * CHUNK:g * CHUNK + n], psum[:, g, 0:n],
                                         ACT.Copy).then_inc(back_out, 1)




def edge_layers(nc, weights, psum, keep, hT, dst_rows, tables, debug):
    with ExitStack() as ctx:
        def sb(name, shape, dt):
            return ctx.enter_context(nc.sbuf_tensor(name, shape, dt))

        t = {
            "q_parts": sb("q_parts", [P, WINDOWS, 3, D], BF16),
            "agg_t": sb("agg_t", [P, PADDED], F32),
            "dst_loc": sb("dst_loc_e", [P, STEPS], F32),
            "weight": sb("weight_e", [P, STEPS], F32),
            "src_i": sb("src_i", [P, STEPS + SLOTS * GROUP], I32),
        }
        p_dram = nc.dram_tensor("p_dram", (NODES, D), F32, kind="Internal").ap()
        e_dram = [nc.dram_tensor(f"e{i}_dram", (GROUPS, P, CHUNK), F32, kind="Internal").ap()
                  for i in range(2)]
        for l, (We, be, Wn, bn) in enumerate(weights):
            clear_semaphores(nc)
            node_products(nc, l, We, be, psum, keep, hT, tables, t, p_dram)
            edge_pass(nc, f"_{l}", We[2 * D:3 * D, :] if l else None, psum, keep, t, dst_rows, p_dram,
                      e_dram[l - 1] if l else None, e_dram[l] if l < 2 else None)
            node_update(nc, f"_{l}", Wn, bn, psum, hT, t)
            if debug:
                debug(f"l{l}", nc, {"hT": hT, "agg": t["agg_t"]})


def node_products(nc, l, We, be, psum, keep, hT, tables, t, p_dram):
    tag = f"_{l}"
    with ExitStack() as ctx:
        def sb(name, shape, dt):
            return ctx.enter_context(nc.sbuf_tensor(name + tag, shape, dt))

        def sem(name):
            return ctx.enter_context(nc.semaphore(name + tag))

        w_ab = sb("w_ab", [P, 2 * D], F32)
        b_rep = sb("b_rep", [P, D], F32)
        p_sb = sb("p_sb", [P, WINDOWS, D], F32)
        residue = sb("residue_q", [P, 2, 2, D], F32)
        src_f = sb("src_f_e", [P, STEPS], F32) if l == 0 else None
        loads = sem("w_loads")
        b_in = sem("b_in")
        product = sem("product")
        p_out = sem("p_out")
        high, mid, resid, low = sem("q_high"), sem("q_mid"), sem("q_resid"), sem("q_low")
        stored = sem("p_stored")
        tabs = sem("tabs_in")
        made = sem("made")
        pairs = [range(a, min(a + 2, WINDOWS)) for a in range(0, WINDOWS, 2)]
        N = len(pairs)
        q_parts = t["q_parts"]

        def bank(i, half):
            k = len(pairs[i])
            return psum[:, i % 8, 0:k * 2 * D].rearrange("p (k h d) -> p k h d", k=k, h=2)[:, :, half, :]

        block = ctx.enter_context(nc.Block())

        @block.sync
        def _(sp):
            sp.dma_start(w_ab[:, 0:D], We[0:D, :]).then_inc(loads, 16)
            sp.dma_start(w_ab[:, D:2 * D], We[D:2 * D, :]).then_inc(loads, 16)
            sp.dma_start(b_rep[:], be.rearrange("(a n) -> a n", a=1).broadcast_to([P, D])).then_inc(b_in, 16)
            if l == 0:
                for i, to in enumerate((src_f, t["dst_loc"], t["weight"])):
                    sp.dma_start(to[:], tables[i]).then_inc(tabs, 16)
            for i in (3, 6, 9, N - 2):
                a = {3: 0, 6: 4, 9: 7, N - 2: 10}[i] * 2
                b = (i + 1) * 2
                sp.wait_ge(p_out, i + 1)
                sp.dma_start(p_dram[a * P:b * P, :].rearrange("(t p) d -> p t d", p=P),
                             p_sb[:, a:b, :]).then_inc(stored, 16)
            sp.wait_ge(p_out, N)
            sp.dma_start(p_dram[(WINDOWS - 1) * P:NODES, :], p_sb[0:LAST, WINDOWS - 1, :]).then_inc(stored, 16)
            sp.wait_ge(stored, 80)

        @block.gpsimd
        def _(pool):
            nc.gpsimd.memset(t["agg_t"][:], 0.0).then_inc(made, 1)
            if l == 0:
                nc.gpsimd.memset(t["src_i"][:, STEPS:], 0).then_inc(made, 1)
                pool.wait_ge(tabs, 48)
                nc.gpsimd.tensor_copy(t["src_i"][:, 0:STEPS], src_f[:]).then_inc(made, 1)

        @block.tensor
        def _(pe):
            pe.wait_ge(loads, 32)
            for i, pair in enumerate(pairs):
                if i >= 8:
                    pe.wait_ge(p_out, i - 7)
                    pe.wait_ge(resid, i - 7)
                for k, w in enumerate(pair):
                    mm = nc.tensor.matmul(psum[:, i % 8, k * 2 * D:(k + 1) * 2 * D],
                                          hT[:, w * P:(w + 1) * P], w_ab[:], start=True, stop=True)
                mm.then_inc(product, 1)

        @block.scalar
        def _(act):
            def second_part(i):
                a, k = pairs[i][0], len(pairs[i])
                act.wait_ge(resid, i + 1)
                nc.scalar.activation(q_parts[:, a:a + k, 1, :], residue[:, i % 2, 0:k, :],
                                     ACT.Copy).then_inc(mid, 1)

            for i, pair in enumerate(pairs):
                a, k = pair[0], len(pair)
                act.wait_ge(product, i + 1)
                nc.scalar.activation(q_parts[:, a:a + k, 0, :], bank(i, 1), ACT.Copy).then_inc(high, 1)
                if i >= 1:
                    second_part(i - 1)
            second_part(N - 1)

        @block.vector
        def _(dve):
            def third_part(i):
                a, k = pairs[i][0], len(pairs[i])
                dve.wait_ge(mid, i + 1)
                nc.vector.tensor_tensor(q_parts[:, a:a + k, 2, :], residue[:, i % 2, 0:k, :],
                                        q_parts[:, a:a + k, 1, :], ALU.subtract).then_inc(low, 1)

            dve.wait_ge(b_in, 16)
            for i, pair in enumerate(pairs):
                a, k = pair[0], len(pair)
                dve.wait_ge(high, i + 1)
                if i >= 2:
                    dve.wait_ge(low, i - 1)
                nc.vector.tensor_tensor(residue[:, i % 2, 0:k, :], bank(i, 1), q_parts[:, a:a + k, 0, :],
                                        ALU.subtract).then_inc(resid, 1)
                nc.vector.tensor_tensor(p_sb[:, a:a + k, :], bank(i, 0),
                                        b_rep[:].unsqueeze(1).broadcast_to([P, k, D]),
                                        ALU.add).then_inc(p_out, 1)
                if i >= 1:
                    third_part(i - 1)
            third_part(N - 1)


def edge_pass(nc, tag, Wc, psum, keep, t, dst_rows, p_dram, e_before, e_after):
    with ExitStack() as ctx:
        def sb(name, shape, dt):
            return ctx.enter_context(nc.sbuf_tensor(name + tag, shape, dt))

        def sem(name):
            return ctx.enter_context(nc.semaphore(name + tag))

        w_c = sb("w_c", [P, D], F32)
        ids = sb("ids", [P, SLOTS, GROUP], I32)
        p_rows = sb("p_rows", [P, SLOTS, CHUNK], F32)
        before = sb("before", [P, SLOTS, CHUNK], F32)
        locals_ = sb("locals", [P, SLOTS, CHUNK], BF16)
        hot_t = sb("hot_t", [P, 2, CHUNK], BF16)
        pre = sb("pre", [P, 2, CHUNK], F32)
        e = sb("e", [P, 2, CHUNK], F32)
        after = sb("after", [P, SLOTS, CHUNK], F32)
        hot_w = sb("hot_w", [P, 2, GROUP, P], F32)

        w_in = sem("w_in")
        ids_on = sem("ids_on")
        gathering = sem("gathering")
        rows_in = [sem(f"rows{j}") for j in range(SLOTS)]
        before_in = [sem(f"before{j}") for j in range(SLOTS)]
        locals_in = [sem(f"locals{j}") for j in range(SLOTS)]
        stored = [sem(f"stored{j}") for j in range(SLOTS)]
        all_stored = sem("all_stored")
        hot_t_on = sem("hot_t_on")
        spread = sem("spread")
        added = sem("added")
        hot_on = sem("hot_on")
        e_on = sem("e_on")
        e_turned = sem("e_turned")
        after_on = sem("after_on")
        summed = sem("summed_e")
        agg_on = sem("agg_on")

        E_BANKS, T_BANKS, A_BANKS = (0, 1), (2, 3), (4, 5)

        def rounds(engine):
            return nc.values_load(keep["rounds_i"][0:1, 0:1], engines=(engine,),
                                  min_val=MIN_ROUNDS, max_val=MAX_ROUNDS)

        def windows_of(i, engine):
            _, windows = nc.values_load_multi_w_load_instructions(
                keep["win_i"][0:1, bass.ds(i * SLOTS, SLOTS)], engines=(engine,),
                min_val=0, max_val=WINDOWS - 1)
            return windows

        block = ctx.enter_context(nc.Block())

        @block.gpsimd
        def _(pool):
            with pool.Fori(0, rounds(mybir.EngineType.Pool)) as i:
                for j in range(SLOTS):
                    pool.wait_ge(ids_on, i * SLOTS + j + 1)
                    pool.sem_inc(gathering, 1)
                    for m in range(GROUP):
                        nc.gpsimd.indirect_dma_start(
                            out=p_rows[:, j, m * D:(m + 1) * D], out_offset=None, in_=p_dram,
                            in_offset=bass.IndirectOffsetOnAxis(ap=ids[:, j, m:m + 1].bitcast(U32), axis=0),
                        ).then_inc(rows_in[j], 16)

        @block.sync
        def _(sp):
            if e_before is not None:
                sp.dma_start(w_c[:], Wc).then_inc(w_in, 16)

            def load_locals(g, j):
                sp.dma_start(locals_[:, j, :], dst_rows[bass.ds(g * CHUNK, CHUNK)]
                             .rearrange("(a n) -> a n", a=1).broadcast_to([P, CHUNK])
                             ).then_inc(locals_in[j], 16)

            def load_before(g, j):
                sp.dma_start(before[:, j, :], e_before[bass.ds(g, 1), :, :]
                             .rearrange("a p n -> (a p) n")).then_inc(before_in[j], 16)

            def store(i, j):
                sp.wait_ge(after_on, i * SLOTS + j + 3)
                sp.dma_start(e_after[bass.ds(i * SLOTS + j, 1), :, :].rearrange("a p n -> (a p) n"),
                             after[:, j, :]).then_inc(stored[j], 16)

            for j in range(SLOTS):
                load_locals(j, j)
                if e_before is not None:
                    load_before(j, j)
            last = nc.values_load(keep["rounds_i"][0:1, 1:2], engines=(mybir.EngineType.SP,),
                                  min_val=MIN_ROUNDS - 1, max_val=MAX_ROUNDS - 1)
            with sp.Fori(0, last) as i:
                for j in range(SLOTS):
                    sp.wait_ge(hot_t_on, i * SLOTS + j + 1)
                    load_locals((i + 1) * SLOTS + j, j)
                    if e_before is not None:
                        sp.wait_ge(spread, i * SLOTS + j + 1)
                        load_before((i + 1) * SLOTS + j, j)
                    if e_after is not None:
                        store(i, j)
            sp.wait_ge(hot_t_on, last * SLOTS + 1)
            load_locals((last + 1) * SLOTS, 0)
            if e_after is not None:
                for j in range(SLOTS):
                    store(last, j)
                for j in range(SLOTS):
                    sp.wait_ge(stored[j], last * 16 + 32)
                    sp.sem_inc(all_stored, 1)

        @block.tensor
        def _(pe):
            pe.sem_inc(summed, 2)
            if e_before is not None:
                pe.wait_ge(w_in, 16)

            def products(i, j, windows):
                if j >= 2:
                    pe.wait_ge(added, i * SLOTS + j - 1)
                pe.wait_ge(hot_t_on, i * SLOTS + j + 1)
                if e_before is not None:
                    pe.wait_ge(before_in[j], i * 16 + 16)
                for m in range(GROUP):
                    o = psum[:, E_BANKS[j % 2], m * D:(m + 1) * D]
                    for part in range(3):
                        mm = nc.tensor.matmul(o, hot_t[:, j % 2, m * P:(m + 1) * P],
                                              t["q_parts"][:, bass.ds(windows[j], 1), part, :],
                                              start=(part == 0), stop=(part == 2 and e_before is None))
                    if e_before is not None:
                        mm = nc.tensor.matmul(o, before[:, j, m * P:(m + 1) * P], w_c[:],
                                              start=False, stop=True)
                mm.then_inc(spread, 1)

            def turn_and_sum(i, j):
                pe.wait_ge(e_on, i * SLOTS + j + 3)
                if e_after is not None:
                    pe.wait_ge(after_on, i * SLOTS + j + 1)
                    for m in range(GROUP):
                        mm = nc.tensor.transpose(psum[:, T_BANKS[j % 2], m * P:(m + 1) * P],
                                                 e[:, j % 2, m * D:(m + 1) * D], keep["ident"][:])
                    mm.then_inc(e_turned, 1)
                pe.wait_ge(hot_on, i * (SLOTS * GROUP) + (j + 1) * GROUP)
                pe.wait_ge(agg_on, i * SLOTS + j + 1)
                for m in range(GROUP):
                    mm = nc.tensor.matmul(psum[:, A_BANKS[j % 2], 0:P],
                                          e[:, j % 2, m * D:(m + 1) * D], hot_w[:, j % 2, m, :],
                                          start=(m == 0), stop=(m == GROUP - 1))
                mm.then_inc(summed, 1)

            with pe.Fori(0, rounds(mybir.EngineType.PE)) as i:
                windows = windows_of(i, mybir.EngineType.PE)
                products(i, 0, windows)
                for j in range(1, SLOTS):
                    products(i, j, windows)
                    turn_and_sum(i, j - 1)
                turn_and_sum(i, SLOTS - 1)

        @block.scalar
        def _(act):
            act.sem_inc(e_on, 2)
            act.sem_inc(after_on, 2)
            for j in range(SLOTS):
                act.sem_inc(stored[j], 16)

            def relu(i, j):
                act.wait_ge(added, i * SLOTS + j + 1)
                act.wait_ge(summed, i * SLOTS + j + 1)
                nc.scalar.activation(e[:, j % 2, :], pre[:, j % 2, :], ACT.Relu).then_inc(e_on, 1)

            def take(i, j):
                if e_after is not None:
                    act.wait_ge(e_turned, i * SLOTS + j + 1)
                    act.wait_ge(stored[j], i * 16 + 16)
                    nc.scalar.activation(after[:, j, :], psum[:, T_BANKS[j % 2], :],
                                         ACT.Copy).then_inc(after_on, 1)

            nc.scalar.preload_act_table(ACT.Relu)
            with act.Fori(0, rounds(mybir.EngineType.Activation)) as i:
                relu(i, 0)
                for j in range(1, SLOTS):
                    relu(i, j)
                    take(i, j - 1)
                take(i, SLOTS - 1)

        @block.vector
        def _(dve):
            dve.sem_inc(agg_on, 2)
            nc.vector.tensor_copy(ids[:], t["src_i"][:, 0:SLOTS * GROUP]
                                  .rearrange("p (j m) -> p j m", m=GROUP)).then_inc(ids_on, 1)
            dve.wait_ge(ids_on, 1)
            dve.sem_inc(ids_on, SLOTS - 1)

            def turned_hot(i, j):
                dve.wait_ge(locals_in[j], i * 16 + 16)
                nc.vector.tensor_scalar(hot_t[:, j % 2, :], locals_[:, j, :], keep["lane_f"][:, 0:1],
                                        None, ALU.is_equal).then_inc(hot_t_on, 1)

            def hots(i, j):
                for m in range(GROUP):
                    k = i * (SLOTS * GROUP) + (j * GROUP + m)
                    nc.vector.tensor_scalar(hot_w[:, j % 2, m, :], keep["col_f"][:],
                                            t["dst_loc"][:, bass.ds(k, 1)],
                                            t["weight"][:, bass.ds(k, 1)],
                                            ALU.is_equal, ALU.mult).then_inc(hot_on, 1)

            def add(i, j):
                dve.wait_ge(spread, i * SLOTS + j + 1)
                dve.wait_ge(rows_in[j], i * (16 * GROUP) + 16 * GROUP)
                dve.wait_ge(e_on, i * SLOTS + j + 1)
                nc.vector.tensor_tensor(pre[:, j % 2, :], psum[:, E_BANKS[j % 2], :], p_rows[:, j, :],
                                        ALU.add).then_inc(added, 1)
                dve.wait_ge(added, i * SLOTS + j + 1)
                nc.vector.tensor_copy(ids[:, j, :],
                                      t["src_i"][:, bass.ds(i * (SLOTS * GROUP) + (SLOTS + j) * GROUP, GROUP)]
                                      ).then_inc(ids_on, 1)

            def gather_up(i, j, windows):
                dve.wait_ge(summed, i * SLOTS + j + 3)
                dve.wait_ge(agg_on, i * SLOTS + j + 2)
                a = t["agg_t"][:, bass.ds(windows[j] * P, P)]
                nc.vector.tensor_tensor(a, psum[:, A_BANKS[j % 2], 0:P], a, ALU.add).then_inc(agg_on, 1)

            turned_hot(0, 0)
            with dve.Fori(0, rounds(mybir.EngineType.DVE)) as i:
                windows = windows_of(i, mybir.EngineType.DVE)
                for j in range(SLOTS):
                    hots(i, j)
                    add(i, j)
                    if j + 1 < SLOTS:
                        turned_hot(i, j + 1)
                    else:
                        turned_hot(i + 1, 0)
                    if j:
                        gather_up(i, j - 1, windows)
                gather_up(i, SLOTS - 1, windows)


def node_update(nc, tag, Wn, bn, psum, hT, t):
    with ExitStack() as ctx:
        def sb(name, shape, dt):
            return ctx.enter_context(nc.sbuf_tensor(name + tag, shape, dt))

        def sem(name):
            return ctx.enter_context(nc.semaphore(name + tag))

        w_n = sb("w_n", [P, 2, D], F32)
        b_n = sb("b_n", [P, 1], F32)
        loads = sem("wn_loads")
        product = sem("wn_product")
        x_on = sem("x_on")
        block = ctx.enter_context(nc.Block())

        @block.sync
        def _(sp):
            sp.dma_start(w_n[:], Wn.rearrange("(h p) d -> p h d", p=P)).then_inc(loads, 16)
            sp.dma_start(b_n[:], bn.rearrange("(p a) -> p a", a=1)).then_inc(loads, 16)

        @block.tensor
        def _(pe):
            pe.wait_ge(loads, 32)
            for c in range(CHUNKS):
                n = chunk_width(c)
                nc.tensor.matmul(psum[:, c, 0:n], w_n[:, 0, :], hT[:, c * CHUNK:c * CHUNK + n],
                                 start=True, stop=False)
                nc.tensor.matmul(psum[:, c, 0:n], w_n[:, 1, :], t["agg_t"][:, c * CHUNK:c * CHUNK + n],
                                 start=False, stop=True).then_inc(product, 1)

        @block.scalar
        def _(act):
            act.wait_ge(loads, 32)
            for c in range(CHUNKS):
                n = chunk_width(c)
                act.wait_ge(product, c + 1)
                nc.scalar.activation(hT[:, c * CHUNK:c * CHUNK + n], psum[:, c, 0:n], ACT.Relu,
                                     bias=b_n[:, 0:1]).then_inc(x_on, 1)


_INS = ["x", "src", "dst", "edge_weight", "L0_gnn_W_msg", "L0_gnn_b_msg", "L0_gnn_W_ih", "L0_gnn_W_hh",
        "L0_gnn_b_ih", "L0_gnn_b_hh", "L1_gnn_We0", "L1_gnn_be0", "L1_gnn_Wn0", "L1_gnn_bn0",
        "L1_gnn_We1", "L1_gnn_be1", "L1_gnn_Wn1", "L1_gnn_bn1", "L1_gnn_We2", "L1_gnn_be2",
        "L1_gnn_Wn2", "L1_gnn_bn2"]
_TRANSPOSED = ("L0_gnn_W_msg", "L0_gnn_W_ih", "L0_gnn_W_hh")


def kernel(**inputs):
    import numpy as np
    from concourse import bacc
    from concourse.bass_utils import run_bass_kernel_spmd

    nc = bacc.Bacc("TRN2", target_bir_lowering=False, num_devices=1)
    laid = []
    for name in _INS:
        a = np.asarray(inputs[name])
        laid.append((name, np.ascontiguousarray(a.T if name in _TRANSPOSED else a)))
        if name == "x":
            laid.append(("xT", np.ascontiguousarray(a.T)))
    arrays, args = {}, []
    for name, a in laid:
        arrays[f"in_{name}"] = a
        args.append(nc.dram_tensor(f"in_{name}", a.shape, mybir.dt.from_np(a.dtype),
                                   kind="ExternalInput").ap())
    out = nc.dram_tensor("out", (NODES, D), F32, kind="ExternalOutput").ap()
    build(nc, *args, out)
    results = run_bass_kernel_spmd(nc, [arrays], core_ids=[0])
    return results.results[0]["out"]
```

```python
from contextlib import ExitStack

import concourse.bass as bass
from concourse import mybir

F32 = mybir.dt.float32
BF16 = mybir.dt.bfloat16
F16 = mybir.dt.float16
I32 = mybir.dt.int32
U32 = mybir.dt.uint32
ALU = mybir.AluOpType
ACT = mybir.ActivationFunctionType
AXIS_X = mybir.AxisListType.X

P = 128
NODES = 3125
EDGES = 50000
D = 128
GRU_STEPS = 5
EPS = 1e-5
WINDOWS = -(-NODES // P)
PADDED = WINDOWS * P
LAST = NODES - (WINDOWS - 1) * P
TILES = -(-EDGES // P)
EVAC_DVE = (1, 3, 5)
TCH = 4
GROUP = 2
SLOTS = 8
MAX_ROUNDS = -(-(TILES + WINDOWS - 1 + 3 * WINDOWS) // (GROUP * SLOTS))
GROUPS = MAX_ROUNDS * SLOTS
STEPS = GROUPS * GROUP
MOVED = 2 * GROUP
MIN_ROUNDS = TILES // (GROUP * SLOTS)
CHUNK = 512
CHUNKS = -(-NODES // CHUNK)
CENTER = NODES // 2
NO_NODE = 100000.0


class Marks:

    def __init__(self, sem, base=0):
        self.sem, self.base, self.n = sem, base, 0

    def on(self, ins):
        self.n += 1
        ins.then_inc(self.sem, 1)
        return self.base + self.n


def build(nc, x, xT, src, dst, edge_weight, W_msgT, b_msg, W_ihT, W_hhT, b_ih, b_hh,
          We0, be0, Wn0, bn0, We1, be1, Wn1, bn1, We2, be2, Wn2, bn2, out, debug=None):
    ctx = ExitStack()
    with ctx:
        psum = ctx.enter_context(nc.psum_tensor("psum", [P, 8, CHUNK], F32))

        def sb(name, shape, dt):
            return ctx.enter_context(nc.sbuf_tensor(name, shape, dt))

        keep = {
            "ident": sb("ident", [P, P], F32),
            "ones": sb("ones", [P, P], F32),
            "lane_f": sb("lane_f", [P, 1], F32),
            "col_f": sb("col_f", [P, P], F32),
            "pairs_i": sb("pairs_i", [1, WINDOWS, 2], I32),
            "win_i": sb("win_i", [1, GROUPS], I32),
            "rounds_i": sb("rounds_i", [1, 2], I32),
        }
        hT = sb("hT", [P, PADDED], F32)
        dst_rows = nc.dram_tensor("dst_rows", ((STEPS + MOVED) * P,), BF16, kind="Internal").ap()
        tables = nc.dram_tensor("tables", (3, P, STEPS), F32, kind="Internal").ap()

        with ExitStack() as l0:
            def l0_sb(name, shape, dt):
                return l0.enter_context(nc.sbuf_tensor(name, shape, dt))

            for name in ("src_f", "dst_loc", "weight"):
                keep[name] = l0_sb(name, [P, STEPS], F32)
            keep["node_room"] = l0_sb("node_h", [P, 3 * CHUNK * 2 + P], F16)
            keep["node_h"] = keep["node_room"][:, 0:NODES]
            keep["col_h"] = l0_sb("col_h", [P, P], F16)
            params = {name: l0_sb(name, shape, F32) for name, shape in (
                ("w_msg", [P, D]), ("w_ih", [P, 3 * D]), ("w_hh", [P, 3 * D]),
                ("b_rep", [P, D]), ("b_i", [P, 3]), ("b_h", [P, 3]),
                ("largest", [P, 3]))}
            tables_out = l0.enter_context(nc.semaphore("tables_out"))
            step_tables(nc, src, dst, edge_weight, (xT, W_msgT, b_msg, W_ihT, W_hhT, b_ih, b_hh),
                        psum, keep, hT, params, dst_rows, tables, tables_out)
            if debug:
                debug("tables", nc, keep)
            adj = l0_sb("adj", [P, WINDOWS, NODES], F16)
            build_adjacency(nc, psum, keep, adj, tables_out)
            if debug:
                debug("adj", nc, {"adj": adj})
            gated_steps(nc, psum, keep, hT, params, adj)
            if debug:
                debug("h5", nc, {"hT": hT})
        x1 = sb("x1", [P, WINDOWS, D], F32)
        add_and_norm(nc, "_0", x1, x, None, psum, keep, hT)
        if debug:
            debug("x1", nc, {"hT": hT})
        edge_layers(nc, ((We0, be0, Wn0, bn0), (We1, be1, Wn1, bn1), (We2, be2, Wn2, bn2)),
                    psum, keep, hT, dst_rows, tables, debug)
        add_and_norm(nc, "_1", x1, None, out, psum, keep, hT)


def clear_semaphores(nc):
    used = sorted(int(n) for n in nc.released_uncleared_semaphores)
    with nc.Block() as block:
        @block.sync
        def _(sp):
            start = 0
            for i in range(1, len(used) + 1):
                if i == len(used) or used[i] != used[i - 1] + 1:
                    sp.sem_clear(range(used[start], used[i - 1] + 1))
                    start = i


def step_tables(nc, src, dst, edge_weight, l0_inputs, psum, keep, hT, params, dst_rows, tables,
                tables_out):
    xT, W_msgT, b_msg, W_ihT, W_hhT, b_ih, b_hh = l0_inputs
    with ExitStack() as ctx:
        def sb(name, shape, dt):
            return ctx.enter_context(nc.sbuf_tensor(name, shape, dt))

        def sem(name):
            return ctx.enter_context(nc.semaphore(name))

        W = WINDOWS
        whole = EDGES // P
        rest = EDGES - whole * P
        q_full = whole // P
        q_rows = whole - q_full * P
        raw = {n: sb(f"raw_{n}", [P, TCH, P], dt) for n, dt in
               (("dst", I32), ("src", I32), ("weight", F32))}
        rows = {"dst": sb("rows_dst", [P, TCH, P], F32), "src": sb("rows_src", [P, TCH, P], F32),
                "weight": raw["weight"]}
        dst_h = sb("dst_h", [P, TCH * P], F16)
        counts = sb("counts", [P, W + 1], F32)
        step_f = sb("step_f", [P, STEPS], F32)
        lane_i = sb("lane_i", [P, 1], I32)
        tri = sb("tri", [P, P], F32)
        edge_i = sb("edge_i", [W, 2], I32)
        edge_f = sb("edge_f", [W, 2], F32)
        size_f = sb("size_f", [W, 1], F32)
        size_i = sb("size_i", [W, 1], I32)
        size_g = sb("size_g", [W, 1], F32)
        bounds = sb("bounds", [W, 5], F32)
        flags = sb("flags", [W, 2, STEPS], F32)
        names = sb("names", [W, 2, P], F32)
        totals_i = sb("totals_i", [1, 2], I32)
        tile_of = sb("tile_of", [P, STEPS], F32)
        lane_q = sb("lane_q", [P, TCH], F32)
        pick = sb("pick", [P, TCH, STEPS], F32)
        below = pick[:].rearrange("p q s -> p (q s)")[:, 0:TCH * P].bitcast(F16)[:, 0:TCH * P]
        step_i = pick[:, TCH - 1, :].bitcast(I32)
        dst_t = sb("dst_t", [P, TCH, P], BF16)

        edges_in = {n: sem(f"{n}_in") for n in raw}
        padded = sem("padded")
        iotas = sem("iotas")
        vec = sem("vec")
        small = sem("small")
        picked = sem("picked")
        turned = sem("turned")
        loads = sem("l0_loads")
        done = {}

        block = ctx.enter_context(nc.Block())

        @block.gpsimd
        def _(pool):
            nc.gpsimd.memset(raw["dst"][:, TCH - 1, :], int(NO_NODE)).then_inc(padded, 1)
            nc.gpsimd.memset(raw["src"][:, TCH - 1, :], 0).then_inc(padded, 1)
            nc.gpsimd.memset(raw["weight"][:, TCH - 1, :], 0.0).then_inc(padded, 1)
            nc.gpsimd.iota(step_i, [[1, STEPS]], 0, 0).then_inc(iotas, 1)
            nc.gpsimd.iota(lane_i[:], [[0, 1]], 0, 1).then_inc(iotas, 1)
            nc.gpsimd.memset(keep["ones"][:], 1.0).then_inc(iotas, 1)
            nc.gpsimd.iota(keep["node_h"], [[1, NODES]], -CENTER, 0,
                           allow_small_or_imprecise_dtypes=True).then_inc(iotas, 1)
            nc.gpsimd.iota(keep["col_h"][:], [[1, P]], 0, 0,
                           allow_small_or_imprecise_dtypes=True).then_inc(iotas, 1)

        @block.vector
        def _(dve):
            v = Marks(vec)

            def after(ins):
                dve.wait_ge(vec, v.on(ins))

            dve.wait_ge(iotas, 3)
            v.on(nc.vector.memset(dst_t[:, TCH - 1, :], 0.0))
            v.on(nc.vector.tensor_copy(step_f[:], step_i))
            v.on(nc.vector.tensor_copy(keep["lane_f"][:], lane_i[:]))
            v.on(nc.vector.memset(counts[:, 0:1], 0.0))
            after(nc.vector.tensor_copy(keep["col_f"][:], step_i[:, 0:P]))
            v.on(nc.vector.tensor_scalar(keep["ident"][:], keep["col_f"][:], keep["lane_f"][:, 0:1],
                                         None, ALU.is_equal))
            v.on(nc.vector.tensor_scalar(tri[:], keep["col_f"][:], keep["lane_f"][:, 0:1],
                                         None, ALU.is_gt))
            v.on(nc.vector.tensor_scalar(names[:, 0, :], keep["ones"][0:W, :], keep["lane_f"][0:W, 0:1],
                                         None, ALU.mult))
            for q in range(TCH):
                v.on(nc.vector.tensor_scalar(lane_q[:, q:q + 1], keep["lane_f"][:], float(q * P), None,
                                             ALU.add))
            dve.wait_ge(edges_in["dst"], 48)
            after(nc.vector.tensor_scalar(dst_h[:], raw["dst"][:].rearrange("p q c -> p (q c)"),
                                          -float(CENTER), 2000.0, ALU.add, ALU.min))
            for w in range(1, W + 1):
                after(nc.vector.tensor_scalar(below, dst_h[:], float(w * P - CENTER), 0.0, ALU.is_lt,
                                              ALU.add, accum_out=counts[:, w:w + 1]))
            done["counts"] = v.n
            dve.wait_ge(edges_in["src"], 48)
            v.on(nc.vector.tensor_copy(rows["src"][:], raw["src"][:]))
            v.on(nc.vector.tensor_copy(rows["dst"][:], raw["dst"][:]))
            dve.wait_ge(small, 1)
            after(nc.vector.tensor_copy(edge_i[:], psum[0:W, 0, 0:2]))
            after(nc.vector.tensor_scalar(edge_i[:], edge_i[:], P.bit_length() - 1, None,
                                          ALU.logical_shift_right))
            after(nc.vector.tensor_copy(edge_f[:], edge_i[:]))
            after(nc.vector.tensor_tensor(size_f[:], edge_f[:, 1:2], edge_f[:, 0:1], ALU.subtract))
            after(nc.vector.tensor_scalar(size_i[:], size_f[:], float(GROUP), float(2 * GROUP),
                                          ALU.add, ALU.max))
            after(nc.vector.tensor_scalar(size_i[:], size_i[:], GROUP.bit_length() - 1, None,
                                          ALU.logical_shift_right))
            after(nc.vector.tensor_copy(size_g[:], size_i[:]))
            done["sizes"] = v.n
            dve.wait_ge(small, 2)
            after(nc.vector.tensor_scalar(bounds[:, 0:1], psum[0:W, 1, 0:1], float(GROUP), None, ALU.mult))
            v.on(nc.vector.scalar_tensor_tensor(out=bounds[:, 1:2], in0=size_g[:],
                                                scalar=float(GROUP), in1=bounds[:, 0:1],
                                                op0=ALU.mult, op1=ALU.add))
            v.on(nc.vector.tensor_copy(bounds[:, 3:4], psum[0:W, 1, 0:1]))
            v.on(nc.vector.tensor_tensor(bounds[:, 4:5], psum[0:W, 1, 0:1], size_g[:], ALU.add))
            after(nc.vector.tensor_tensor(bounds[:, 2:3], bounds[:, 0:1], edge_f[:, 0:1], ALU.subtract))
            v.on(nc.vector.tensor_scalar(names[:, 1, :], keep["ones"][0:W, :], bounds[:, 2:3],
                                         None, ALU.mult))
            v.on(nc.vector.tensor_scalar(flags[:, 0, :], step_f[0:W, :], bounds[:, 0:1], None, ALU.is_ge))
            after(nc.vector.tensor_scalar(flags[:, 1, :], step_f[0:W, :], bounds[:, 1:2], None,
                                          ALU.is_lt))
            after(nc.vector.tensor_tensor(flags[:, 1, :], flags[:, 1, :], flags[:, 0, :], ALU.mult))
            done["flags"] = v.n
            dve.wait_ge(small, 3)
            for i in range(2):
                v.on(nc.vector.tensor_copy(keep["pairs_i"][:, :, i], psum[0:1, 2, i * W:(i + 1) * W]))
            after(nc.vector.tensor_scalar(totals_i[:, 0:1], psum[0:1, 2, 2 * W:2 * W + 1],
                                          float(SLOTS - 1), None, ALU.add))
            v.on(nc.vector.tensor_scalar(totals_i[:, 1:2], psum[0:1, 2, 2 * W:2 * W + 1], -1.0, None,
                                         ALU.add))
            v.on(nc.vector.tensor_scalar(keep["rounds_i"][:, 0:1], totals_i[:, 0:1],
                                         SLOTS.bit_length() - 1, None, ALU.logical_shift_right))
            dve.wait_ge(vec, v.n)
            v.on(nc.vector.tensor_scalar(keep["rounds_i"][:, 1:2], totals_i[:, 1:2],
                                         SLOTS.bit_length() - 1, None, ALU.logical_shift_right))
            dve.wait_ge(small, 4)
            v.on(nc.vector.tensor_copy(keep["win_i"][:], psum[0:1, 3, 0:STEPS:GROUP]))
            after(nc.vector.scalar_tensor_tensor(out=tile_of[:], in0=psum[:, 4, 0:STEPS], scalar=-1.0,
                                                 in1=step_f[:], op0=ALU.mult, op1=ALU.add))
            for q in range(TCH):
                v.on(nc.vector.tensor_scalar(pick[:, q, :], tile_of[:], lane_q[:, q:q + 1], None,
                                             ALU.is_equal))
            done["pick"] = v.n
            dve.wait_ge(vec, v.n)
            after(nc.vector.tensor_copy(tile_of[:], psum[:, 3, 0:STEPS]))
            dve.wait_ge(loads, 7 * 16)
            v.on(nc.vector.memset(hT[:, NODES:PADDED], 0.0))
            for i, of in enumerate((hT[:, 0:NODES], params["w_msg"][:], params["b_rep"][:])):
                v.on(nc.vector.tensor_reduce(params["largest"][:, i:i + 1], of, AXIS_X, ALU.max,
                                             apply_absolute_value=True))
            dve.wait_ge(picked, 1)
            v.on(nc.vector.tensor_copy(keep["src_f"][:], psum[:, 5, 0:STEPS]))
            dve.wait_ge(picked, 2)
            after(nc.vector.scalar_tensor_tensor(
                out=keep["dst_loc"][:], in0=tile_of[:], scalar=-float(P), in1=psum[:, 6, 0:STEPS],
                op0=ALU.mult, op1=ALU.add))
            done["dst_loc"] = v.n
            dve.wait_ge(picked, 3)
            v.on(nc.vector.tensor_copy(keep["weight"][:], psum[:, 7, 0:STEPS]))
            for q in range(TCH):
                n_q = min(P, STEPS - q * P)
                dve.wait_ge(turned, q + 1)
                v.on(nc.vector.tensor_copy(dst_t[0:n_q, q, :], psum[0:n_q, q, 0:P]))
            done["dst_t"] = v.n

        @block.tensor
        def _(pe):
            ones = keep["ones"]
            pe.wait_ge(vec, done["counts"])
            pe.wait_ge(iotas, 3)
            nc.tensor.matmul(psum[0:W, 0, 0:1], counts[:, 0:W], ones[:, 0:1], start=True, stop=True)
            nc.tensor.matmul(psum[0:W, 0, 1:2], counts[:, 1:W + 1], ones[:, 0:1],
                             start=True, stop=True).then_inc(small, 1)
            pe.wait_ge(vec, done["sizes"])
            nc.tensor.matmul(psum[0:W, 1, 0:1], tri[0:W, 0:W], size_g[:],
                             start=True, stop=True).then_inc(small, 1)
            pe.wait_ge(vec, done["flags"])
            for i in range(2):
                nc.tensor.matmul(psum[0:1, 2, i * W:(i + 1) * W], bounds[:, 3 + i:4 + i],
                                 keep["ident"][0:W, 0:W], start=True, stop=True)
            nc.tensor.matmul(psum[0:1, 2, 2 * W:2 * W + 1], size_g[:], ones[0:W, 0:1],
                             start=True, stop=True).then_inc(small, 1)
            for b in range(2):
                mm = nc.tensor.matmul(psum[:, 3 + b, 0:STEPS], names[:, b, :], flags[:, 1, :],
                                      start=True, stop=True)
            mm.then_inc(small, 1)
            pe.wait_ge(vec, done["pick"])
            pe.wait_ge(edges_in["weight"], 48)
            for b, name in ((5, "src"), (6, "dst"), (7, "weight")):
                for q in range(TCH):
                    mm = nc.tensor.matmul(psum[:, b, 0:STEPS], rows[name][:, q, :], pick[:, q, :],
                                          start=(q == 0), stop=(q == TCH - 1))
                mm.then_inc(picked, 1)
            pe.wait_ge(vec, done["dst_loc"])
            for q in range(TCH):
                n = min(P, STEPS - q * P)
                nc.tensor.transpose(psum[0:n, q, 0:P], keep["dst_loc"][:, q * P:q * P + n],
                                    keep["ident"][:]).then_inc(turned, 1)

        @block.sync
        def _(sp):
            sp.wait_ge(padded, 3)
            for n, dram in (("dst", dst), ("src", src), ("weight", edge_weight)):
                full = dram[0:q_full * P * P].rearrange("(q r p) -> r q p", p=P, r=P)
                sp.dma_start(raw[n][:, 0:q_full, :], full).then_inc(edges_in[n], 16)
                part = dram[q_full * P * P:whole * P].rearrange("(r p) -> r p", p=P)
                sp.dma_start(raw[n][0:q_rows, q_full, :], part).then_inc(edges_in[n], 16)
                tail = dram[whole * P:EDGES].rearrange("(r p) -> r p", r=1)
                sp.dma_start(raw[n][q_rows:q_rows + 1, q_full, 0:rest], tail).then_inc(edges_in[n], 16)
            sp.dma_start(hT[:, 0:NODES], xT).then_inc(loads, 16)
            for name, dram in (("w_msg", W_msgT), ("w_ih", W_ihT), ("w_hh", W_hhT)):
                sp.dma_start(params[name][:], dram).then_inc(loads, 16)
            sp.dma_start(params["b_rep"][:], b_msg.rearrange("(a n) -> a n", a=1)
                         .broadcast_to([P, D])).then_inc(loads, 16)
            for name, dram in (("b_i", b_ih), ("b_h", b_hh)):
                with nc.allow_non_contiguous_dma(reason="384 biases, one a partition"):
                    sp.dma_start(params[name][:], dram.rearrange("(g p) -> p g", p=P)).then_inc(loads, 16)
            sp.wait_ge(vec, done["dst_t"])
            for q in range(TCH):
                n = min(P, STEPS + MOVED - q * P)
                sp.dma_start(dst_rows[q * P * P:(q * P + n) * P].rearrange("(r p) -> r p", p=P),
                             dst_t[0:n, q, :]).then_inc(tables_out, 16)
            for i, name in enumerate(("src_f", "dst_loc", "weight")):
                sp.dma_start(tables[i], keep[name][:]).then_inc(tables_out, 16)
            sp.wait_ge(loads, 7 * 16)


def build_adjacency(nc, psum, keep, adj, tables_out):
    with ExitStack() as ctx:
        def sb(name, shape, dt):
            return ctx.enter_context(nc.sbuf_tensor(name, shape, dt))

        def sem(name):
            return ctx.enter_context(nc.semaphore(name))

        node_h, col_h = keep["node_h"], keep["col_h"]
        src_c = sb("src_c", [P, STEPS], F32)
        src_hot = sb("src_hot", [P, 2, NODES], F16)
        dst_hot = sb("dst_hot", [P, 2, P], F16)
        HALF = CHUNKS // 2 * CHUNK

        consts = sem("consts_a")
        hot = sem("hot")
        half_used = sem("half_used")
        used = sem("used")
        act_out = sem("act_out")
        dve_out = sem("dve_out")

        def width(c):
            return min(CHUNK, NODES - c * CHUNK)

        STORED = 16 * (TCH + 3)
        act_banks = [c for c in range(CHUNKS) if c not in EVAC_DVE]
        block = ctx.enter_context(nc.Block())

        def window_pairs(w, engine):
            _, (first, end) = nc.values_load_multi_w_load_instructions(
                keep["pairs_i"][0:1, w if isinstance(w, int) else bass.ds(w, 1), :],
                engines=(engine,), min_val=0, max_val=GROUPS)
            return first, end

        @block.vector
        def _(dve):
            nc.vector.tensor_scalar(src_c[:], keep["src_f"][:], -float(CENTER), None,
                                    ALU.add).then_inc(consts, 1)
            dve.sem_inc(half_used, 2)
            dve.sem_inc(used, 2)
            dve.wait_ge(consts, 1)

            def one_hots(pair):
                step = nc.s_assert_within(
                    pair * GROUP, 0, STEPS - GROUP,
                    skip_runtime_bounds_check_because="the tables have room for all windows' groups")
                for j in range(2):
                    k = bass.ds(step + j, 1)
                    dve.wait_ge(half_used, pair * 2 + j + 1)
                    nc.vector.tensor_scalar(src_hot[:, j, 0:HALF], node_h[:, 0:HALF], src_c[:, k],
                                            None, ALU.is_equal).then_inc(hot, 1)
                    dve.wait_ge(used, pair * 2 + j + 1)
                    nc.vector.tensor_scalar(dst_hot[:, j, :], col_h[:], keep["dst_loc"][:, k], None,
                                            ALU.is_equal).then_inc(hot, 1)
                    nc.vector.tensor_scalar(src_hot[:, j, HALF:NODES], node_h[:, HALF:NODES],
                                            src_c[:, k], None, ALU.is_equal).then_inc(hot, 1)

            def rest_of(first, end):
                with dve.Fori(first + 1, end) as pair:
                    one_hots(pair)

            def take(w, end):
                dve.wait_ge(used, end * 2 + 2)
                for c in EVAC_DVE:
                    nc.vector.tensor_copy(adj[:, w, c * CHUNK:c * CHUNK + width(c)],
                                          psum[:, c, 0:width(c)]).then_inc(dve_out, 1)

            first, _ = window_pairs(0, mybir.EngineType.DVE)
            one_hots(first)
            dve.wait_ge(tables_out, STORED)
            dve.sem_inc(consts, 1)
            with dve.Fori(0, WINDOWS - 1) as w:
                first, end = window_pairs(w, mybir.EngineType.DVE)
                rest_of(first, end)
                first, _ = window_pairs(w + 1, mybir.EngineType.DVE)
                one_hots(first)
                take(bass.ds(w, 1), end)
            first, end = window_pairs(WINDOWS - 1, mybir.EngineType.DVE)
            rest_of(first, end)
            take(WINDOWS - 1, end)

        @block.scalar
        def _(act):
            nc.scalar.preload_act_table(ACT.Copy)
            act.wait_ge(tables_out, STORED)
            with act.Fori(0, WINDOWS) as w:
                _, end = window_pairs(w, mybir.EngineType.Activation)
                act.wait_ge(used, end * 2 + 2)
                for c in act_banks:
                    nc.scalar.copy(adj[:, bass.ds(w, 1), c * CHUNK:c * CHUNK + width(c)],
                                   psum[:, c, 0:width(c)]).then_inc(act_out, 1)

        @block.sync
        def _(sp):
            sp.wait_ge(tables_out, STORED)

        @block.tensor
        def _(pe):
            pe.sem_inc(act_out, len(act_banks))
            pe.sem_inc(dve_out, len(EVAC_DVE))

            def multiply(pair, w=None):
                for j in range(2):
                    pe.wait_ge(hot, pair * 6 + 3 * j + 2)
                    for c in range(CHUNKS):
                        if c * CHUNK == HALF:
                            pe.wait_ge(hot, pair * 6 + 3 * j + 3)
                        start = w is not None and j == 0
                        if start and c in EVAC_DVE:
                            pe.wait_ge(dve_out, w * len(EVAC_DVE) + EVAC_DVE.index(c) + 1)
                        elif start:
                            pe.wait_ge(act_out, w * len(act_banks) + act_banks.index(c) + 1)
                        mm = nc.tensor.matmul(psum[:, c, 0:width(c)], dst_hot[:, j, :],
                                              src_hot[:, j, c * CHUNK:c * CHUNK + width(c)],
                                              start=start, stop=False, skip_group_check=True)
                        if (c + 1) * CHUNK == HALF:
                            mm.then_inc(half_used, 1)
                    mm.then_inc(used, 1)

            with pe.Fori(0, WINDOWS) as w:
                first, end = window_pairs(w, mybir.EngineType.PE)
                multiply(first, w)
                with pe.Fori(first + 1, end) as pair:
                    multiply(pair)


def chunk_width(c):
    return min(CHUNK, NODES - c * CHUNK)


def group_tiles(g):
    return range(4 * g, min(4 * g + 4, WINDOWS))


def gated_steps(nc, psum, keep, hT, params, adj):
    with ExitStack() as ctx:
        def sb(name, shape, dt):
            return ctx.enter_context(nc.sbuf_tensor(name, shape, dt))

        def sem(name):
            return ctx.enter_context(nc.semaphore(name))

        parts = sb("parts", [P, WINDOWS, 2, P], F16)
        scaled_m = sb("scaled_m", [P, 2, CHUNK], F32)
        agg = sb("agg", [P, 2, CHUNK], F32)
        r, z, n = (keep["node_room"][:].bitcast(F32)[:, i * CHUNK:(i + 1) * CHUNK] for i in range(3))
        b_rz = sb("b_rz", [P, 2], F32)
        of_all = sb("of_all", [3, 1], F32)
        spread3 = sb("spread3", [3, 3], F32)
        limits = sb("limits", [P, 3], F32)
        scales = sb("scales", [P, 2], F32)
        w_msg, w_ih, w_hh, b_rep, b_i, b_h = (
            params[k] for k in ("w_msg", "w_ih", "w_hh", "b_rep", "b_i", "b_h"))

        setup = sem("l0_setup")
        limit = sem("limit")
        messages = sem("messages")
        scaled = sem("scaled")
        high = sem("high")
        low = sem("low")
        summed = sem("summed")
        agg_out = sem("agg_out")
        gates = sem("gates")
        r_on = sem("r_on")
        z_on = sem("z_on")
        n_pre = sem("n_pre")
        n_on = sem("n_on")
        h_new = sem("h_new")
        inner = sem("l0_inner")

        M_BANKS, AGG_BANK = (0, 1, 2), 3
        R_BANK, Z_BANK, IN_BANK, HN_BANK = 4, 5, 6, 7
        AHEAD = len(M_BANKS)
        EARLY = 5
        EXPONENT, TOP, TWICE = 0x7F800000, float((127 + 127 + 14) << 23), float((127 + 127) << 23)
        at = {}

        block = ctx.enter_context(nc.Block())

        @block.vector
        def _(dve):
            m = Marks(setup)

            def after(ins):
                dve.wait_ge(setup, m.on(ins))

            m.on(nc.vector.tensor_tensor(b_rz[:], b_i[:, 0:2], b_h[:, 0:2], ALU.add))
            dve.wait_ge(limit, 1)
            after(nc.vector.tensor_reduce(of_all[:], psum[0:3, R_BANK, 0:P], AXIS_X, ALU.max))
            at["spread3"] = m.on(nc.vector.tensor_scalar(spread3[:], keep["ident"][0:3, 0:3], of_all[:, 0:1],
                                                         None, ALU.mult))
            dve.wait_ge(limit, 2)
            after(nc.vector.tensor_copy(limits[:], psum[:, Z_BANK, 0:3]))
            after(nc.vector.tensor_scalar(limits[:, 0:1], limits[:, 0:1], 1.0, float(D), ALU.max, ALU.mult))
            after(nc.vector.scalar_tensor_tensor(out=limits[:, 0:1], in0=limits[:, 0:1],
                                                 scalar=limits[:, 1:2], in1=limits[:, 2:3],
                                                 op0=ALU.mult, op1=ALU.add))
            after(nc.vector.tensor_scalar(limits[:, 0:1], limits[:, 0:1], 1e-30, None, ALU.max))
            bits = scales[:].bitcast(I32)
            after(nc.vector.tensor_scalar(bits[:, 1:2], limits[:, 0:1].bitcast(I32), EXPONENT, None,
                                          ALU.bitwise_and))
            after(nc.vector.tensor_scalar(bits[:, 0:1], bits[:, 1:2], -1.0, TOP, ALU.mult, ALU.add))
            after(nc.vector.tensor_scalar(bits[:, 1:2], bits[:, 0:1], -1.0, TWICE, ALU.mult, ALU.add))
            after(nc.vector.tensor_scalar(b_rep[:], b_rep[:], scales[:, 0:1], None, ALU.mult))
            at["scales"] = m.n
            dve.sem_inc(h_new, CHUNKS)

            def scale(s, g):
                k = len(group_tiles(g))
                dve.wait_ge(messages, s * CHUNKS + g + 1)
                nc.vector.scalar_tensor_tensor(
                    out=scaled_m[:, g % 2, 0:k * P].rearrange("p (t d) -> p t d", d=P),
                    in0=psum[:, M_BANKS[g % AHEAD], 0:k * P].rearrange("p (t d) -> p t d", d=P),
                    scalar=scales[:, 0:1], in1=b_rep[:].unsqueeze(1).broadcast_to([P, k, D]),
                    op0=ALU.mult, op1=ALU.add).then_inc(scaled, 1)

            def split(s, g):
                k = len(group_tiles(g))
                dve.wait_ge(high, s * CHUNKS + g + 1)
                nc.vector.tensor_tensor(parts[:, 4 * g:4 * g + k, 1, :],
                                        scaled_m[:, g % 2, 0:k * P].rearrange("p (t d) -> p t d", d=P),
                                        parts[:, 4 * g:4 * g + k, 0, :], ALU.subtract).then_inc(low, 1)

            def split_groups(s, groups):
                if groups[0] or not isinstance(s, int):
                    dve.wait_ge(low, s * CHUNKS + groups[0])
                scale(s, groups[0])
                for g in groups[1:]:
                    if g >= 2:
                        dve.wait_ge(low, s * CHUNKS + g - 1)
                    scale(s, g)
                    split(s, g - 1)
                split(s, groups[-1])

            def gate(at, cols, n_cols):
                h_c = hT[:, cols]
                first = at * 3 - 3
                dve.wait_ge(r_on, at)
                nc.vector.scalar_tensor_tensor(
                    out=n[:, 0:n_cols], in0=psum[:, HN_BANK, 0:n_cols], scalar=b_h[:, 2:3],
                    in1=r[:, 0:n_cols], op0=ALU.add, op1=ALU.mult).then_inc(inner, 1)
                dve.wait_ge(inner, first + 1)
                nc.vector.tensor_tensor(n[:, 0:n_cols], psum[:, IN_BANK, 0:n_cols], n[:, 0:n_cols],
                                        ALU.add).then_inc(n_pre, 1)
                dve.wait_ge(n_on, at)
                nc.vector.tensor_tensor(r[:, 0:n_cols], h_c, n[:, 0:n_cols],
                                        ALU.subtract).then_inc(inner, 1)
                dve.wait_ge(inner, first + 2)
                dve.wait_ge(z_on, at)
                nc.vector.tensor_tensor(r[:, 0:n_cols], r[:, 0:n_cols], z[:, 0:n_cols],
                                        ALU.mult).then_inc(inner, 1)
                dve.wait_ge(inner, first + 3)
                nc.vector.tensor_tensor(h_c, r[:, 0:n_cols], n[:, 0:n_cols],
                                        ALU.add).then_inc(h_new, 1)
                dve.wait_ge(h_new, at + CHUNKS)

            def step(s, last):
                first = s * CHUNKS
                split_groups(s, range(EARLY, CHUNKS))
                with dve.Fori(0, CHUNKS - 2) as c:
                    gate(first + c + 1, bass.ds(c * CHUNK, CHUNK), CHUNK)
                if not last:
                    split_groups(s + 1, range(AHEAD))
                c = CHUNKS - 1
                gate(first + c, slice((c - 1) * CHUNK, c * CHUNK), CHUNK)
                if not last:
                    split_groups(s + 1, range(AHEAD, EARLY))
                gate(first + c + 1, slice(c * CHUNK, NODES), chunk_width(c))

            split_groups(0, range(EARLY))
            with dve.Fori(0, GRU_STEPS - 1) as s:
                step(s, last=False)
            step(GRU_STEPS - 1, last=True)

        @block.tensor
        def _(pe):
            def make_messages(s, g):
                pe.wait_ge(h_new, s * CHUNKS + g + 1)
                if g >= AHEAD:
                    pe.wait_ge(scaled, s * CHUNKS + g - AHEAD + 1)
                for i, t in enumerate(group_tiles(g)):
                    mm = nc.tensor.matmul(psum[:, M_BANKS[g % AHEAD], i * P:(i + 1) * P],
                                          hT[:, t * P:(t + 1) * P], w_msg[:], start=True, stop=True)
                mm.then_inc(messages, 1)

            def sum_over(cols, n_cols, windows):
                for w in windows:
                    for part in range(2):
                        mm = nc.tensor.matmul(psum[:, AGG_BANK, 0:n_cols], parts[:, w, part, :],
                                              adj[:, w, cols], start=(w == 0 and part == 0),
                                              stop=(w == WINDOWS - 1 and part == 1))
                return mm

            def sum_chunk(at, cols, n_cols):
                pe.wait_ge(agg_out, at - 1)
                sum_over(cols, n_cols, range(WINDOWS)).then_inc(summed, 1)

            def gate_products(at, slot, cols, n_cols):
                pe.wait_ge(h_new, at + CHUNKS - 1)
                for bank, g, alone in ((R_BANK, 0, False), (Z_BANK, 1, False), (HN_BANK, 2, True)):
                    nc.tensor.matmul(psum[:, bank, 0:n_cols], w_hh[:, g * D:(g + 1) * D], hT[:, cols],
                                     start=True, stop=alone)
                pe.wait_ge(agg_out, at)
                for bank, g, alone in ((R_BANK, 0, False), (Z_BANK, 1, False), (IN_BANK, 2, True)):
                    mm = nc.tensor.matmul(psum[:, bank, 0:n_cols], w_ih[:, g * D:(g + 1) * D],
                                          agg[:, slot, 0:n_cols], start=alone, stop=True)
                mm.then_inc(gates, 1)

            nc.tensor.transpose(psum[0:3, R_BANK, 0:P], params["largest"][:], keep["ident"][:]).then_inc(limit, 1)
            pe.wait_ge(setup, at["spread3"])
            nc.tensor.matmul(psum[:, Z_BANK, 0:3], keep["ones"][0:3, :], spread3[:],
                             start=True, stop=True).then_inc(limit, 1)

            def sum_groups(s, groups, to_make):
                for g in groups:
                    pe.wait_ge(low, s * CHUNKS + g + 1)
                    mm = sum_over(slice(0, CHUNK), CHUNK, group_tiles(g))
                    if g + AHEAD in to_make:
                        make_messages(s, g + AHEAD)
                return mm

            def start_step(s):
                for g in range(AHEAD):
                    make_messages(s, g)

            def step(s, last):
                first = s * CHUNKS
                make_messages(s, EARLY)
                sum_groups(s, range(AHEAD, CHUNKS), range(EARLY + 1, CHUNKS)).then_inc(summed, 1)
                with pe.Fori(0, (CHUNKS - 3) // 2) as c2:
                    for k in range(2):
                        sum_chunk(first + (c2 * 2 + k + 2), bass.ds((c2 * 2 + k + 1) * CHUNK, CHUNK), CHUNK)
                        gate_products(first + (c2 * 2 + k + 1), k, bass.ds((c2 * 2 + k) * CHUNK, CHUNK), CHUNK)
                for c in range(CHUNKS - 2, CHUNKS):
                    sum_chunk(first + c + 1, slice(c * CHUNK, c * CHUNK + chunk_width(c)), chunk_width(c))
                    if c + 1 == CHUNKS and not last:
                        start_step(s + 1)
                    gate_products(first + c, (c - 1) % 2, slice((c - 1) * CHUNK, c * CHUNK), CHUNK)
                if not last:
                    pe.wait_ge(agg_out, first + CHUNKS)
                    sum_groups(s + 1, range(AHEAD), range(AHEAD, EARLY))
                gate_products(first + CHUNKS, (CHUNKS - 1) % 2, slice(c * CHUNK, NODES), chunk_width(c))

            start_step(0)
            sum_groups(0, range(AHEAD), range(AHEAD, EARLY))
            with pe.Fori(0, GRU_STEPS - 1) as s:
                step(s, last=False)
            step(GRU_STEPS - 1, last=True)

        @block.scalar
        def _(act):
            def split(s, g):
                k = len(group_tiles(g))
                act.wait_ge(scaled, s * CHUNKS + g + 1)
                nc.scalar.activation(parts[:, 4 * g:4 * g + k, 0, :],
                                     scaled_m[:, g % 2, 0:k * P].rearrange("p (t d) -> p t d", d=P),
                                     ACT.Copy).then_inc(high, 1)

            def take_sum(at, slot, n_cols):
                act.wait_ge(summed, at)
                nc.scalar.activation(agg[:, slot, 0:n_cols], psum[:, AGG_BANK, 0:n_cols],
                                     ACT.Copy, scale=scales[:, 1:2]).then_inc(agg_out, 1)

            def gate(at, n_cols):
                act.wait_ge(gates, at)
                act.wait_ge(h_new, at + CHUNKS - 1)
                nc.scalar.activation(r[:, 0:n_cols], psum[:, R_BANK, 0:n_cols], ACT.Sigmoid,
                                     bias=b_rz[:, 0:1]).then_inc(r_on, 1)
                nc.scalar.activation(z[:, 0:n_cols], psum[:, Z_BANK, 0:n_cols], ACT.Sigmoid,
                                     bias=b_rz[:, 1:2]).then_inc(z_on, 1)
                act.wait_ge(n_pre, at)
                nc.scalar.activation(n[:, 0:n_cols], n[:, 0:n_cols], ACT.Tanh,
                                     bias=b_i[:, 2:3]).then_inc(n_on, 1)

            nc.scalar.preload_act_table(ACT.Sigmoid)
            act.wait_ge(setup, at["scales"])
            def step(s, last):
                first = s * CHUNKS
                for g in range(EARLY, CHUNKS):
                    split(s, g)
                take_sum(first + 1, 0, CHUNK)
                with act.Fori(0, (CHUNKS - 3) // 2) as c2:
                    for k in range(2):
                        take_sum(first + (c2 * 2 + k + 2), (k + 1) % 2, CHUNK)
                        gate(first + (c2 * 2 + k + 1), CHUNK)
                c = CHUNKS - 2
                take_sum(first + c + 1, c % 2, CHUNK)
                gate(first + c, CHUNK)
                take_sum(first + CHUNKS, (CHUNKS - 1) % 2, chunk_width(CHUNKS - 1))
                if not last:
                    for g in range(AHEAD):
                        split(s + 1, g)
                gate(first + CHUNKS - 1, CHUNK)
                if not last:
                    for g in range(AHEAD, EARLY):
                        split(s + 1, g)
                gate(first + CHUNKS, chunk_width(CHUNKS - 1))

            for g in range(EARLY):
                split(0, g)
            with act.Fori(0, GRU_STEPS - 1) as s:
                step(s, last=False)
            step(GRU_STEPS - 1, last=True)


def add_and_norm(nc, tag, v, base, result, psum, keep, hT):
    with ExitStack() as ctx:
        def sb(name, shape, dt):
            return ctx.enter_context(nc.sbuf_tensor(name + tag, shape, dt))

        def sem(name):
            return ctx.enter_context(nc.semaphore(name + tag))

        BATCHES = (range(0, 1), range(1, 3), range(3, 5), range(5, 7))
        stats = sb("stats", [P, WINDOWS, 6], F32)
        moments = sb("moments", [P, WINDOWS, 2], F32)
        spread = sb("spread", [P, WINDOWS], F32)
        base_in = [sem(f"base_in{b}") for b in range(len(BATCHES))]
        cleared = sem("cleared")
        turned = sem("turned_n")
        vec = sem("vec_n")
        rooted = sem("rooted")
        scaled = sem("scaled")
        back = sem("back")
        back_out = sem("back_out")
        stored = sem("stored")
        full = WINDOWS - 1
        at = {}

        def tiles(batch):
            return range(group_tiles(batch[0])[0], group_tiles(batch[-1])[-1] + 1)

        def parts(dram, batch):
            a, b = tiles(batch)[0], tiles(batch)[-1] + 1
            whole = min(b, full)
            yield v[:, a:whole, :], dram[a * P:whole * P, :].rearrange("(t p) d -> p t d", p=P)
            if b > full:
                yield v[0:LAST, full, :], dram[full * P:NODES, :]

        block = ctx.enter_context(nc.Block())

        @block.sync
        def _(sp):
            if base is not None:
                for b, batch in enumerate(BATCHES):
                    for to, dram in parts(base, batch):
                        if b == len(BATCHES) - 1:
                            sp.wait_ge(cleared, 1)
                        sp.dma_start(to, dram).then_inc(base_in[b], 16)
            if result is not None:
                n = 0
                for batch in BATCHES:
                    sp.wait_ge(scaled, tiles(batch)[-1] + 1)
                    for rows, dram in parts(result, batch):
                        sp.dma_start(dram, rows).then_inc(stored, 16)
                        n += 16
                sp.wait_ge(stored, n)

        @block.tensor
        def _(pe):
            for g in range(CHUNKS):
                for i, t in enumerate(group_tiles(g)):
                    mm = nc.tensor.transpose(psum[:, g, i * P:(i + 1) * P], hT[:, t * P:(t + 1) * P],
                                             keep["ident"][:])
                mm.then_inc(turned, 1)
            if result is None:
                for g in range(CHUNKS):
                    pe.wait_ge(scaled, group_tiles(g)[-1] + 1)
                    for i, t in enumerate(group_tiles(g)):
                        mm = nc.tensor.transpose(psum[:, g, i * P:(i + 1) * P], v[:, t, :],
                                                 keep["ident"][:])
                    mm.then_inc(back, 1)

        @block.vector
        def _(dve):
            m = Marks(vec)
            if base is not None:
                nc.vector.memset(v[:, full, :], 0.0).then_inc(cleared, 1)
            for b, batch in enumerate(BATCHES):
                if base is not None:
                    dve.wait_ge(base_in[b], 16 * len(list(parts(base, batch))))
                for g in batch:
                    k = len(group_tiles(g))
                    v_g = v[:, 4 * g:4 * g + k, :]
                    dve.wait_ge(turned, g + 1)
                    dve.wait_ge(vec, m.on(nc.vector.tensor_tensor(
                        v_g, psum[:, g, 0:k * P].rearrange("p (t d) -> p t d", d=D), v_g, ALU.add)))
                    for t in group_tiles(g):
                        m.on(nc.vector.bn_stats(stats[:, t, :], v[:, t, :]))
                dve.wait_ge(vec, m.n)
                for t in tiles(batch):
                    m.on(nc.vector.bn_aggr(moments[:, t, :], stats[:, t, :]))
                dve.wait_ge(vec, m.n)
                ts = slice(tiles(batch)[0], tiles(batch)[-1] + 1)
                at[b] = m.on(nc.vector.tensor_scalar(spread[:, ts], moments[:, ts, 1], EPS, None, ALU.add))
            for b, batch in enumerate(BATCHES):
                ts = slice(tiles(batch)[0], tiles(batch)[-1] + 1)
                dve.wait_ge(rooted, b + 1)
                dve.wait_ge(vec, m.on(nc.vector.reciprocal(spread[:, ts], spread[:, ts])))
                for t in tiles(batch):
                    nc.vector.tensor_scalar(v[:, t, :], v[:, t, :], moments[:, t, 0:1], spread[:, t:t + 1],
                                            ALU.subtract, ALU.mult).then_inc(scaled, 1)

        @block.scalar
        def _(act):
            nc.scalar.preload_act_table(ACT.Sqrt)
            for b, batch in enumerate(BATCHES):
                ts = slice(tiles(batch)[0], tiles(batch)[-1] + 1)
                act.wait_ge(vec, at[b])
                nc.scalar.activation(spread[:, ts], spread[:, ts], ACT.Sqrt).then_inc(rooted, 1)
            if result is None:
                for g in range(CHUNKS):
                    n = chunk_width(g)
                    act.wait_ge(back, g + 1)
                    nc.scalar.activation(hT[:, g * CHUNK:g * CHUNK + n], psum[:, g, 0:n],
                                         ACT.Copy).then_inc(back_out, 1)


def edge_layers(nc, weights, psum, keep, hT, dst_rows, tables, debug):
    with ExitStack() as ctx:
        def sb(name, shape, dt):
            return ctx.enter_context(nc.sbuf_tensor(name, shape, dt))

        t = {
            "q_parts": sb("q_parts", [P, WINDOWS, 3, D], BF16),
            "agg_t": sb("agg_t", [P, PADDED], F32),
            "dst_loc": sb("dst_loc_e", [P, STEPS], F32),
            "weight": sb("weight_e", [P, STEPS], F32),
            "src_i": sb("src_i", [P, STEPS + SLOTS * GROUP], I32),
        }
        for name, shape in (("w_n", [P, 2, D]), ("b_n", [P, 1]), ("w_ab", [P, 2 * D]), ("b_rep_e", [P, D])):
            t[name] = sb(name, shape, F32)
        p_dram = nc.dram_tensor("p_dram", (NODES, D), F32, kind="Internal").ap()
        e_dram = [nc.dram_tensor(f"e{i}_dram", (STEPS // MOVED, P, MOVED * P), F32, kind="Internal").ap()
                  for i in range(2)]
        first_loads = weight_loads(t, None, weights[0][0:2])
        node_stage(nc, "_first", False, True, psum, hT, t, p_dram, first_loads, tables)
        for l, (We, be, Wn, bn) in enumerate(weights):
            more = l + 1 < len(weights)
            clear_semaphores(nc)
            edge_pass(nc, f"_{l}", We[2 * D:3 * D, :] if l else None, psum, keep, t, dst_rows, p_dram,
                      e_dram[l - 1] if l else None, e_dram[l] if more else None,
                      weight_loads(t, (Wn, bn), weights[l + 1][0:2] if more else None))
            node_stage(nc, f"_{l}", True, more, psum, hT, t, p_dram)
            if debug:
                debug(f"l{l}", nc, {"hT": hT, "agg": t["agg_t"]})


def weight_loads(t, update, products):
    loads = []
    if update is not None:
        Wn, bn = update
        loads += [(t["w_n"][:], Wn.rearrange("(h p) d -> p h d", p=P)),
                  (t["b_n"][:], bn.rearrange("(p a) -> p a", a=1))]
    if products is not None:
        We, be = products
        loads += [(t["w_ab"][:, 0:D], We[0:D, :]), (t["w_ab"][:, D:2 * D], We[D:2 * D, :]),
                  (t["b_rep_e"][:], be.rearrange("(a n) -> a n", a=1).broadcast_to([P, D]))]
    return loads


def node_stage(nc, tag, update, products, psum, hT, t, p_dram, loads=(), tables=None):
    with ExitStack() as ctx:
        def sb(name, shape, dt):
            return ctx.enter_context(nc.sbuf_tensor(name + tag, shape, dt))

        def sem(name):
            return ctx.enter_context(nc.semaphore(name + tag))

        p_sb = sb("p_sb", [P, WINDOWS, D], F32)
        residue = sb("residue_q", [P, 2, 2, D], F32)
        src_f = sb("src_f_e", [P, STEPS], F32) if tables is not None else None
        w_in = sem("weights_in")
        updated = sem("updated")
        x_on = sem("x_on")
        product = sem("product")
        p_out = sem("p_out")
        high, mid = sem("q_high"), sem("q_mid")
        resid, low = sem("q_resid"), sem("q_low")
        stored = sem("p_stored")
        tabs = sem("tabs_in")
        made = sem("made")
        pairs = [range(a, min(a + 2, WINDOWS)) for a in range(0, WINDOWS, 2)] if products else []
        N = len(pairs)
        q_parts = t["q_parts"]
        P_BANKS, U_BANKS = 6, 2

        def bank(i, half):
            k = len(pairs[i])
            return psum[:, i % P_BANKS, 0:k * 2 * D].rearrange("p (k h d) -> p k h d", k=k, h=2)[:, :, half, :]

        block = ctx.enter_context(nc.Block())

        @block.sync
        def _(sp):
            for to, dram in loads:
                sp.dma_start(to, dram).then_inc(w_in, 16)
            if tables is not None:
                for i, to in enumerate((src_f, t["dst_loc"], t["weight"])):
                    sp.dma_start(to[:], tables[i]).then_inc(tabs, 16)
            if products:
                starts = (0, 4, 7, 10, N - 1)
                for a, b in zip(starts, starts[1:]):
                    sp.wait_ge(p_out, b)
                    sp.dma_start(p_dram[a * 2 * P:b * 2 * P, :].rearrange("(t p) d -> p t d", p=P),
                                 p_sb[:, a * 2:b * 2, :]).then_inc(stored, 16)
                sp.wait_ge(p_out, N)
                sp.dma_start(p_dram[(WINDOWS - 1) * P:NODES, :],
                             p_sb[0:LAST, WINDOWS - 1, :]).then_inc(stored, 16)
                sp.wait_ge(stored, 16 * len(starts))

        @block.gpsimd
        def _(pool):
            if products:
                if update:
                    pool.wait_ge(updated, CHUNKS)
                nc.gpsimd.memset(t["agg_t"][:], 0.0).then_inc(made, 1)
            if tables is not None:
                nc.gpsimd.memset(t["src_i"][:, STEPS:], 0).then_inc(made, 1)
                pool.wait_ge(tabs, 48)
                nc.gpsimd.tensor_copy(t["src_i"][:, 0:STEPS], src_f[:]).then_inc(made, 1)

        @block.tensor
        def _(pe):
            def new_x(c):
                n = chunk_width(c)
                o = psum[:, P_BANKS + c % U_BANKS, 0:n]
                if c >= U_BANKS:
                    pe.wait_ge(x_on, c - U_BANKS + 1)
                nc.tensor.matmul(o, t["w_n"][:, 0, :], hT[:, c * CHUNK:c * CHUNK + n],
                                 start=True, stop=False)
                nc.tensor.matmul(o, t["w_n"][:, 1, :], t["agg_t"][:, c * CHUNK:c * CHUNK + n],
                                 start=False, stop=True).then_inc(updated, 1)

            if loads:
                pe.wait_ge(w_in, 16 * len(loads))
            if update:
                for c in range(CHUNKS if not products else U_BANKS):
                    new_x(c)
            for i, pair in enumerate(pairs):
                if update:
                    pe.wait_ge(x_on, i // 2 + 1)
                if i >= P_BANKS:
                    pe.wait_ge(p_out, i - P_BANKS + 1)
                    pe.wait_ge(resid, i - P_BANKS + 1)
                for k, w in enumerate(pair):
                    mm = nc.tensor.matmul(psum[:, i % P_BANKS, k * 2 * D:(k + 1) * 2 * D],
                                          hT[:, w * P:(w + 1) * P], t["w_ab"][:], start=True, stop=True)
                mm.then_inc(product, 1)
                if update and i % 2 == 0 and i // 2 + U_BANKS < CHUNKS:
                    new_x(i // 2 + U_BANKS)

        @block.scalar
        def _(act):
            def take_x(c):
                n = chunk_width(c)
                act.wait_ge(updated, c + 1)
                nc.scalar.activation(hT[:, c * CHUNK:c * CHUNK + n], psum[:, P_BANKS + c % U_BANKS, 0:n],
                                     ACT.Relu, bias=t["b_n"][:, 0:1]).then_inc(x_on, 1)

            def second_part(i):
                a, k = pairs[i][0], len(pairs[i])
                act.wait_ge(resid, i + 1)
                nc.scalar.activation(q_parts[:, a:a + k, 1, :], residue[:, i % 2, 0:k, :],
                                     ACT.Copy).then_inc(mid, 1)

            if update:
                for c in range(CHUNKS if not products else U_BANKS):
                    take_x(c)
            for i, pair in enumerate(pairs):
                a, k = pair[0], len(pair)
                act.wait_ge(product, i + 1)
                nc.scalar.activation(q_parts[:, a:a + k, 0, :], bank(i, 1), ACT.Copy).then_inc(high, 1)
                if update and i % 2 == 0 and i // 2 + U_BANKS < CHUNKS:
                    take_x(i // 2 + U_BANKS)
                if i >= 1:
                    second_part(i - 1)
            if pairs:
                second_part(N - 1)

        @block.vector
        def _(dve):
            def third_part(i):
                a, k = pairs[i][0], len(pairs[i])
                dve.wait_ge(mid, i + 1)
                nc.vector.tensor_tensor(q_parts[:, a:a + k, 2, :], residue[:, i % 2, 0:k, :],
                                        q_parts[:, a:a + k, 1, :], ALU.subtract).then_inc(low, 1)

            if loads:
                dve.wait_ge(w_in, 16 * len(loads))
            for i, pair in enumerate(pairs):
                a, k = pair[0], len(pair)
                dve.wait_ge(high, i + 1)
                if i >= 2:
                    dve.wait_ge(low, i - 1)
                nc.vector.tensor_tensor(residue[:, i % 2, 0:k, :], bank(i, 1), q_parts[:, a:a + k, 0, :],
                                        ALU.subtract).then_inc(resid, 1)
                nc.vector.tensor_tensor(p_sb[:, a:a + k, :], bank(i, 0),
                                        t["b_rep_e"][:].unsqueeze(1).broadcast_to([P, k, D]),
                                        ALU.add).then_inc(p_out, 1)
                if i >= 1:
                    third_part(i - 1)
            if pairs:
                third_part(N - 1)


def edge_pass(nc, tag, Wc, psum, keep, t, dst_rows, p_dram, e_before, e_after, next_loads):
    with ExitStack() as ctx:
        def sb(name, shape, dt):
            return ctx.enter_context(nc.sbuf_tensor(name + tag, shape, dt))

        def sem(name):
            return ctx.enter_context(nc.semaphore(name + tag))

        WIDE = GROUP * P
        MOVES = SLOTS // 2
        w_c = sb("w_c", [P, D], F32)
        ids = sb("ids", [P, SLOTS, GROUP], I32)
        p_rows = sb("p_rows", [P, SLOTS, WIDE], F32)
        before = sb("before", [P, MOVES, 2 * WIDE], F32)
        locals_ = sb("locals", [P, MOVES, 2 * WIDE], BF16)
        hot_t = sb("hot_t", [P, 4, WIDE], BF16)
        pre = sb("pre", [P, 2, WIDE], F32)
        e = sb("e", [P, 2, WIDE], F32)
        after = sb("after", [P, MOVES, 2 * WIDE], F32)
        hot_w = sb("hot_w", [P, 2, GROUP, P], F32)

        w_in = sem("w_in")
        ids_on = sem("ids_on")
        gathering = sem("gathering")
        rows_in = [sem(f"rows{j}") for j in range(SLOTS)]
        before_in = [sem(f"before{q}") for q in range(MOVES)]
        locals_in = [sem(f"locals{q}") for q in range(MOVES)]
        stored = [sem(f"stored{q}") for q in range(MOVES)]
        next_in = sem("next_in")
        all_stored = sem("all_stored")
        hot_t_on = sem("hot_t_on")
        spread = sem("spread")
        added = sem("added")
        hot_on = sem("hot_on")
        e_on = sem("e_on")
        e_turned = sem("e_turned")
        after_on = sem("after_on")
        summed = sem("summed_e")
        agg_on = sem("agg_on")

        E_BANKS, T_BANKS, A_BANKS = (0, 1), (2, 3), (4, 5)

        def at(j, m=None):
            return (slice(j % 2 * WIDE, (j % 2 + 1) * WIDE) if m is None else
                    slice(j % 2 * WIDE + m * P, j % 2 * WIDE + (m + 1) * P))

        def groups_ahead(i, is_last):
            for j in range(SLOTS):
                yield j, ((i, j + 1) if j + 1 < SLOTS else None if is_last else (i + 1, 0))

        def rounds(engine):
            return nc.values_load(keep["rounds_i"][0:1, 0:1], engines=(engine,),
                                  min_val=MIN_ROUNDS, max_val=MAX_ROUNDS)

        def last_round(engine):
            return nc.values_load(keep["rounds_i"][0:1, 1:2], engines=(engine,),
                                  min_val=MIN_ROUNDS - 1, max_val=MAX_ROUNDS - 1)

        def windows_of(i, j, n, engine):
            _, windows = nc.values_load_multi_w_load_instructions(
                keep["win_i"][0:1, bass.ds(i * SLOTS + j, n)], engines=(engine,),
                min_val=0, max_val=WINDOWS - 1)
            return windows

        block = ctx.enter_context(nc.Block())

        @block.gpsimd
        def _(pool):
            with pool.Fori(0, rounds(mybir.EngineType.Pool)) as i:
                for j in range(SLOTS):
                    pool.wait_ge(ids_on, i * SLOTS + j + 1)
                    pool.sem_inc(gathering, 1)
                    for m in range(GROUP):
                        nc.gpsimd.indirect_dma_start(
                            out=p_rows[:, j, m * D:(m + 1) * D], out_offset=None, in_=p_dram,
                            in_offset=bass.IndirectOffsetOnAxis(ap=ids[:, j, m:m + 1].bitcast(U32), axis=0),
                        ).then_inc(rows_in[j], 16)

        @block.sync
        def _(sp):
            if e_before is not None:
                sp.dma_start(w_c[:], Wc).then_inc(w_in, 16)

            def load_locals(n, q):
                sp.dma_start(locals_[:, q, :], dst_rows[bass.ds(n * (2 * WIDE), 2 * WIDE)]
                             .rearrange("(a n) -> a n", a=1).broadcast_to([P, 2 * WIDE])
                             ).then_inc(locals_in[q], 16)

            def load_before(n, q):
                sp.dma_start(before[:, q, :], e_before[bass.ds(n, 1), :, :]
                             .rearrange("a p n -> (a p) n")).then_inc(before_in[q], 16)

            def store(i, q):
                sp.wait_ge(after_on, i * SLOTS + 2 * q + 4)
                sp.dma_start(e_after[bass.ds(i * MOVES + q, 1), :, :].rearrange("a p n -> (a p) n"),
                             after[:, q, :]).then_inc(stored[q], 16)

            for q in range(MOVES):
                load_locals(q, q)
                if e_before is not None:
                    load_before(q, q)
            for to, dram in next_loads:
                sp.dma_start(to, dram).then_inc(next_in, 16)
            last = last_round(mybir.EngineType.SP)
            with sp.Fori(0, last) as i:
                for q in range(MOVES):
                    sp.wait_ge(hot_t_on, i * SLOTS + 2 * q + 2)
                    load_locals((i + 1) * MOVES + q, q)
                    if e_before is not None:
                        sp.wait_ge(spread, i * SLOTS + 2 * q + 2)
                        load_before((i + 1) * MOVES + q, q)
                    if e_after is not None:
                        store(i, q)
            sp.wait_ge(next_in, 16 * len(next_loads))
            sp.wait_ge(hot_t_on, last * SLOTS + 2)
            load_locals((last + 1) * MOVES, 0)
            if e_after is not None:
                for q in range(MOVES):
                    store(last, q)
                for q in range(MOVES):
                    sp.wait_ge(stored[q], last * 16 + 32)
                    sp.sem_inc(all_stored, 1)

        @block.tensor
        def _(pe):
            pe.sem_inc(summed, 2)
            if e_before is not None:
                pe.wait_ge(w_in, 16)

            def products(i, j, window):
                if j >= 2:
                    pe.wait_ge(added, i * SLOTS + j - 1)
                pe.wait_ge(hot_t_on, i * SLOTS + j + 1)
                if e_before is not None:
                    pe.wait_ge(before_in[j // 2], i * 16 + 16)
                for m in range(GROUP):
                    o = psum[:, E_BANKS[j % 2], m * D:(m + 1) * D]
                    for part in range(3):
                        mm = nc.tensor.matmul(o, hot_t[:, j % 4, m * P:(m + 1) * P],
                                              t["q_parts"][:, bass.ds(window, 1), part, :],
                                              start=(part == 0), stop=(part == 2 and e_before is None))
                    if e_before is not None:
                        mm = nc.tensor.matmul(o, before[:, j // 2, at(j, m)], w_c[:],
                                              start=False, stop=True)
                mm.then_inc(spread, 1)

            def turn_and_sum(i, j):
                pe.wait_ge(e_on, i * SLOTS + j + 3)
                if e_after is not None:
                    pe.wait_ge(after_on, i * SLOTS + j + 1)
                    for m in range(GROUP):
                        mm = nc.tensor.transpose(psum[:, T_BANKS[j % 2], m * P:(m + 1) * P],
                                                 e[:, j % 2, m * D:(m + 1) * D], keep["ident"][:])
                    mm.then_inc(e_turned, 1)
                pe.wait_ge(hot_on, i * (SLOTS * GROUP) + (j + 1) * GROUP)
                pe.wait_ge(agg_on, i * SLOTS + j + 1)
                for m in range(GROUP):
                    mm = nc.tensor.matmul(psum[:, A_BANKS[j % 2], 0:P],
                                          e[:, j % 2, m * D:(m + 1) * D], hot_w[:, j % 2, m, :],
                                          start=(m == 0), stop=(m == GROUP - 1))
                mm.then_inc(summed, 1)

            def run_round(i, is_last):
                for j, ahead in groups_ahead(i, is_last):
                    if j % (SLOTS // 2) == 0:
                        n = min(SLOTS // 2, SLOTS - 1 - j) if is_last else SLOTS // 2
                        windows = windows_of(i, j + 1, n, mybir.EngineType.PE)
                    if ahead is not None:
                        products(*ahead, windows[j % (SLOTS // 2)])
                    turn_and_sum(i, j)

            last = last_round(mybir.EngineType.PE)
            products(0, 0, windows_of(0, 0, 1, mybir.EngineType.PE)[0])
            with pe.Fori(0, last) as i:
                run_round(i, False)
            run_round(last, True)

        @block.scalar
        def _(act):
            nc.scalar.copy(ids[:], t["src_i"][:, 0:SLOTS * GROUP]
                           .rearrange("p (j m) -> p j m", m=GROUP)).then_inc(ids_on, 1)
            act.wait_ge(ids_on, 1)
            act.sem_inc(ids_on, SLOTS - 1)
            act.sem_inc(e_on, 2)
            act.sem_inc(after_on, 2)
            for q in range(MOVES):
                act.sem_inc(stored[q], 16)

            def relu(i, j):
                act.wait_ge(added, i * SLOTS + j + 1)
                act.wait_ge(summed, i * SLOTS + j + 1)
                nc.scalar.activation(e[:, j % 2, :], pre[:, j % 2, :], ACT.Relu).then_inc(e_on, 1)
                nc.scalar.copy(ids[:, j, :],
                               t["src_i"][:, bass.ds(i * (SLOTS * GROUP) + (SLOTS + j) * GROUP, GROUP)]
                               ).then_inc(ids_on, 1)

            def take(i, j):
                if e_after is not None:
                    act.wait_ge(e_turned, i * SLOTS + j + 1)
                    act.wait_ge(stored[j // 2], i * 16 + 16)
                    nc.scalar.activation(after[:, j // 2, at(j)], psum[:, T_BANKS[j % 2], 0:WIDE],
                                         ACT.Copy).then_inc(after_on, 1)

            nc.scalar.preload_act_table(ACT.Relu)
            last = last_round(mybir.EngineType.Activation)

            def run_round(i, is_last):
                for j, ahead in groups_ahead(i, is_last):
                    if ahead is not None:
                        relu(*ahead)
                    take(i, j)

            relu(0, 0)
            with act.Fori(0, last) as i:
                run_round(i, False)
            run_round(last, True)

        @block.vector
        def _(dve):
            dve.sem_inc(agg_on, 2)

            def turned_hot(i, j):
                dve.wait_ge(locals_in[j // 2], i * 16 + 16)
                nc.vector.tensor_scalar(hot_t[:, j % 4, :], locals_[:, j // 2, at(j)], keep["lane_f"][:, 0:1],
                                        None, ALU.is_equal).then_inc(hot_t_on, 1)

            def hots(i, j):
                for m in range(GROUP):
                    k = i * (SLOTS * GROUP) + (j * GROUP + m)
                    nc.vector.tensor_scalar(hot_w[:, j % 2, m, :], keep["col_f"][:],
                                            t["dst_loc"][:, bass.ds(k, 1)],
                                            t["weight"][:, bass.ds(k, 1)],
                                            ALU.is_equal, ALU.mult).then_inc(hot_on, 1)

            def add(i, j):
                dve.wait_ge(spread, i * SLOTS + j + 1)
                dve.wait_ge(rows_in[j], i * (16 * GROUP) + 16 * GROUP)
                dve.wait_ge(e_on, i * SLOTS + j + 1)
                nc.vector.tensor_tensor(pre[:, j % 2, :], psum[:, E_BANKS[j % 2], 0:WIDE], p_rows[:, j, :],
                                        ALU.add).then_inc(added, 1)

            def gather_up(i, j, window):
                dve.wait_ge(summed, i * SLOTS + j + 3)
                dve.wait_ge(agg_on, i * SLOTS + j + 2)
                a = t["agg_t"][:, bass.ds(window * P, P)]
                nc.vector.tensor_tensor(a, psum[:, A_BANKS[j % 2], 0:P], a, ALU.add).then_inc(agg_on, 1)

            turned_hot(0, 0)
            turned_hot(0, 1)

            def rows_added(i, j):
                hots(i, j)
                add(i, j)
                if j + 2 < SLOTS:
                    turned_hot(i, j + 2)
                else:
                    turned_hot(i + 1, j + 2 - SLOTS)

            def run_round(i, is_last):
                for j, ahead in groups_ahead(i, is_last):
                    if ahead is not None:
                        rows_added(*ahead)
                    if j % (SLOTS // 2) == 0:
                        windows = windows_of(i, j, SLOTS // 2, mybir.EngineType.DVE)
                    gather_up(i, j, windows[j % (SLOTS // 2)])

            last = last_round(mybir.EngineType.DVE)
            rows_added(0, 0)
            with dve.Fori(0, last) as i:
                run_round(i, False)
            run_round(last, True)


_INS = ["x", "src", "dst", "edge_weight", "L0_gnn_W_msg", "L0_gnn_b_msg", "L0_gnn_W_ih", "L0_gnn_W_hh",
        "L0_gnn_b_ih", "L0_gnn_b_hh", "L1_gnn_We0", "L1_gnn_be0", "L1_gnn_Wn0", "L1_gnn_bn0",
        "L1_gnn_We1", "L1_gnn_be1", "L1_gnn_Wn1", "L1_gnn_bn1", "L1_gnn_We2", "L1_gnn_be2",
        "L1_gnn_Wn2", "L1_gnn_bn2"]
_TRANSPOSED = ("L0_gnn_W_msg", "L0_gnn_W_ih", "L0_gnn_W_hh")


def kernel(**inputs):
    import numpy as np
    from concourse import bacc
    from concourse.bass_utils import run_bass_kernel_spmd

    nc = bacc.Bacc("TRN2", target_bir_lowering=False, num_devices=1)
    laid = []
    for name in _INS:
        a = np.asarray(inputs[name])
        laid.append((name, np.ascontiguousarray(a.T if name in _TRANSPOSED else a)))
        if name == "x":
            laid.append(("xT", np.ascontiguousarray(a.T)))
    arrays, args = {}, []
    for name, a in laid:
        arrays[f"in_{name}"] = a
        args.append(nc.dram_tensor(f"in_{name}", a.shape, mybir.dt.from_np(a.dtype),
                                   kind="ExternalInput").ap())
    out = nc.dram_tensor("out", (NODES, D), F32, kind="ExternalOutput").ap()
    build(nc, *args, out)
    results = run_bass_kernel_spmd(nc, [arrays], core_ids=[0])
    return results.results[0]["out"]
```
